# Optimizing a Trainium2 kernel written in Bass

```python
import numpy as np
import jax
import jax.numpy as jnp

def _softmax(x, axis=-1):
    return jax.nn.softmax(x, axis=axis)

def _gelu(x):
    return jax.nn.gelu(x, approximate=True)

def _silu(x):
    return jax.nn.silu(x)

def _sigmoid(x):
    return jax.nn.sigmoid(x)

def _layernorm(x, axis=-1, eps=1e-05):
    m = jnp.mean(x, axis=axis, keepdims=True)
    v = jnp.var(x, axis=axis, keepdims=True)
    return (x - m) / jnp.sqrt(v + eps)

def _scatter_add(tgt, idx, src, axis=0):
    return tgt.at[idx].add(src)

def _segment_sum(src, seg, n):
    return jax.ops.segment_sum(src, seg, n)
kernel_name = 'mk_adaln_d1_jaxref_r8_cb290e'

def setup_inputs(seed: int=0):
    np.random.seed(seed)
    _w = jnp.asarray

    def _L0_attn_setup():
        import jax, jax.numpy as jnp
        import numpy as np
        B, T, DM = (1, 1024, 128)
        DS, DC, EXP = (16, 4, 2)
        DI = DM * EXP
        key = jax.random.key(seed)
        ks = jax.random.split(key, 6)
        sc = lambda k, shape, s: jax.random.normal(k, shape, jnp.float32) * s
        return {'x': jax.random.normal(ks[0], (B, T, DM), jnp.float32), 'W_in': sc(ks[1], (DM, 2 * DI), 0.02), 'conv_w': sc(ks[2], (DI, 1, DC), 0.2), 'conv_b': jnp.zeros((DI,), jnp.float32), 'W_x': sc(ks[3], (DI, 2 * DS + 1), 0.02), 'A_log': jnp.log(jnp.arange(1, DS + 1, dtype=jnp.float32)), 'D': jnp.ones((DI,), jnp.float32), 'W_out': sc(ks[4], (DI, DM), 0.02)}
    _L0_attn_in = _L0_attn_setup()

    def _L0_ffn_setup():
        import jax, jax.numpy as jnp
        import numpy as np
        B, S, D = (4, 256, 128)
        E = 8
        TOPK = 2
        I = 938

        def _swiglu(x, gate_up, down):
            h = jnp.einsum('bsd,fd->bsf', x, gate_up)
            g, u = jnp.split(h, 2, axis=-1)
            return jnp.einsum('bsi,di->bsd', jax.nn.silu(g) * u, down)
        key = jax.random.key(seed)
        ks = jax.random.split(key, 6)
        scale = 1.0 / np.sqrt(D)
        return {'hidden_states': jax.random.normal(ks[0], (B, S, D), dtype=jnp.float32), 'gate_weight': jax.random.normal(ks[1], (E, D), dtype=jnp.float32) * scale, 'shared_gate_up': jax.random.normal(ks[2], (2 * I, D), dtype=jnp.float32) * scale, 'shared_down': jax.random.normal(ks[3], (D, I), dtype=jnp.float32) * (1.0 / np.sqrt(I)), 'experts_gate_up': jax.random.normal(ks[4], (E, 2 * I, D), dtype=jnp.float32) * scale, 'experts_down': jax.random.normal(ks[5], (E, D, I), dtype=jnp.float32) * (1.0 / np.sqrt(I))}
    _L0_ffn_in = _L0_ffn_setup()
    _L0_c = _w((lambda *s: np.random.randn(*s).astype(np.float32) * 0.05)(16, 128))
    _L0_wmod = _w((lambda *s: np.random.randn(*s).astype(np.float32) * 0.05)(128, 6 * 128) * 128 ** (-0.5))
    _d = {'L0_attn_x': _L0_attn_in['x'], 'L0_attn_W_in': _L0_attn_in['W_in'], 'L0_attn_conv_w': _L0_attn_in['conv_w'], 'L0_attn_conv_b': _L0_attn_in['conv_b'], 'L0_attn_W_x': _L0_attn_in['W_x'], 'L0_attn_A_log': _L0_attn_in['A_log'], 'L0_attn_D': _L0_attn_in['D'], 'L0_attn_W_out': _L0_attn_in['W_out'], 'L0_ffn_gate_weight': _L0_ffn_in['gate_weight'], 'L0_ffn_shared_gate_up': _L0_ffn_in['shared_gate_up'], 'L0_ffn_shared_down': _L0_ffn_in['shared_down'], 'L0_ffn_experts_gate_up': _L0_ffn_in['experts_gate_up'], 'L0_ffn_experts_down': _L0_ffn_in['experts_down'], 'L0_c': _L0_c, 'L0_wmod': _L0_wmod}
    _x0 = _d['L0_attn_x']
    _d['L0_attn_x'] = jax.random.normal(jax.random.fold_in(jax.random.key(seed), 1), (16, 256, 128), dtype=_x0.dtype)
    del _x0
    return _d

def reference(L0_attn_x, L0_attn_W_in, L0_attn_conv_w, L0_attn_conv_b, L0_attn_W_x, L0_attn_A_log, L0_attn_D, L0_attn_W_out, L0_ffn_gate_weight, L0_ffn_shared_gate_up, L0_ffn_shared_down, L0_ffn_experts_gate_up, L0_ffn_experts_down, L0_c, L0_wmod):

    def _L0_attn_ref(x, W_in, conv_w, conv_b, W_x, A_log, D, W_out):
        import jax, jax.numpy as jnp
        import numpy as np
        B, T, DM = (1, 1024, 128)
        DS, DC, EXP = (16, 4, 2)
        DI = DM * EXP
        Bq, Tq, _ = x.shape
        xz = x @ W_in
        xc, z = jnp.split(xz, 2, axis=-1)
        xcT = jnp.transpose(xc, (0, 2, 1))
        conv = jax.lax.conv_general_dilated(xcT, conv_w, window_strides=(1,), padding=[(DC - 1, 0)], feature_group_count=DI)
        conv = conv + conv_b[None, :, None]
        xs = jax.nn.silu(jnp.transpose(conv, (0, 2, 1)))
        x_dbl = xs @ W_x
        delta = jax.nn.softplus(x_dbl[..., :1])
        Bp = x_dbl[..., 1:1 + DS]
        Cp = x_dbl[..., 1 + DS:]
        A = -jnp.exp(A_log)
        A_bar = jnp.exp(delta * A)
        B_bar = delta * Bp

        def step(h, inp):
            a_t, b_t, x_t, c_t = inp
            h = a_t[:, None, :] * h + b_t[:, None, :] * x_t[:, :, None]
            y_t = jnp.einsum('bdn,bn->bd', h, c_t)
            return (h, y_t)
        h0 = jnp.zeros((Bq, DI, DS), xs.dtype)
        seq = (jnp.swapaxes(A_bar, 0, 1), jnp.swapaxes(B_bar, 0, 1), jnp.swapaxes(xs, 0, 1), jnp.swapaxes(Cp, 0, 1))
        _, ys = jax.lax.scan(step, h0, seq)
        y = jnp.swapaxes(ys, 0, 1) + D * xs
        y = y * jax.nn.silu(z)
        return y @ W_out

    def _L0_ffn_ref(hidden_states, gate_weight, shared_gate_up, shared_down, experts_gate_up, experts_down):
        import jax, jax.numpy as jnp
        import numpy as np
        B, S, D = (4, 256, 128)
        E = 8
        TOPK = 2
        I = 938

        def _swiglu(x, gate_up, down):
            h = jnp.einsum('bsd,fd->bsf', x, gate_up)
            g, u = jnp.split(h, 2, axis=-1)
            return jnp.einsum('bsi,di->bsd', jax.nn.silu(g) * u, down)
        x = hidden_states
        out = _swiglu(x, shared_gate_up, shared_down)
        logits = jnp.einsum('bsd,ed->bse', x, gate_weight)
        probs = jax.nn.softmax(logits.astype(jnp.float32), axis=-1)
        top_p, sel = jax.lax.top_k(probs, TOPK)
        top_p = top_p / (jnp.sum(top_p, axis=-1, keepdims=True) + 1e-08)
        cw = jnp.sum(top_p[..., None] * jax.nn.one_hot(sel, E, dtype=top_p.dtype), axis=2)
        for e in range(E):
            y = _swiglu(x, experts_gate_up[e], experts_down[e])
            out = out + cw[..., e:e + 1] * y
        return out
    x = L0_attn_x
    mod = (_silu(L0_c) @ L0_wmod).reshape(L0_c.shape[0], 6, 1, -1)
    sa, ca, ga, sb, cb, gb = (mod[:, 0], mod[:, 1], mod[:, 2], mod[:, 3], mod[:, 4], mod[:, 5])
    ga = (2 * (ga >= 0) - 1) * jnp.maximum(jnp.abs(ga), 0.25)
    gb = (2 * (gb >= 0) - 1) * jnp.maximum(jnp.abs(gb), 0.25)
    h = _layernorm(x, axis=-1) * (1 + ca) + sa
    x = x + ga * _L0_attn_ref(h, L0_attn_W_in, L0_attn_conv_w, L0_attn_conv_b, L0_attn_W_x, L0_attn_A_log, L0_attn_D, L0_attn_W_out)
    h = _layernorm(x, axis=-1) * (1 + cb) + sb
    x = x + gb * _L0_ffn_ref(h, L0_ffn_gate_weight, L0_ffn_shared_gate_up, L0_ffn_shared_down, L0_ffn_experts_gate_up, L0_ffn_experts_down)
    return x

_drawn_inputs = setup_inputs


def setup_inputs(seed=0):
    import zlib

    import numpy as np

    out = dict(_drawn_inputs(seed))
    spreads = {'L0_attn_conv_b': (0.0, 0.1), 'L0_attn_D': (1.0, 0.2)}
    factors = {}
    for name, (base, spread) in spreads.items():
        noise = np.random.default_rng([zlib.crc32(name.encode()), seed]).standard_normal(out[name].shape)
        drawn = base * np.exp(spread * noise) if base else spread * noise
        out[name] = jnp.asarray(drawn.astype(out[name].dtype))
    for name, factor in factors.items():
        out[name] = (out[name] * factor).astype(out[name].dtype)
    return out
```

```python
from contextlib import ExitStack

import numpy as np
import concourse.bass as bass
from concourse import mybir

F32 = mybir.dt.float32
F32R = mybir.dt.float32r
I32 = mybir.dt.int32
U32 = mybir.dt.uint32
ALU = mybir.AluOpType
ACT = mybir.ActivationFunctionType
AX = mybir.AxisListType

P = 128
SEQS = 16
SEQ = 256
TOKENS = SEQS * SEQ
CH = TOKENS // P
G = 4
GC = CH // G
GS = SEQS // G
GT = GC * P
DI = 2 * P
NS = 16
XD = 2 * NS + 1
TAPS = 4
BLK = 16
NB = P // BLK
LEVELS = (128, 64, 32, 16)
E = 8
FF = 938
FC = 8
FL = FF - (FC - 1) * P
WC = 3 * FC * P
TILE = 512
TR = TILE // P
REGION = TOKENS + TILE
ROW = P + 2
NOWHERE = 4 * TOKENS
SHARED = TOKENS // TILE
EPS = 1e-5

CONST = ("ident", "below7", "above7", "lvl6", "lvl5", "lvl4", "later16", "upto16", "before", "ones")


def constants():
    u = np.arange(P)[:, None]
    t = np.arange(P)[None, :]
    same = u // BLK == t // BLK

    def span(half):
        mid = t // (2 * half) * (2 * half) + half
        return np.where(t >= mid, (u >= mid) & (u <= t), (u > t) & (u < mid))

    mats = [u == t, u > t, u <= t, span(64), span(32), span(16), same & (u > t), same & (u >= t), u < t, u >= 0]
    tau = np.arange(BLK)[None, :]
    upto = u % BLK <= tau
    equal = u % BLK == tau
    block = u // BLK == np.arange(NB)[None, :]
    roles = []
    for want in (1, 0):
        cols = [np.full((P, 1), par == want) for par in (0, 1)]
        for half in LEVELS[1:]:
            for b in range(P // (2 * half)):
                cols.append((u // (2 * half) == b) & ((u // half) % 2 == want))
        roles.append(np.concatenate(cols, 1))
    expert = np.arange(E)[None, :] + 0 * u
    seg = np.tile(np.arange(GC) > 0, E)[None, :] & (u >= 0)
    many = np.arange(E)[None, :] * TILE + 0 * u
    small = np.concatenate([upto, equal, block, *roles, seg, E - expert, expert * REGION, many], 1)
    big = np.concatenate([np.broadcast_to(m, (P, P)) for m in mats], 1)
    token = (np.arange(CH)[None, :, None] * P + np.arange(P)[:, None, None]) * 2 + np.arange(2)[None, None, :]
    return (np.ascontiguousarray(big, np.float32), np.ascontiguousarray(small, np.float32),
            np.ascontiguousarray(token, np.int32))


SMALL = {}
_at = 0
for _name, _n in (("upto", BLK), ("equal", BLK), ("block", NB), ("upper", 9), ("lower", 9), ("seg", E * GC),
                  ("rev", E), ("region", E), ("many", E)):
    SMALL[_name] = (_at, _n)
    _at += _n
NSMALL = _at
NCONST = 9


def adaln_block(nc, a):
    ctx = ExitStack()
    with ctx:
        def sb(name, shape, dt=F32):
            return ctx.enter_context(nc.sbuf_tensor(name, shape, dt))

        def arena(name, shape):
            at = -(-nc.sbuf_base // 32) * 32
            return sb(name, shape), at

        def over(name, shape, at, dt=F32):
            return nc.alloc_sbuf_tensor_at(name, shape, dt, offset=at)

        def sem(name):
            return ctx.enter_context(nc.semaphore(name))

        def merge(ap, dims):
            return ap.rearrange(dims)

        mods_dram = nc.dram_tensor("mods_dram", (SEQS, 4, P), F32, kind="Internal").ap()
        sorted_dram = nc.dram_tensor("sorted_dram", (E * REGION, ROW), F32, kind="Internal").ap()
        result_dram = nc.dram_tensor("result_dram", (2 * TOKENS, P), F32, kind="Internal").ap()

        mats = sb("mats", [P, len(CONST), P])
        M = {n: mats[:, i, :] for i, n in enumerate(CONST)}
        small = sb("small", [P, NSMALL])
        S = {n: small[:, o:o + k] for n, (o, k) in SMALL.items()}
        token2 = sb("token2", [P, CH, 2], I32)
        w_in = sb("w_in", [P, 4, P])
        w_out = sb("w_out", [P, 2, P])
        w_x = sb("w_x", [P, 2, XD])
        cols = sb("cols", [P, 2, TAPS + 2])
        a_log = sb("a_log", [P, NS])
        a_neg = sb("a_neg", [P, NS])
        gate_w = sb("gate_w", [P, E])
        gate_hi = sb("gate_hi", [P, E], F32R)
        gate_lo = sb("gate_lo", [P, E], F32R)
        c_t = sb("c_t", [P, SEQS])
        sc_t = sb("sc_t", [P, SEQS])
        shift_a = sb("shift_a", [P, SEQS])
        scale_a = sb("scale_a", [P, SEQS])
        mod_rows = sb("mod_rows", [SEQS, 4, P])
        mod_tmp = sb("mod_tmp", [SEQS, 2, P])
        table = sb("table", [P, GS, 4, P])
        gb_all = table[:, :, :, :].rearrange("p q m d -> p (q m) d")

        X = sb("X", [P, CH, P])
        nx = sb("nx", [P, GC, P])
        diag = nx
        hT, hT_at = arena("hT", [P, GS * 3 * P])
        mT = hT[:, :].rearrange("p (q k t) -> p q k t", q=GS, k=3)
        stats = sb("stats", [P, GC, 6])
        mv = sb("mv", [P, GC, 2])
        rstd = sb("rstd", [P, GC])
        minus_half = sb("minus_half", [P, GC])
        xcp = sb("xcp", [P, 2, GS, SEQ + TAPS - 1])
        inner, inner_at = arena("inner", [P, 6, GT])
        acc, xsT, sz = inner[:, 0:2], inner[:, 2:4], inner[:, 4:6]
        yT = acc
        xs_tok = sb("xs_tok", [P, GC, DI])
        dbc = sb("dbc", [P, GC, XD])
        sp0 = sb("sp0", [P, GC])
        sp1 = sb("sp1", [P, GC])
        sp2 = sb("sp2", [P, GC])
        delta = sb("delta", [P, GC])
        dl_upto = sb("dl_upto", [P, GC, BLK])
        dB = sb("dB", [P, GC, NS])
        pq = sb("pq", [P, 2, GC, P])
        c_exp = pq[:, :, :, :].rearrange("p k j (a n) -> p (k j a) n", n=NS).rearrange(
            "p (j a) n -> p j a n", j=GC)
        pqT = sb("pqT", [P, 2, GC, P])
        lev = sb("lev", [P, GC, 4, NS])
        lev_c, lev_b = (pqT[:, k, 0:GC // 2, :].rearrange("p j t -> p (j t)").rearrange(
            "p (j l n) -> p j l n", j=GC, l=4) for k in range(2))
        pair = sb("pair", [P, GC, BLK, NS])
        wd = sb("wd", [P, GC, BLK])
        h2 = sb("h2", [P, 2, GC, ROW])
        lg = sb("lg", [P, GC, E])
        r1 = sb("r1", [P, GC, E])
        r2 = sb("r2", [P, GC, E])
        oh = sb("oh", [P, 2, GC, E])
        ex = sb("ex", [P, GC, E])
        top = sb("top", [P, 8, GC])
        picked = sb("picked", [P, E, GC])
        ranks = sb("ranks", [P, E, GC])
        base = sb("base", [P, E])
        base2 = sb("base2", [P, E])
        slot = sb("slot", [P, 2, GC], I32)
        plan_f = sb("plan_f", [P, 4, E])
        plan = sb("plan", [P, 3, E], I32)
        cmp = sb("cmp", [P, E, E])
        pad = sb("pad", [P, TR, ROW])
        xh = sb("xh", [P, GT], F32R)
        xl = sb("xl", [P, GT], F32R)
        stage = sb("stage", [P, WC])
        w_hi = [sb("w_hi0", [P, WC], F32R), over("w_hi1", [P, WC], inner_at, F32R)]
        w_lo = [sb("w_lo0", [P, WC], F32R), over("w_lo1", [P, WC], inner_at + 4 * WC, F32R)]
        assert 2 * WC <= 6 * GT
        sg = sb("sg", [P, 3, TILE])
        prod = sb("prod", [P, 3, TILE])
        ah = sb("ah", [P, 3, TILE], F32R)
        al = sb("al", [P, 3, TILE], F32R)
        y_sb = sb("y_sb", [P, TILE])
        xin = over("xin", [P, TR, ROW], hT_at)
        y_rows = over("y_rows", [P, TR, P], hT_at + 4 * TR * (ROW + 2))
        aux_w = sb("aux_w", [P, 2, TR])
        aux_d = sb("aux_d", [P, 2, TR], I32)
        fin = [pair[:, :, :, :].rearrange("p j a n -> p (j a n)").rearrange("p (j k d) -> p j k d", j=GC, k=2),
               pqT[:, :, :, :].rearrange("p k j t -> p (k j t)").rearrange("p (j k d) -> p j k d", j=GC, k=2)]

        PS = ctx.enter_context(nc.psum_tensor("PS", [P, 8, 512], F32))

        def banks(b, n):
            return PS[:, b:b + n, :].rearrange("p b c -> p (b c)")

        names = """passed consts_in x_in weights_small_in act_setup setup_chain silu_c mods_pe mods_rows mods_out
            table_in table_used nx_ready nxT_done hT_ready xz_done xcp_ready tap_ready conv_done sz_ready xs_ready
            dbc_done xst_done xst_ready nabs_ready act_chain soft_ready delta_ready cexp_ready spans_done
            cg_done levels_in pairs_in levels_exp pairs_exp pq_ready pqT_done pqT_ready cg_used m_done mT_ready
            mo_ready y_done y_ready o_done h2_ready h2T_done xh_ready xl_ready logits_done soft_in soft_out
            var_ready eps_added rstd_ready picked_ready counts_done rows_ready sorted_out dve_chain copy_ready
            raw_in split_hi split_done gate_done up_done silu_done prod_done ah_ready al_ready
            y_bank_done y_sb_ready yt_done y_out tile_in xt_done rh_ready rl_ready aux_read
            results_out plan_ready pads_out pad_ready final_in0 final_in1 final_ready out_done gb_in""".split()
        s = {n: sem(n) for n in names}
        block = ctx.enter_context(nc.Block())

        def apart(engine):
            engine.sem_inc(s["passed"], 1)

        NRAW = 4

        @block.sync
        def _(sp):
            def load_raw(x):
                gu = a["w_gu"][bass.ds(x, 1)].rearrange("o d f -> (o d) f")
                dn = a["w_dn"][bass.ds(x, 1)].rearrange("o f d -> (o f) d")
                last = FC - 1
                sp.dma_start(stage[:, 0:FF], gu[:, 0:FF]).then_inc(s["raw_in"], 16)
                sp.dma_start(stage[:, FC * P:FC * P + FF], gu[:, FF:2 * FF]).then_inc(s["raw_in"], 16)
                sp.dma_start(stage[:, 2 * FC * P:2 * FC * P + last * P].rearrange("p (c d) -> p c d", d=P),
                             dn[0:last * P, :].rearrange("(c p) d -> p c d", p=P)).then_inc(s["raw_in"], 16)
                sp.dma_start(stage[0:FL, 2 * FC * P + last * P:WC], dn[last * P:FF, :]).then_inc(s["raw_in"], 16)

            sp.dma_start(c_t[:], a["c_t"]).then_inc(s["weights_small_in"], 16)
            sp.dma_start(stage[:, 0:6 * P], a["L0_wmod"]).then_inc(s["weights_small_in"], 16)
            x_view = a["x"].rearrange("(c p) d -> p c d", p=P)
            for g in range(G):
                sp.dma_start(X[:, g * GC:(g + 1) * GC, :], x_view[:, g * GC:(g + 1) * GC, :]).then_inc(s["x_in"], 16)
                if g == 0:
                    sp.dma_start(mats[:].rearrange("p m t -> p (m t)"), a["big"]).then_inc(s["consts_in"], 16)
                    sp.dma_start(small[:], a["small"]).then_inc(s["consts_in"], 16)
                    sp.dma_start(token2[:], a["token"]).then_inc(s["consts_in"], 16)
                    sp.dma_start(w_in[:].rearrange("p m t -> p (m t)"), a["L0_attn_W_in"]).then_inc(s["consts_in"], 16)
                    sp.dma_start(w_out[:], a["L0_attn_W_out"].rearrange("(h p) d -> p h d", p=P)).then_inc(
                        s["consts_in"], 16)
                    sp.dma_start(w_x[:], a["L0_attn_W_x"].rearrange("(h p) d -> p h d", p=P)).then_inc(
                        s["consts_in"], 16)
                    sp.dma_start(cols[:], a["cols"].rearrange("(h p) d -> p h d", p=P)).then_inc(s["consts_in"], 16)
                    sp.dma_start(a_log[:], a["a_log"].to_broadcast([P, NS])).then_inc(s["consts_in"], 16)
                    sp.dma_start(gate_w[:], a["gate_t"]).then_inc(s["consts_in"], 16)
            sp.wait_ge(s["mods_rows"], 1)
            sp.dma_start(mods_dram, mod_rows[:]).then_inc(s["mods_out"], 16)
            sp.wait_ge(s["mods_out"], 16)
            sp.wait_ge(s["act_setup"], 1)
            load_raw(0)
            with sp.Fori(0, G) as g:
                sp.wait_ge(s["table_used"], g + 1)
                sp.dma_start(table[:].rearrange("p q m d -> p (q m d)"),
                             mods_dram[bass.ds(g * GS, GS)].rearrange("q m d -> (q m d)").unsqueeze(0)
                             .to_broadcast([P, GS * 4 * P])).then_inc(s["table_in"], 16)
            sp.wait_ge(s["split_done"], 1)
            load_raw(1)
            sp.wait_ge(s["plan_ready"], 1)
            sp.wait_ge(s["pad_ready"], 2)
            sp.wait_ge(s["sorted_out"], 16 * 2 * CH)
            for e in range(E):
                row = sp.value_load(plan[0:1, 2, e:e + 1], min_val=e * REGION, max_val=e * REGION + TOKENS)
                sp.dma_start(sorted_dram[bass.ds(row, TILE)].rearrange("(p r) d -> p (r d)", p=P),
                             pad[:].rearrange("p r d -> p (r d)")).then_inc(s["pads_out"], 16)
            sp.wait_ge(s["pads_out"], 16 * E)

            def load_tile(row, i):
                sp.wait_ge(s["aux_read"], i + 1)
                sp.dma_start(xin[:].rearrange("p r d -> p (r d)"),
                             sorted_dram[bass.ds(row, TILE)].rearrange("(p r) d -> p (r d)", p=P)).then_inc(
                    s["tile_in"], 16)

            def expert(e, more):
                tiles = sp.value_load(plan[0:1, 0, bass.ds(e, 1)], min_val=1, max_val=TOKENS // TILE)
                first = sp.value_load(plan[0:1, 1, bass.ds(e, 1)], min_val=0, max_val=3 * TOKENS // TILE)
                if more:
                    sp.wait_ge(s["split_done"], e + 2)
                    load_raw(e + 2)
                with sp.Fori(0, tiles) as t:
                    i = first + t
                    load_tile(e * REGION + t * TILE, i)

            with sp.Fori(0, E - 1) as e:
                expert(e, True)
            expert(E - 1, False)
            last_tiles = sp.value_load(plan[0:1, 0, E - 1:E], min_val=1, max_val=TOKENS // TILE)
            last_first = sp.value_load(plan[0:1, 1, E - 1:E], min_val=0, max_val=3 * TOKENS // TILE)
            count = last_first + last_tiles
            load_tile(0, count)
            sp.wait_ge(s["table_used"], G + 1)
            sp.dma_start(gb_all, mods_dram[:, 3, :].unsqueeze(0).to_broadcast([P, SEQS, P])).then_inc(s["gb_in"], 16)
            sp.wait_ge(s["results_out"], 64 * (count + 1))
            res = result_dram.rearrange("(c p k) d -> p c k d", p=P, k=2)
            out_view = a["out"].rearrange("(c p) d -> p c d", p=P)
            for g in range(G):
                if g >= 2:
                    sp.wait_ge(s["final_ready"], g - 1)
                sp.dma_start(fin[g % 2], res[:, g * GC:(g + 1) * GC]).then_inc(s[f"final_in{g % 2}"], 16)
            for g in range(G):
                sp.wait_ge(s["final_ready"], g + 1)
                sp.dma_start(out_view[:, g * GC:(g + 1) * GC, :], X[:, g * GC:(g + 1) * GC, :]).then_inc(
                    s["out_done"], 16)
            sp.wait_ge(s["tile_in"], 16 * (count + 1))
            apart(sp)
            sp.wait_ge(s["out_done"], 16 * G)

        @block.gpsimd
        def _(pool):
            def split(x, buf):
                pool.wait_ge(s["raw_in"], 16 * NRAW * (x + 1))
                apart(pool)
                nc.gpsimd.tensor_copy(w_hi[buf][:], stage[:]).then_inc(s["split_hi"], 1)
                pool.wait_ge(s["split_hi"], x + 1)
                nc.gpsimd.tensor_tensor(w_lo[buf][:], stage[:], w_hi[buf][:].bitcast(F32), ALU.subtract).then_inc(
                    s["split_done"], 1)

            nc.gpsimd.memset(pad[:], 0.0).then_inc(s["pad_ready"], 1)
            nc.gpsimd.memset(minus_half[:], -0.5)
            nc.gpsimd.memset(xcp[:, :, :, 0:TAPS - 1], 0.0).then_inc(s["setup_chain"], 1)
            pool.wait_ge(s["pad_ready"], 1)
            nc.gpsimd.memset(pad[:, :, P + 1:P + 2].bitcast(I32), NOWHERE).then_inc(s["pad_ready"], 1)
            pool.wait_ge(s["mods_pe"], 1)
            nc.gpsimd.memset(stage[:], 0.0).then_inc(s["act_setup"], 1)
            split(0, 0)
            with pool.Fori(0, G) as g:
                for k in range(2):
                    pool.wait_ge(s["var_ready"], 2 * g + k + 1)
                    apart(pool)
                    nc.gpsimd.tensor_scalar_add(rstd[:], mv[:, :, 1], EPS).then_inc(s["eps_added"], 1)
                    pool.wait_ge(s["eps_added"], 2 * g + k + 1)
                    nc.gpsimd.tensor_tensor(rstd[:], rstd[:], minus_half[:], ALU.pow).then_inc(s["rstd_ready"], 1)
                pool.wait_ge(s["rows_ready"], g + 1)
                apart(pool)
                for k in range(2):
                    for j in range(GC):
                        pool.indirect_dma_start(
                            out=sorted_dram, out_offset=bass.IndirectOffsetOnAxis(
                                ap=slot[:, k, j:j + 1].bitcast(U32), axis=0),
                            in_=h2[:, k, j, :], in_offset=None, bounds_check=E * REGION - 1,
                            oob_is_err=False).then_inc(s["sorted_out"], 16)
            split(1, 1)
            pool.wait_ge(s["plan_ready"], 1)

            def results(i):
                pool.wait_ge(s["y_out"], SHARED + 1 + i)
                apart(pool)
                for r in range(TR):
                    pool.indirect_dma_start(
                        out=result_dram, out_offset=bass.IndirectOffsetOnAxis(
                            ap=aux_d[:, 0, r:r + 1].bitcast(U32), axis=0),
                        in_=y_rows[:, r, :], in_offset=None, bounds_check=2 * TOKENS - 1,
                        oob_is_err=False).then_inc(s["results_out"], 16)

            def expert(e, buf, more):
                tiles = pool.value_load(plan[0:1, 0, bass.ds(e, 1)], min_val=1, max_val=TOKENS // TILE)
                first = pool.value_load(plan[0:1, 1, bass.ds(e, 1)], min_val=0, max_val=3 * TOKENS // TILE)
                if more:
                    pool.wait_ge(s["y_bank_done"], SHARED + first)
                    split(e + 2, 1 - buf)
                with pool.Fori(0, tiles) as t:
                    results(first + t)
                return first, tiles

            with pool.Fori(0, E // 2 - 1) as k:
                expert(2 * k, 1, True)
                expert(2 * k + 1, 0, True)
            expert(E - 2, 1, True)
            first, tiles = expert(E - 1, 0, False)
            results(first + tiles)

        @block.tensor
        def _(pe):
            def mm(out, lhsT, rhs, start=True, stop=True, **k):
                return nc.tensor.matmul(out, lhsT, rhs, start=start, stop=stop, **k)

            def three(out, lo, hi, w0, wn, rl, rh, start, stop):
                mm(out, lo[:, w0:w0 + wn], rh, start, False)
                mm(out, hi[:, w0:w0 + wn], rl, False, False)
                return mm(out, hi[:, w0:w0 + wn], rh, False, stop)

            def gate_up(buf, c, rh, rl):
                three(PS[:, c % 3, :], w_lo[buf], w_hi[buf], c * P, P, rl, rh, True, True).then_inc(s["gate_done"], 1)
                three(PS[:, 3 + c % 3, :], w_lo[buf], w_hi[buf], (FC + c) * P, P, rl, rh, True, True).then_inc(
                    s["up_done"], 1)

            def down(buf, c, I):
                pe.wait_ge(s["ah_ready"], I * FC + c + 1)
                pe.wait_ge(s["al_ready"], I * FC + c + 1)
                last = three(PS[:, 6, :], w_lo[buf], w_hi[buf], (2 * FC + c) * P, P, al[:, c % 3, :], ah[:, c % 3, :],
                             c == 0, c == FC - 1)
                if c == FC - 1:
                    last.then_inc(s["y_bank_done"], 1)

            def turn_result():
                for r in range(TR):
                    last = nc.tensor.transpose(PS[:, 7, r * P:(r + 1) * P], y_sb[:, r * P:(r + 1) * P], M["ident"])
                last.then_inc(s["yt_done"], 1)

            pe.wait_ge(s["weights_small_in"], 32)
            pe.wait_ge(s["silu_c"], 1)
            mm(PS[:, 0, 0:SEQS], stage[:, 0:P], sc_t[:])
            mm(PS[:, 0, SEQS:2 * SEQS], stage[:, P:2 * P], sc_t[:])
            mm(PS[0:SEQS, 1, :], sc_t[:], stage[:, 2 * P:6 * P]).then_inc(s["mods_pe"], 1)

            pe.wait_ge(s["consts_in"], 16 * NCONST)
            with pe.Fori(0, G) as g:
                pe.wait_ge(s["nx_ready"], g + 1)
                for j in range(GC):
                    last = nc.tensor.transpose(PS[:, j // 4, (j % 4) * P:(j % 4 + 1) * P], nx[:, j, :], M["ident"])
                last.then_inc(s["nxT_done"], 1)
                pe.wait_ge(s["hT_ready"], 2 * g + 2)
                for m in range(4):
                    for k in range(2):
                        mm(PS[:, (2 + 2 * m + k) % 8, :], w_in[:, m, :], hT[:, k * 512:(k + 1) * 512]).then_inc(
                            s["xz_done"], 1)
                pe.wait_ge(s["sz_ready"], 4 * g + 4)
                pe.wait_ge(s["xs_ready"], 2 * g + 2)
                for j in range(GC):
                    for h in range(2):
                        last = mm(PS[:, 6, j * XD:(j + 1) * XD], xsT[:, h, j * P:(j + 1) * P], w_x[:, h, :],
                                  h == 0, h == 1)
                last.then_inc(s["dbc_done"], 1)
                for j in range(GC):
                    for h in range(2):
                        c0 = (j % 2) * DI + h * P
                        last = nc.tensor.transpose(PS[:, 2 + j // 2, c0:c0 + P], xsT[:, h, j * P:(j + 1) * P],
                                                   M["ident"])
                    if j % 2:
                        last.then_inc(s["xst_done"], 1)
                pe.wait_ge(s["cexp_ready"], g + 1)
                for b in range(4):
                    if b == 2:
                        pe.wait_ge(s["xst_ready"], 4 * g + 2)
                    mm(PS[:, b, :], M["upto16"], c_exp[:, 2 * b:2 * b + 2].rearrange("p j a n -> p (j a n)")).then_inc(
                        s["cg_done"], 1)
                pe.wait_ge(s["delta_ready"], g + 1)
                sp_out = PS[:, 7, 0:4 * GC].rearrange("p (l j) -> p l j", l=4)
                mm(sp_out[:, 0, 0::2], M["below7"], delta[:, 0::2])
                mm(sp_out[:, 0, 1::2], M["above7"], delta[:, 1::2])
                for k, n in enumerate(("lvl6", "lvl5", "lvl4")):
                    mm(sp_out[:, k + 1, :], M[n], delta[:])
                mm(PS[:, 7, 64:64 + P], M["later16"], dl_upto[:].rearrange("p j a -> p (j a)")).then_inc(
                    s["spans_done"], 1)
                pe.wait_ge(s["pq_ready"], g + 1)
                pe.wait_ge(s["xst_ready"], 4 * g + 4)
                for k in range(2):
                    for j in range(GC):
                        last = nc.tensor.transpose(PS[:, 4 + 2 * k + j // 4, (j % 4) * P:(j % 4 + 1) * P],
                                                   pq[:, k, j, :], M["ident"])
                        if j % 4 == 3:
                            last.then_inc(s["pqT_done"], 1)
                pe.wait_ge(s["pqT_ready"], 4 * g + 4)
                pe.wait_ge(s["cg_used"], 4 * g + 4)
                for j in range(GC):
                    mm(PS[:, j // 4, (j % 4) * P:(j % 4 + 1) * P], pqT[:, 1, j, :], pqT[:, 0, j, :])
                for q in range(GS):
                    last = mm(PS[:, 2, q * P:(q + 1) * P], pqT[0:NS, 1, 2 * q, :], pqT[0:NS, 0, 2 * q + 1, :])
                last.then_inc(s["m_done"], 1)
                pe.wait_ge(s["mT_ready"], g + 1)
                pe.wait_ge(s["mo_ready"], g + 1)
                for h in range(2):
                    for q in range(GS):
                        o = PS[:, 4 + 2 * h + q // 2, (q % 2) * SEQ:(q % 2 + 1) * SEQ]
                        mm(o, xs_tok[:, 2 * q, h * P:(h + 1) * P], mT[:, q, 0:2, :].rearrange("p k t -> p (k t)"),
                           True, True)
                        last = mm(o[:, P:SEQ], xs_tok[:, 2 * q + 1, h * P:(h + 1) * P], mT[:, q, 2, :], False, True,
                                  skip_group_check=True)
                    last.then_inc(s["y_done"], 1)
                pe.wait_ge(s["y_ready"], 2 * g + 2)
                for j in range(GC):
                    for h in range(2):
                        last = mm(PS[:, j // 4, (j % 4) * P:(j % 4 + 1) * P], yT[:, h, j * P:(j + 1) * P],
                                  w_out[:, h, :], h == 0, h == 1)
                last.then_inc(s["o_done"], 1)
                pe.wait_ge(s["h2_ready"], g + 1)
                for j in range(GC):
                    last = nc.tensor.transpose(PS[:, 2 + j // 4, (j % 4) * P:(j % 4 + 1) * P], h2[:, 0, j, 0:P],
                                               M["ident"])
                last.then_inc(s["h2T_done"], 1)
                pe.wait_ge(s["xh_ready"], g + 1)
                pe.wait_ge(s["xl_ready"], g + 1)
                for j in range(GC):
                    o = PS[:, 4, j * E:(j + 1) * E]
                    mm(o, xl[:, j * P:(j + 1) * P], gate_hi[:], True, False)
                    mm(o, xh[:, j * P:(j + 1) * P], gate_lo[:], False, False)
                    last = mm(o, xh[:, j * P:(j + 1) * P], gate_hi[:], False, True)
                last.then_inc(s["logits_done"], 1)
                pe.wait_ge(s["picked_ready"], g + 1)
                mm(PS[:, 5, 0:E], M["before"], ranks[:, :, GC - 1])
                mm(PS[:, 5, E:2 * E], M["ones"], ranks[:, :, GC - 1]).then_inc(s["counts_done"], 1)
                pe.wait_ge(s["rows_ready"], g + 1)
                pe.wait_ge(s["split_done"], 1)
                for k in range(2):
                    I = 2 * g + k
                    rh, rl = xh[:, k * TILE:(k + 1) * TILE], xl[:, k * TILE:(k + 1) * TILE]
                    for c in range(FC):
                        gate_up(0, c, rh, rl)
                        if c >= 2:
                            down(0, c - 2, I)
                    down(0, FC - 2, I)
                    down(0, FC - 1, I)
                    pe.wait_ge(s["y_sb_ready"], I + 1)
                    turn_result()

            def turn_tile(i):
                pe.wait_ge(s["tile_in"], 16 * (i + 1))
                for r in range(TR):
                    last = nc.tensor.transpose(PS[:, 7, r * P:(r + 1) * P], xin[:, r, 0:P], M["ident"])
                last.then_inc(s["xt_done"], 1)

            pe.wait_ge(s["plan_ready"], 1)
            pe.wait_ge(s["y_out"], SHARED)
            turn_tile(0)

            def tile_body(buf, i):
                I = SHARED + i
                pe.wait_ge(s["rh_ready"], i + 1)
                pe.wait_ge(s["rl_ready"], i + 1)
                rh, rl = xh[:, 0:TILE], xl[:, 0:TILE]
                for c in range(FC):
                    gate_up(buf, c, rh, rl)
                    if c == 0:
                        pe.wait_ge(s["y_sb_ready"], I)
                        turn_result()
                    if c >= 2:
                        down(buf, c - 2, I)
                pe.wait_ge(s["y_out"], I + 1)
                turn_tile(i + 1)
                down(buf, FC - 2, I)
                down(buf, FC - 1, I)

            def expert(e, buf):
                tiles = pe.value_load(plan[0:1, 0, bass.ds(e, 1)], min_val=1, max_val=TOKENS // TILE)
                first = pe.value_load(plan[0:1, 1, bass.ds(e, 1)], min_val=0, max_val=3 * TOKENS // TILE)
                pe.wait_ge(s["split_done"], e + 2)
                apart(pe)
                with pe.Fori(0, tiles) as t:
                    tile_body(buf, first + t)
                return first + tiles

            with pe.Fori(0, E // 2 - 1) as k:
                expert(2 * k, 1)
                expert(2 * k + 1, 0)
            expert(E - 2, 1)
            count = expert(E - 1, 0)
            pe.wait_ge(s["y_sb_ready"], SHARED + count)
            pe.wait_ge(s["rl_ready"], count + 1)
            turn_result()

        @block.scalar
        def _(act):
            def silu_hi(I):
                for c in range(FC):
                    act.wait_ge(s["gate_done"], I * FC + c + 1)
                    nc.scalar.activation(sg[:, c % 3, :], PS[:, c % 3, :], ACT.Silu).then_inc(s["silu_done"], 1)
                    act.wait_ge(s["prod_done"], I * FC + c + 1)
                    nc.scalar.copy(ah[:, c % 3, :], prod[:, c % 3, :]).then_inc(s["ah_ready"], 1)

            def keep_result(I):
                act.wait_ge(s["y_bank_done"], I + 1)
                nc.scalar.copy(y_sb[:], PS[:, 6, :]).then_inc(s["y_sb_ready"], 1)

            act.wait_ge(s["weights_small_in"], 32)
            nc.scalar.activation(sc_t[:], c_t[:], ACT.Silu).then_inc(s["silu_c"], 1)
            act.wait_ge(s["consts_in"], 16 * NCONST)
            nc.scalar.activation(a_neg[:], a_log[:], ACT.Exp).then_inc(s["act_chain"], 1)
            act.wait_ge(s["act_chain"], 1)
            nc.scalar.mul(a_neg[:], a_neg[:], -1.0).then_inc(s["act_chain"], 1)
            act.wait_ge(s["mods_rows"], 1)
            act.wait_ge(s["setup_chain"], 1)
            with act.Fori(0, G) as g:
                act.wait_ge(s["nxT_done"], g + 1)
                for q in range(GS):
                    last = nc.scalar.activation(hT[:, q * SEQ:(q + 1) * SEQ], banks(0, 2)[:, q * SEQ:(q + 1) * SEQ],
                                                ACT.Identity, bias=shift_a[:, bass.ds(g * GS + q, 1)],
                                                scale=scale_a[:, bass.ds(g * GS + q, 1)])
                    if q % 2:
                        last.then_inc(s["hT_ready"], 1)
                for h in range(2):
                    act.wait_ge(s["xz_done"], 8 * g + 2 * h + 2)
                    src = banks(2 + 2 * h, 2)
                    nc.scalar.copy(xcp[:, h, :, TAPS - 1:], src.rearrange("p (q t) -> p q t", q=GS)).then_inc(
                        s["xcp_ready"], 1)
                    nc.scalar.activation(acc[:, h, :], src, ACT.Identity, bias=cols[:, h, TAPS:TAPS + 1],
                                         scale=cols[:, h, TAPS - 1:TAPS]).then_inc(s["tap_ready"], 1)
                for h in range(2):
                    for k in range(2):
                        act.wait_ge(s["xz_done"], 8 * g + 4 + 2 * h + k + 1)
                        nc.scalar.activation(sz[:, h, k * 512:(k + 1) * 512], PS[:, (6 + 2 * h + k) % 8, :],
                                             ACT.Silu).then_inc(s["sz_ready"], 1)
                for h in range(2):
                    act.wait_ge(s["conv_done"], 2 * g + h + 1)
                    nc.scalar.activation(xsT[:, h, :], acc[:, h, :], ACT.Silu).then_inc(s["xs_ready"], 1)
                act.wait_ge(s["nabs_ready"], g + 1)
                nc.scalar.activation(sp1[:], sp0[:], ACT.Exp).then_inc(s["act_chain"], 1)
                act.wait_ge(s["act_chain"], g + 3)
                nc.scalar.activation(sp2[:], sp1[:], ACT.Ln, bias=1.0).then_inc(s["soft_ready"], 1)
                for k in range(4):
                    act.wait_ge(s["xst_done"], 4 * g + k + 1)
                    nc.scalar.copy(xs_tok[:, 2 * k:2 * k + 2, :].rearrange("p j d -> p (j d)"),
                                   PS[:, 2 + k, :]).then_inc(s["xst_ready"], 1)
                act.wait_ge(s["levels_in"], g + 1)
                nc.scalar.activation(lev[:], lev[:], ACT.Exp).then_inc(s["levels_exp"], 1)
                for k in range(2):
                    act.wait_ge(s["pairs_in"], 2 * g + k + 1)
                    v = pair[:, 4 * k:4 * k + 4].rearrange("p j a n -> p (j a n)")
                    nc.scalar.activation(v, v, ACT.Exp).then_inc(s["pairs_exp"], 1)
                for k in range(4):
                    act.wait_ge(s["pqT_done"], 4 * g + k + 1)
                    nc.scalar.copy(pqT[:, k // 2, 4 * (k % 2):4 * (k % 2) + 4, :].rearrange("p j t -> p (j t)"),
                                   PS[:, 4 + k, :]).then_inc(s["pqT_ready"], 1)
                act.wait_ge(s["m_done"], g + 1)
                nc.scalar.copy(mT[:, :, 1, :], PS[:, 2, :].rearrange("p (q t) -> p q t", q=GS)).then_inc(
                    s["mo_ready"], 1)
                act.wait_ge(s["h2_ready"], g + 1)
                nc.scalar.copy(h2[:, 1, :, 0:P], h2[:, 0, :, 0:P]).then_inc(s["copy_ready"], 1)
                act.wait_ge(s["h2T_done"], g + 1)
                nc.scalar.copy(xh[:], banks(2, 2)).then_inc(s["xh_ready"], 1)
                act.wait_ge(s["soft_in"], g + 1)
                nc.scalar.activation(ex[:], ex[:], ACT.Exp).then_inc(s["soft_out"], 1)
                for k in range(2):
                    silu_hi(2 * g + k)
                    keep_result(2 * g + k)

            act.wait_ge(s["plan_ready"], 1)

            def split_tile(i):
                act.wait_ge(s["xt_done"], i + 1)
                nc.scalar.copy(xh[:, 0:TILE], PS[:, 7, :]).then_inc(s["rh_ready"], 1)

            split_tile(0)
            with act.Fori(0, E) as e:
                tiles = act.value_load(plan[0:1, 0, bass.ds(e, 1)], min_val=1, max_val=TOKENS // TILE)
                first = act.value_load(plan[0:1, 1, bass.ds(e, 1)], min_val=0, max_val=3 * TOKENS // TILE)
                with act.Fori(0, tiles) as t:
                    i = first + t
                    silu_hi(SHARED + i)
                    split_tile(i + 1)
                    keep_result(SHARED + i)

        @block.vector
        def _(dve):
            V = nc.vector
            PER_GROUP = 47
            chain = {"base": 0, "n": 0}

            def link(ins):
                ins.then_inc(s["dve_chain"], 1)
                chain["n"] += 1
                dve.wait_ge(s["dve_chain"], chain["base"] + chain["n"])

            def bc(ap, shape):
                return ap.to_broadcast(shape)

            dve.wait_ge(s["mods_pe"], 1)
            V.tensor_copy(shift_a[:], PS[:, 0, 0:SEQS])
            V.tensor_scalar_add(scale_a[:], PS[:, 0, SEQS:2 * SEQS], 1.0)
            rows = PS[0:SEQS, 1, :].rearrange("p (m d) -> p m d", m=4)
            V.tensor_copy(mod_rows[:, 1, :], rows[:, 1, :])
            V.tensor_scalar_add(mod_rows[:, 2, :], rows[:, 2, :], 1.0)
            V.tensor_copy(mod_rows[:, 0, :], rows[:, 0, :])
            link(V.tensor_copy(mod_rows[:, 3, :], rows[:, 3, :]))
            for k, m in enumerate((0, 3)):
                V.tensor_scalar(mod_tmp[:, k, :], mod_rows[:, m, :], 0.0, 2.0, ALU.is_ge, ALU.mult)
                link(V.scalar_tensor_tensor(mod_rows[:, m, :], mod_rows[:, m, :], -1.0, mod_rows[:, m, :],
                                            ALU.mult, ALU.max))
            link(V.tensor_scalar_add(mod_tmp[:], mod_tmp[:], -1.0))
            for k, m in enumerate((0, 3)):
                last = V.scalar_tensor_tensor(mod_rows[:, m, :], mod_rows[:, m, :], 0.25, mod_tmp[:, k, :],
                                              ALU.max, ALU.mult)
            last.then_inc(s["mods_rows"], 1)
            dve.wait_ge(s["consts_in"], 16 * NCONST)
            V.tensor_copy(base[:], S["region"])
            link(V.tensor_copy(gate_hi[:], gate_w[:]))
            link(V.tensor_tensor(gate_lo[:], gate_w[:], gate_hi[:].bitcast(F32), ALU.subtract))
            V.memset(aux_w[:], 0.0)
            link(V.memset(aux_d[:], NOWHERE))
            V.engine_nop().then_inc(s["table_used"], 1)
            dve.wait_ge(s["act_chain"], 2)
            setup_links = chain["n"]

            def norm(src, out, count):
                apart(dve)
                for j in range(GC):
                    last = V.bn_stats(stats[:, j, :], src(j))
                link(last)
                apart(dve)
                for j in range(GC):
                    last = V.bn_aggr(mv[:, j, :], stats[:, j, :])
                last.then_inc(s["var_ready"], 1)
                dve.wait_ge(s["var_ready"], count)
                dve.wait_ge(s["rstd_ready"], count)
                for j in range(GC):
                    last = V.tensor_scalar(out[:, j, :], src(j), mv[:, j, 0:1], rstd[:, j:j + 1],
                                           ALU.subtract, ALU.mult)
                return last

            def product(I, c):
                dve.wait_ge(s["silu_done"], I * FC + c + 1)
                dve.wait_ge(s["up_done"], I * FC + c + 1)
                V.tensor_tensor(prod[:, c % 3, :], PS[:, 3 + c % 3, :], sg[:, c % 3, :], ALU.mult).then_inc(
                    s["prod_done"], 1)

            def low(I, c):
                dve.wait_ge(s["ah_ready"], I * FC + c + 1)
                V.tensor_tensor(al[:, c % 3, :], prod[:, c % 3, :], ah[:, c % 3, :].bitcast(F32),
                                ALU.subtract).then_inc(s["al_ready"], 1)

            with dve.Fori(0, G) as g:
                chain["base"], chain["n"] = g * PER_GROUP + setup_links, 0

                def xg(j):
                    return X[:, bass.ds(g * GC + j, 1), :].rearrange("p o d -> p (o d)")

                xall = X[:, bass.ds(g * GC, GC), :]
                dve.wait_ge(s["x_in"], 16 * G)
                norm(xg, nx, 2 * g + 1).then_inc(s["nx_ready"], 1)
                for h in range(2):
                    dve.wait_ge(s["xcp_ready"], 2 * g + h + 1)
                    dve.wait_ge(s["tap_ready"], 2 * g + h + 1)
                    o = acc[:, h, :].rearrange("p (q t) -> p q t", q=GS)
                    for k in range(TAPS - 1):
                        last = V.scalar_tensor_tensor(o, xcp[:, h, :, k:k + SEQ], cols[:, h, k:k + 1], o,
                                                      ALU.mult, ALU.add)
                        if k < TAPS - 2:
                            link(last)
                    last.then_inc(s["conv_done"], 1)
                dve.wait_ge(s["dbc_done"], g + 1)
                link(V.tensor_copy(dbc[:].rearrange("p j n -> p (j n)"), PS[:, 6, 0:GC * XD]))
                V.scalar_tensor_tensor(sp0[:], dbc[:, :, 0], -1.0, dbc[:, :, 0], ALU.mult, ALU.min).then_inc(
                    s["nabs_ready"], 1)
                Bp, Cp = dbc[:, :, 1:1 + NS], dbc[:, :, 1 + NS:XD]
                full = [P, GC, BLK, NS]
                V.tensor_tensor(c_exp, bc(Cp.unsqueeze(2), full), bc(S["equal"].unsqueeze(1).unsqueeze(3), full),
                                ALU.mult).then_inc(s["cexp_ready"], 1)
                dve.wait_ge(s["soft_ready"], g + 1)
                link(V.scalar_tensor_tensor(delta[:], dbc[:, :, 0], 0.0, sp2[:], ALU.max, ALU.add))
                V.tensor_tensor(dl_upto[:], bc(delta[:].unsqueeze(2), [P, GC, BLK]),
                                bc(S["upto"].unsqueeze(1), [P, GC, BLK]), ALU.mult).then_inc(s["delta_ready"], 1)
                link(V.tensor_tensor(dB[:], bc(delta[:].unsqueeze(2), [P, GC, NS]), Bp, ALU.mult))
                dve.wait_ge(s["spans_done"], g + 1)
                lv = [P, GC, 4, NS]
                spans = PS[:, 7, 0:4 * GC].rearrange("p (l j) -> p j l", l=4)
                A = a_neg[:]
                V.tensor_tensor(lev[:], bc(spans.unsqueeze(3), lv), bc(A.unsqueeze(1).unsqueeze(1), lv),
                                ALU.mult).then_inc(s["levels_in"], 1)
                within = PS[:, 7, 64:64 + P].rearrange("p (j a) -> p j a", j=GC)
                half = [P, GC // 2, BLK, NS]
                for k in range(2):
                    j0, j1 = k * GC // 2, (k + 1) * GC // 2
                    V.tensor_tensor(pair[:, j0:j1], bc(within[:, j0:j1].unsqueeze(3), half),
                                    bc(A.unsqueeze(1).unsqueeze(1), half), ALU.mult).then_inc(s["pairs_in"], 1)
                dve.wait_ge(s["levels_exp"], g + 1)
                dve.wait_ge(s["cg_done"], 4 * g + 4)
                V.tensor_tensor(lev_c[:], lev[:], bc(Cp.unsqueeze(2), lv), ALU.mult)
                link(V.tensor_tensor(lev_b[:], lev[:], bc(dB[:].unsqueeze(2), lv), ALU.mult))
                for k, (src, role) in enumerate(((lev_c, "upper"), (lev_b, "lower"))):
                    pv = pq[:, k].rearrange("p j (b n) -> p j b n", n=NS)
                    role7 = S[role][:, 0:2].unsqueeze(1).unsqueeze(3)
                    V.tensor_tensor(pv[:, :, 0, :].rearrange("p (q k) n -> p q k n", k=2),
                                    src[:, :, 0, :].rearrange("p (q k) n -> p q k n", k=2),
                                    bc(role7, [P, GS, 2, NS]), ALU.mult)
                    b0 = 1
                    for l in range(1, 4):
                        nb = 1 << (l - 1)
                        sh = [P, GC, nb, NS]
                        last = V.tensor_tensor(pv[:, :, b0:b0 + nb, :], bc(src[:, :, l, :].unsqueeze(2), sh),
                                               bc(S[role][:, b0 + 1:b0 + 1 + nb].unsqueeze(1).unsqueeze(3), sh),
                                               ALU.mult)
                        b0 += nb
                last.then_inc(s["pq_ready"], 1)
                for k in range(4):
                    if k % 2 == 0:
                        dve.wait_ge(s["pairs_exp"], 2 * g + k // 2 + 1)
                    v = pair[:, 2 * k:2 * k + 2].rearrange("p j a n -> p (j a n)")
                    V.tensor_tensor(v, v, PS[:, k, :], ALU.mult).then_inc(s["cg_used"], 1)
                dve.wait_ge(s["cg_used"], 4 * g + 4)
                link(V.tensor_tensor(pair[:], pair[:], bc(dB[:].unsqueeze(2), full), ALU.mult))
                link(V.tensor_reduce(wd[:], pair[:], AX.X, ALU.add))
                sh = [P, GC, NB, BLK]
                dg = diag[:].rearrange("p j (b a) -> p j b a", a=BLK)
                link(V.tensor_tensor(dg, bc(wd[:].unsqueeze(2), sh), bc(S["block"].unsqueeze(1).unsqueeze(3), sh),
                                     ALU.mult))
                dve.wait_ge(s["m_done"], g + 1)
                V.tensor_tensor(mT[:, :, 0:3:2, :], banks(0, 2).rearrange("p (q k t) -> p q k t", q=GS, k=2),
                                diag[:].rearrange("p (q k) t -> p q k t", k=2), ALU.add).then_inc(s["mT_ready"], 1)
                for h in range(2):
                    dve.wait_ge(s["y_done"], 2 * g + h + 1)
                    link(V.scalar_tensor_tensor(yT[:, h, :], xsT[:, h, :], cols[:, h, TAPS + 1:TAPS + 2],
                                                banks(4 + 2 * h, 2), ALU.mult, ALU.add))
                    V.tensor_tensor(yT[:, h, :], yT[:, h, :], sz[:, h, :], ALU.mult).then_inc(s["y_ready"], 1)
                dve.wait_ge(s["o_done"], g + 1)
                dve.wait_ge(s["table_in"], 16 * (g + 1))
                seq = [P, GS, 2, P]

                def tab(m):
                    return bc(table[:, :, m:m + 1, :], seq)

                def by_seq(ap):
                    return ap.rearrange("p (q k) d -> p q k d", k=2)

                link(V.tensor_tensor(by_seq(nx[:]), banks(0, 2).rearrange("p (q k d) -> p q k d", q=GS, k=2), tab(0),
                                     ALU.mult))
                link(V.tensor_tensor(xall, xall, nx[:], ALU.add))
                link(norm(xg, nx, 2 * g + 2))
                link(V.tensor_tensor(by_seq(nx[:]), by_seq(nx[:]), tab(2), ALU.mult))
                V.tensor_tensor(by_seq(h2[:, 0, :, 0:P]), by_seq(nx[:]), tab(1), ALU.add).then_inc(s["h2_ready"], 1)
                dve.wait_ge(s["xh_ready"], g + 1)
                V.tensor_tensor(xl[:], banks(2, 2), xh[:].bitcast(F32), ALU.subtract).then_inc(s["xl_ready"], 1)
                dve.wait_ge(s["logits_done"], g + 1)
                ge = [P, GC, E]
                link(V.tensor_copy(lg[:].rearrange("p j e -> p (j e)"), PS[:, 4, 0:GC * E]))
                rev = bc(S["rev"].unsqueeze(1), ge)
                for k in range(2):
                    src = lg if k == 0 else r2
                    link(V.tensor_reduce(top[:, k, :], src[:], AX.X, ALU.max))
                    if k == 0:
                        V.tensor_tensor(ex[:], lg[:], bc(top[:, 0, :].unsqueeze(2), ge), ALU.subtract).then_inc(
                            s["soft_in"], 1)
                    link(V.tensor_tensor(r1[:], src[:], bc(top[:, k, :].unsqueeze(2), ge), ALU.is_equal))
                    link(V.tensor_tensor(r1[:], r1[:], rev, ALU.mult))
                    link(V.tensor_reduce(top[:, 2, :], r1[:], AX.X, ALU.max))
                    link(V.tensor_tensor(oh[:, k], r1[:], bc(top[:, 2, :].unsqueeze(2), ge), ALU.is_equal))
                    if k == 0:
                        link(V.scalar_tensor_tensor(r2[:], oh[:, 0], -3.0e38, lg[:], ALU.mult, ALU.add))
                link(V.tensor_tensor(picked[:].rearrange("p e j -> p j e"), oh[:, 0], oh[:, 1], ALU.add))
                V.tensor_tensor_scan(ranks[:].rearrange("p e j -> p (e j)"), S["seg"],
                                     picked[:].rearrange("p e j -> p (e j)"), 0.0, ALU.mult, ALU.add).then_inc(
                    s["picked_ready"], 1)
                dve.wait_ge(s["soft_out"], g + 1)
                link(V.tensor_reduce(top[:, 3, :], ex[:], AX.X, ALU.add))
                V.reciprocal(top[:, 4, :], top[:, 3, :])
                link(V.tensor_tensor(r1[:], ex[:], oh[:, 1], ALU.mult))
                link(V.tensor_reduce(top[:, 5, :], r1[:], AX.X, ALU.add))
                link(V.tensor_tensor(top[:, 5, :], top[:, 5, :], top[:, 4, :], ALU.mult))
                link(V.scalar_tensor_tensor(top[:, 6, :], top[:, 4, :], 1e-8, top[:, 5, :], ALU.add, ALU.add))
                link(V.reciprocal(top[:, 7, :], top[:, 6, :]))
                dve.wait_ge(s["counts_done"], g + 1)
                dve.wait_ge(s["picked_ready"], g + 1)
                link(V.tensor_tensor(base2[:], base[:], PS[:, 5, 0:E], ALU.add))
                V.tensor_tensor(base[:], base[:], PS[:, 5, E:2 * E], ALU.add)
                link(V.tensor_tensor(ranks[:], ranks[:], picked[:], ALU.subtract))
                link(V.tensor_tensor(ranks[:], ranks[:], bc(base2[:].unsqueeze(2), [P, E, GC]), ALU.add))
                dve.wait_ge(s["copy_ready"], g + 1)
                for k in range(2):
                    V.tensor_tensor(h2[:, k, :, P], top[:, 4 + k, :], top[:, 7, :], ALU.mult)
                    V.tensor_copy(h2[:, k, :, P + 1].bitcast(I32),
                                  token2[:, bass.ds(g * GC, GC), k:k + 1].rearrange("p j o -> p (j o)"))
                    link(V.tensor_tensor(oh[:, k], oh[:, k], ranks[:].rearrange("p e j -> p j e"), ALU.mult))
                    link(V.tensor_reduce(top[:, k, :], oh[:, k], AX.X, ALU.add))
                    last = V.tensor_copy(slot[:, k, :], top[:, k, :])
                last.then_inc(s["rows_ready"], 1)
                for k in range(2):
                    I = 2 * g + k
                    for c in range(FC):
                        product(I, c)
                        low(I, c)
                    dve.wait_ge(s["yt_done"], I + 1)
                    tb = bc(table[:, 2 * k:2 * k + 2, 3:4, :], [P, 2, 2, P])
                    link(V.tensor_tensor(prod[:, 0, :].rearrange("p (q k d) -> p q k d", q=2, k=2),
                                         PS[:, 7, :].rearrange("p (q k d) -> p q k d", q=2, k=2), tb, ALU.mult))
                    xs_ = X[:, bass.ds(g * GC + 4 * k, 4), :]
                    V.tensor_tensor(xs_, xs_, prod[:, 0, :].rearrange("p (j d) -> p j d", d=P), ALU.add).then_inc(
                        s["y_out"], 1)
                    dve.wait_ge(s["y_out"], I + 1)
                dve.wait_ge(s["sorted_out"], 16 * 2 * GC * (g + 1))
                apart(dve)
                V.engine_nop().then_inc(s["table_used"], 1)
                assert chain["n"] == PER_GROUP, chain["n"]

            chain["base"], chain["n"] = G * PER_GROUP + setup_links, 0
            link(V.tensor_tensor(plan_f[:, 3, :], base[:], S["region"], ALU.subtract))
            link(V.tensor_tensor(cmp[:], bc(plan_f[:, 3, :].unsqueeze(2), [P, E, E]),
                                 bc(S["many"].unsqueeze(1), [P, E, E]), ALU.is_gt))
            link(V.tensor_reduce(plan_f[:, 0, :], cmp[:], AX.X, ALU.add))
            link(V.tensor_scalar(plan_f[:, 0, :], plan_f[:, 0, :], 1.0, None, ALU.max))
            link(V.tensor_tensor_scan(plan_f[:, 1, :], M["ones"][:, 0:E], plan_f[:, 0, :], 0.0, ALU.mult, ALU.add))
            link(V.tensor_tensor(plan_f[:, 1, :], plan_f[:, 1, :], plan_f[:, 0, :], ALU.subtract))
            V.tensor_copy(plan[:, 2, :], base[:])
            V.tensor_copy(plan[:, 0:2, :], plan_f[:, 0:2, :]).then_inc(s["plan_ready"], 1)
            V.engine_nop().then_inc(s["aux_read"], 1)

            def take_aux(i):
                dve.wait_ge(s["rh_ready"], i + 1)
                V.tensor_tensor(xl[:, 0:TILE], PS[:, 7, :], xh[:, 0:TILE].bitcast(F32), ALU.subtract).then_inc(
                    s["rl_ready"], 1)
                V.tensor_copy(aux_w[:, 1, :], xin[:, :, P])
                V.tensor_copy(aux_d[:, 1, :], xin[:, :, P + 1].bitcast(I32)).then_inc(s["aux_read"], 1)

            dve.wait_ge(s["plan_ready"], 1)
            take_aux(0)

            def give_rows(i):
                dve.wait_ge(s["yt_done"], SHARED + 1 + i)
                V.tensor_tensor(y_rows[:], PS[:, 7, :].rearrange("p (r d) -> p r d", r=TR),
                                bc(aux_w[:, 0, :].unsqueeze(2), [P, TR, P]), ALU.mult).then_inc(s["y_out"], 1)

            with dve.Fori(0, E) as e:
                tiles = dve.value_load(plan[0:1, 0, bass.ds(e, 1)], min_val=1, max_val=TOKENS // TILE)
                first = dve.value_load(plan[0:1, 1, bass.ds(e, 1)], min_val=0, max_val=3 * TOKENS // TILE)
                with dve.Fori(0, tiles) as t:
                    i = first + t
                    for c in range(FC):
                        product(SHARED + i, c)
                        if c == 0:
                            give_rows(i)
                        low(SHARED + i, c)
                    dve.wait_ge(s["results_out"], 64 * (i + 1))
                    dve.wait_ge(s["aux_read"], i + 2)
                    V.tensor_copy(aux_w[:, 0, :], aux_w[:, 1, :])
                    V.tensor_copy(aux_d[:, 0, :], aux_d[:, 1, :]).then_inc(s["soft_in"], 1)
                    dve.wait_ge(s["soft_in"], G + i + 1)
                    take_aux(i + 1)
            last_tiles = dve.value_load(plan[0:1, 0, E - 1:E], min_val=1, max_val=TOKENS // TILE)
            last_first = dve.value_load(plan[0:1, 1, E - 1:E], min_val=0, max_val=3 * TOKENS // TILE)
            count = last_first + last_tiles
            give_rows(count)
            dve.wait_ge(s["gb_in"], 16)
            for g in range(G):
                dve.wait_ge(s[f"final_in{g % 2}"], 16 * (g // 2 + 1))
                f = fin[g % 2]
                link(V.tensor_tensor(f[:, :, 0, :], f[:, :, 0, :], f[:, :, 1, :], ALU.add))
                f0 = f[:, :, 0, :].rearrange("p (q k) d -> p q k d", k=2)
                link(V.tensor_tensor(f0, f0, bc(gb_all[:, g * GS:(g + 1) * GS, :].unsqueeze(2), [P, GS, 2, P]),
                                     ALU.mult))
                xg_ = X[:, g * GC:(g + 1) * GC, :]
                V.tensor_tensor(xg_, xg_, f[:, :, 0, :], ALU.add).then_inc(s["final_ready"], 1)


def kernel(L0_attn_x, L0_attn_W_in, L0_attn_conv_w, L0_attn_conv_b, L0_attn_W_x, L0_attn_A_log, L0_attn_D,
           L0_attn_W_out, L0_ffn_gate_weight, L0_ffn_shared_gate_up, L0_ffn_shared_down,
           L0_ffn_experts_gate_up, L0_ffn_experts_down, L0_c, L0_wmod):
    import concourse.bacc as bacc
    from concourse.bass_utils import run_bass_kernel_spmd

    n = np.asarray
    big, small, token = constants()
    arrays = {
        "x": n(L0_attn_x).reshape(TOKENS, P),
        "L0_attn_W_in": n(L0_attn_W_in),
        "L0_attn_W_out": n(L0_attn_W_out),
        "L0_attn_W_x": n(L0_attn_W_x),
        "a_log": n(L0_attn_A_log).reshape(1, NS),
        "cols": np.concatenate([n(L0_attn_conv_w).reshape(DI, TAPS), n(L0_attn_conv_b)[:, None],
                                n(L0_attn_D)[:, None]], 1),
        "gate_t": n(L0_ffn_gate_weight).T,
        "c_t": n(L0_c).T,
        "L0_wmod": n(L0_wmod),
        "w_gu": np.concatenate([n(L0_ffn_shared_gate_up)[None], n(L0_ffn_experts_gate_up)], 0).transpose(0, 2, 1),
        "w_dn": np.concatenate([n(L0_ffn_shared_down)[None], n(L0_ffn_experts_down)], 0).transpose(0, 2, 1),
        "big": big, "small": small, "token": token,
    }
    arrays = {k: np.ascontiguousarray(v) for k, v in arrays.items()}
    nc = bacc.Bacc("TRN2", target_bir_lowering=False, num_devices=1)
    aps = {k: nc.dram_tensor("in_" + k, v.shape, mybir.dt.from_np(v.dtype), kind="ExternalInput").ap()
           for k, v in arrays.items()}
    aps["out"] = nc.dram_tensor("out", (TOKENS, P), F32, kind="ExternalOutput").ap()
    adaln_block(nc, aps)
    r = run_bass_kernel_spmd(nc, [{"in_" + k: v for k, v in arrays.items()}], core_ids=[0])
    return r.results[0]["out"].reshape(SEQS, SEQ, P)
```

```python
from contextlib import ExitStack

import numpy as np
import concourse.bass as bass
from concourse import mybir

F32 = mybir.dt.float32
F32R = mybir.dt.float32r
I32 = mybir.dt.int32
U32 = mybir.dt.uint32
ALU = mybir.AluOpType
ACT = mybir.ActivationFunctionType
AX = mybir.AxisListType

P = 128
SEQS = 16
SEQ = 256
TOKENS = SEQS * SEQ
CH = TOKENS // P
G = 8
GC = CH // G
GS = SEQS // G
GT = GC * P
DI = 2 * P
NS = 16
XD = 2 * NS + 1
TAPS = 4
BLK = 16
NB = P // BLK
LEVELS = (128, 64, 32, 16)
E = 8
FF = 938
FC = 8
FL = FF - (FC - 1) * P
WC = 3 * FC * P
TILE = 512
TR = TILE // P
REGION = TOKENS + TILE
ROW = P + 2
NOWHERE = 4 * TOKENS
SHARED = TOKENS // TILE
EPS = 1e-5

CONST = ("ident", "below7", "above7", "lvl6", "lvl5", "lvl4", "later16", "upto16", "before", "ones")


def constants():
    u = np.arange(P)[:, None]
    t = np.arange(P)[None, :]
    same = u // BLK == t // BLK

    def span(half):
        mid = t // (2 * half) * (2 * half) + half
        return np.where(t >= mid, (u >= mid) & (u <= t), (u > t) & (u < mid))

    mats = [u == t, u > t, u <= t, span(64), span(32), span(16), same & (u > t), same & (u >= t), u < t, u >= 0]
    tau = np.arange(BLK)[None, :]
    upto = u % BLK <= tau
    equal = u % BLK == tau
    block = u // BLK == np.arange(NB)[None, :]
    roles = []
    for want in (1, 0):
        cols = [np.full((P, 1), par == want) for par in (0, 1)]
        for half in LEVELS[1:]:
            for b in range(P // (2 * half)):
                cols.append((u // (2 * half) == b) & ((u // half) % 2 == want))
        roles.append(np.concatenate(cols, 1))
    expert = np.arange(E)[None, :] + 0 * u
    seg = np.tile(np.arange(GC) > 0, E)[None, :] & (u >= 0)
    many = np.arange(E)[None, :] * TILE + 0 * u
    small = np.concatenate([upto, equal, block, *roles, seg, E - expert, expert * REGION, many], 1)
    big = np.concatenate([np.broadcast_to(m, (P, P)) for m in mats], 1)
    token = (np.arange(CH)[None, :, None] * P + np.arange(P)[:, None, None]) * 2 + np.arange(2)[None, None, :]
    return (np.ascontiguousarray(big, np.float32), np.ascontiguousarray(small, np.float32),
            np.ascontiguousarray(token, np.int32))


SMALL = {}
_at = 0
for _name, _n in (("upto", BLK), ("equal", BLK), ("block", NB), ("upper", 9), ("lower", 9), ("seg", E * GC),
                  ("rev", E), ("region", E), ("many", E)):
    SMALL[_name] = (_at, _n)
    _at += _n
NSMALL = _at
NCONST = 9


def adaln_block(nc, a):
    ctx = ExitStack()
    with ctx:
        def sb(name, shape, dt=F32):
            return ctx.enter_context(nc.sbuf_tensor(name, shape, dt))

        def sem(name):
            return ctx.enter_context(nc.semaphore(name))

        mods_dram = nc.dram_tensor("mods_dram", (SEQS, 4, P), F32, kind="Internal").ap()
        sorted_dram = nc.dram_tensor("sorted_dram", (E * REGION, ROW), F32, kind="Internal").ap()
        result_dram = nc.dram_tensor("result_dram", (2 * TOKENS, P), F32, kind="Internal").ap()

        mats = sb("mats", [P, len(CONST), P])
        M = {n: mats[:, i, :] for i, n in enumerate(CONST)}
        small = sb("small", [P, NSMALL])
        S = {n: small[:, o:o + k] for n, (o, k) in SMALL.items()}
        token2 = sb("token2", [P, CH, 2], I32)
        w_in = sb("w_in", [P, 4, P])
        w_out = sb("w_out", [P, 2, P])
        w_x = sb("w_x", [P, 2, XD])
        cols = sb("cols", [P, 2, TAPS + 2])
        a_log = sb("a_log", [P, NS])
        a_neg = sb("a_neg", [P, NS])
        gate_w = sb("gate_w", [P, E])
        gate_hi = sb("gate_hi", [P, E], F32R)
        gate_lo = sb("gate_lo", [P, E], F32R)
        c_t = sb("c_t", [P, SEQS])
        sc_t = sb("sc_t", [P, SEQS])
        shift_a = sb("shift_a", [P, SEQS])
        scale_a = sb("scale_a", [P, SEQS])
        mod_rows = sb("mod_rows", [SEQS, 4, P])
        mod_tmp = sb("mod_tmp", [SEQS, 2, P])
        tab = sb("tab", [P, GS, 3, P])
        tab_g = sb("tab_g", [P, GS, P])
        gb_all = sb("gb_all", [P, SEQS, P])
        minus_half = sb("minus_half", [P, GC])

        X = sb("X", [P, CH, P])
        stats_a = sb("stats_a", [P, GC, 6])
        mv_a = sb("mv_a", [P, GC, 2])
        rstd_a = sb("rstd_a", [P, GC])
        nx_a = sb("nx_a", [P, GC, P])
        hT = sb("hT", [P, GT])
        xcp = sb("xcp", [P, 2, GS, SEQ + TAPS - 1])
        acc = sb("acc", [P, 2, GT])
        xsT = sb("xsT", [P, 2, GT])
        sz = sb("sz", [P, 2, GT])
        xs_tok = sb("xs_tok", [P, GC, DI])
        dbc = sb("dbc", [P, GC, XD])
        sp0 = sb("sp0", [P, GC])
        sp1 = sb("sp1", [P, GC])
        sp2 = sb("sp2", [P, GC])
        delta = sb("delta", [P, GC])
        dl_upto = sb("dl_upto", [P, GC, BLK])
        dB = sb("dB", [P, GC, NS])
        c_exp = sb("c_exp", [P, GC, BLK, NS])
        pq = sb("pq", [P, 2, GC, P])
        pqT = sb("pqT", [P, 2, GC, P])
        lev = sb("lev", [P, GC, 4, NS])
        lev_c = sb("lev_c", [P, GC, 4, NS])
        lev_b = sb("lev_b", [P, GC, 4, NS])
        pair = sb("pair", [P, GC, BLK, NS])
        wd = sb("wd", [P, GC, BLK])
        diag = sb("diag", [P, GC, P])
        mT = sb("mT", [P, GS, 3, P])
        yT = sb("yT", [P, 2, GT])
        nx_b = sb("nx_b", [P, GC, P])
        stats_b = sb("stats_b", [P, GC, 6])
        mv_b = sb("mv_b", [P, GC, 2])
        rstd_b = sb("rstd_b", [P, GC])
        h2 = sb("h2", [P, 2, GC, ROW])
        lg = sb("lg", [P, GC, E])
        r1 = sb("r1", [P, GC, E])
        r2 = sb("r2", [P, GC, E])
        oh = sb("oh", [P, 2, GC, E])
        ex = sb("ex", [P, GC, E])
        top = sb("top", [P, 10, GC])
        picked = sb("picked", [P, E, GC])
        ranks = sb("ranks", [P, E, GC])
        base = sb("base", [P, E])
        base2 = sb("base2", [P, E])
        slot = sb("slot", [P, 2, GC], I32)
        plan_f = sb("plan_f", [P, 4, E])
        plan = sb("plan", [P, 3, E], I32)
        cmp = sb("cmp", [P, E, E])
        pad = sb("pad", [P, TR, ROW])
        xh = sb("xh", [P, TILE], F32R)
        xl = sb("xl", [P, TILE], F32R)
        stage = sb("stage", [P, WC])
        w_hi = [sb(f"w_hi{i}", [P, WC], F32R) for i in range(2)]
        w_lo = [sb(f"w_lo{i}", [P, WC], F32R) for i in range(2)]
        sg = sb("sg", [P, 3, TILE])
        prod = sb("prod", [P, 3, TILE])
        ah = sb("ah", [P, 3, TILE], F32R)
        al = sb("al", [P, 3, TILE], F32R)
        y_sb = sb("y_sb", [P, TILE])
        gated = sb("gated", [P, TILE])
        xin = sb("xin", [P, TR, ROW])
        y_rows = sb("y_rows", [P, TR, P])
        aux_w = sb("aux_w", [P, 2, TR])
        aux_d = sb("aux_d", [P, 2, TR], I32)
        fin = [v[:].rearrange(d).rearrange("p (j k d) -> p j k d", j=GC, k=2)
               for v, d in ((pair, "p j a n -> p (j a n)"), (pqT, "p k j t -> p (k j t)"))]

        PS = ctx.enter_context(nc.psum_tensor("PS", [P, 8, 512], F32))
        NARROW = {"gate": (5,), "up": (6,), "down": 7, "turn": 5}
        WIDE = {"gate": (0, 1, 2), "up": (3, 4, 5), "down": 6, "turn": 7}

        def bank(kind, where, c=0):
            b = where[kind]
            return PS[:, b if isinstance(b, int) else b[c % len(b)], :]

        names = """passed consts_in x_in c_in setup_mem stage_clear silu_c mods_pe mods_rows mods_out a_neg_ready
            tab_in tab_free tab_g_in tab_g_free
            var_a eps_a rstd_a nx_ready nxT_done hT_ready xz_done tap_ready conv_done sz_ready xs_ready
            dbc_done dbc_ready xst_done xst_ready nabs_ready exp1_done soft_ready delta_ready cexp_ready spans_done
            cg_done levels_in pairs_in levels_exp pairs_exp pq_ready pqT_done pqT_ready cg_used pairs_ready
            m_done mT_ready mo_ready y_done y_ready o_done var_b eps_b rstd_b h2_ready h2_both h2T_done
            xh_ready xl_ready logits_done lg_ready soft_in soft_out picked_ready counts_done counts_read
            rows_ready sorted_out dve_chain raw_in split_hi split_done gate_done up_done silu_done prod_done
            ah_ready al_ready y_bank_done y_sb_ready yt_done y_out gated_free tile_in xt_done rh_ready
            rl_ready aux_read aux_moved results_out plan_ready pads_out final_in0 final_in1 final_ready
            out_done gb_in""".split()
        s = {n: sem("s_" + n) for n in names}
        block = ctx.enter_context(nc.Block())

        def apart(engine):
            engine.sem_inc(s["passed"], 1)

        CUT = FC // 2
        NRAW = 4
        MAX_TILES = TOKENS // TILE
        MAX_FIRST = 2 * TOKENS // TILE + E

        def tiles_of(engine, e):
            tiles = engine.value_load(plan[0:1, 0, bass.ds(e, 1)], min_val=1, max_val=MAX_TILES)
            first = engine.value_load(plan[0:1, 1, bass.ds(e, 1)], min_val=0, max_val=MAX_FIRST)
            return tiles, first

        @block.sync
        def _(sp):
            def load_raw(x):
                gu = a["w_gu"][bass.ds(x, 1)].rearrange("o d f -> (o d) f")
                dn = a["w_dn"][bass.ds(x, 1)].rearrange("o f d -> (o f) d")
                last = FC - 1
                sp.dma_start(stage[:, 0:FF], gu[:, 0:FF]).then_inc(s["raw_in"], 16)
                sp.dma_start(stage[:, FC * P:FC * P + FF], gu[:, FF:2 * FF]).then_inc(s["raw_in"], 16)
                sp.dma_start(stage[:, 2 * FC * P:2 * FC * P + last * P].rearrange("p (c d) -> p c d", d=P),
                             dn[0:last * P, :].rearrange("(c p) d -> p c d", p=P)).then_inc(s["raw_in"], 16)
                sp.dma_start(stage[0:FL, 2 * FC * P + last * P:WC], dn[last * P:FF, :]).then_inc(s["raw_in"], 16)

            x_view = a["x"].rearrange("(c p) d -> p c d", p=P)

            def load_x(c0, n):
                sp.dma_start(X[:, c0:c0 + n, :], x_view[:, c0:c0 + n, :]).then_inc(s["x_in"], 16)

            def const(dst, src):
                sp.dma_start(dst, src).then_inc(s["consts_in"], 16)

            load_x(0, GC)
            sp.wait_ge(s["x_in"], 16)
            sp.dma_start(c_t[:], a["c_t"]).then_inc(s["c_in"], 16)
            sp.dma_start(stage[:, 0:6 * P], a["L0_wmod"]).then_inc(s["c_in"], 16)
            const(mats[:].rearrange("p m t -> p (m t)"), a["big"])
            const(w_in[:].rearrange("p m t -> p (m t)"), a["L0_attn_W_in"])
            const(cols[:], a["cols"].rearrange("(h p) d -> p h d", p=P))
            const(small[:], a["small"])
            const(token2[:], a["token"])
            const(w_out[:], a["L0_attn_W_out"].rearrange("(h p) d -> p h d", p=P))
            const(w_x[:], a["L0_attn_W_x"].rearrange("(h p) d -> p h d", p=P))
            const(a_log[:], a["a_log"].to_broadcast([P, NS]))
            const(gate_w[:], a["gate_t"])
            load_x(GC, CH - GC)
            sp.wait_ge(s["mods_rows"], 1)
            sp.dma_start(mods_dram, mod_rows[:]).then_inc(s["mods_out"], 16)
            sp.wait_ge(s["stage_clear"], 1)
            load_raw(0)
            sp.wait_ge(s["mods_out"], 16)

            def load_tab(g):
                sp.dma_start(tab[:], mods_dram[bass.ds(g * GS, GS), 0:3, :].unsqueeze(0).to_broadcast(
                    [P, GS, 3, P])).then_inc(s["tab_in"], 16)

            def load_tab_g(g):
                sp.dma_start(tab_g[:], mods_dram[bass.ds(g * GS, GS), 3, :].unsqueeze(0).to_broadcast(
                    [P, GS, P])).then_inc(s["tab_g_in"], 16)

            load_tab(0)
            load_tab_g(0)
            sp.dma_start(gb_all[:], mods_dram[:, 3, :].unsqueeze(0).to_broadcast([P, SEQS, P])).then_inc(s["gb_in"], 16)
            sp.wait_ge(s["split_done"], 1)
            load_raw(1)
            with sp.Fori(1, G) as g:
                sp.wait_ge(s["tab_free"], g)
                load_tab(g)
                sp.wait_ge(s["tab_g_free"], g)
                load_tab_g(g)
            sp.wait_ge(s["plan_ready"], 1)
            sp.wait_ge(s["setup_mem"], 2)
            sp.wait_ge(s["sorted_out"], 16 * 2 * CH)
            for e in range(E):
                row = sp.value_load(plan[0:1, 2, e:e + 1], min_val=e * REGION, max_val=e * REGION + TOKENS)
                sp.dma_start(sorted_dram[bass.ds(row, TILE)].rearrange("(p r) d -> p (r d)", p=P),
                             pad[:].rearrange("p r d -> p (r d)")).then_inc(s["pads_out"], 16)
            sp.wait_ge(s["pads_out"], 16 * E)

            def load_tile(row, i):
                sp.wait_ge(s["aux_read"], i + 1)
                sp.dma_start(xin[:].rearrange("p r d -> p (r d)"),
                             sorted_dram[bass.ds(row, TILE)].rearrange("(p r) d -> p (r d)", p=P)).then_inc(
                    s["tile_in"], 16)

            def expert(e, more):
                tiles, first = tiles_of(sp, e)
                if more:
                    sp.wait_ge(s["split_done"], e + 2)
                    load_raw(e + 2)
                with sp.Fori(0, tiles) as t:
                    load_tile(e * REGION + t * TILE, first + t)
                return first + tiles

            with sp.Fori(0, E - 1) as e:
                expert(e, True)
            count = expert(E - 1, False)
            load_tile(0, count)
            sp.wait_ge(s["results_out"], 64 * (count + 1))
            res = result_dram.rearrange("(c p k) d -> p c k d", p=P, k=2)
            out_view = a["out"].rearrange("(c p) d -> p c d", p=P)
            for g in range(G + 2):
                if g >= 2:
                    sp.wait_ge(s["final_ready"], g - 1)
                    q = g - 2
                    sp.dma_start(out_view[:, q * GC:(q + 1) * GC, :], X[:, q * GC:(q + 1) * GC, :]).then_inc(
                        s["out_done"], 16)
                if g < G:
                    sp.dma_start(fin[g % 2], res[:, g * GC:(g + 1) * GC]).then_inc(s[f"final_in{g % 2}"], 16)
            sp.wait_ge(s["tile_in"], 16 * (count + 1))
            apart(sp)
            sp.wait_ge(s["out_done"], 16 * G)

        @block.gpsimd
        def _(pool):
            V = nc.gpsimd

            def split_hi(x, buf):
                pool.wait_ge(s["raw_in"], 16 * NRAW * (x + 1))
                apart(pool)
                V.tensor_tensor(w_hi[buf][:], stage[:], M["ones"][:, 0:1].to_broadcast([P, WC]), ALU.mult).then_inc(
                    s["split_hi"], 1)

            def split_lo(x, buf):
                pool.wait_ge(s["split_hi"], x + 1)
                V.tensor_tensor(w_lo[buf][:], stage[:], w_hi[buf][:].bitcast(F32), ALU.subtract).then_inc(
                    s["split_done"], 1)

            def inverse_root(g, mv, rstd, k):
                pool.wait_ge(s["var_" + k], g + 1)
                apart(pool)
                V.tensor_scalar_add(rstd[:], mv[:, :, 1], EPS).then_inc(s["eps_" + k], 1)
                pool.wait_ge(s["eps_" + k], g + 1)
                V.tensor_tensor(rstd[:], rstd[:], minus_half[:], ALU.pow).then_inc(s["rstd_" + k], 1)

            def expand_c(g):
                full = [P, GC, BLK, NS]
                pool.wait_ge(s["dbc_ready"], g + 1)
                V.tensor_tensor(c_exp[:], dbc[:, :, 1 + NS:XD].unsqueeze(2).to_broadcast(full),
                                S["equal"].unsqueeze(1).unsqueeze(3).to_broadcast(full), ALU.mult).then_inc(
                    s["cexp_ready"], 1)

            def pairs_by_b(g):
                for k in range(2):
                    j0, j1 = k * GC // 2, (k + 1) * GC // 2
                    pool.wait_ge(s["cg_used"], 2 * g + k + 1)
                    V.tensor_tensor(pair[:, j0:j1], pair[:, j0:j1],
                                    dB[:, j0:j1].unsqueeze(2).to_broadcast([P, GC // 2, BLK, NS]),
                                    ALU.mult).then_inc(s["pairs_ready"], 1)

            def sort_rows(g):
                pool.wait_ge(s["rows_ready"], g + 1)
                apart(pool)
                for k in range(2):
                    for j in range(GC):
                        pool.indirect_dma_start(
                            out=sorted_dram, out_offset=bass.IndirectOffsetOnAxis(
                                ap=slot[:, k, j:j + 1].bitcast(U32), axis=0),
                            in_=h2[:, k, j, :], in_offset=None, bounds_check=E * REGION - 1,
                            oob_is_err=False).then_inc(s["sorted_out"], 16)

            def add_shared(g):
                pool.wait_ge(s["y_out"], g + 1)
                x = X[:, bass.ds(g * GC, GC), :].rearrange("p j d -> p (j d)")
                V.tensor_tensor(x, x, gated[:], ALU.add).then_inc(s["gated_free"], 1)

            V.memset(minus_half[:], -0.5)
            V.memset(gated[:], 0.0).then_inc(s["gated_free"], 1)
            V.memset(pad[:], 0.0).then_inc(s["setup_mem"], 1)
            V.memset(xcp[:, :, :, 0:TAPS - 1], 0.0)
            pool.wait_ge(s["setup_mem"], 1)
            V.memset(pad[:, :, P + 1:P + 2].bitcast(I32), NOWHERE).then_inc(s["setup_mem"], 1)
            pool.wait_ge(s["setup_mem"], 2)
            inverse_root(0, mv_a, rstd_a, "a")
            pool.wait_ge(s["mods_pe"], 1)
            V.memset(stage[:], 0.0).then_inc(s["stage_clear"], 1)
            pool.wait_ge(s["consts_in"], 16 * NCONST)
            split_hi(0, 0)

            def body(g, head, prev, prev2):
                expand_c(g)
                if prev:
                    inverse_root(g - 1, mv_b, rstd_b, "b")
                if head:
                    inverse_root(g + 1, mv_a, rstd_a, "a")
                if prev2:
                    add_shared(g - 2)
                pairs_by_b(g)
                if prev:
                    sort_rows(g - 1)

            body(0, True, False, False)
            split_lo(0, 0)
            body(1, True, True, False)
            with pool.Fori(2, G - 1) as g:
                body(g, True, True, True)
            split_hi(1, 1)
            body(G - 1, False, True, True)
            inverse_root(G - 1, mv_b, rstd_b, "b")
            split_lo(1, 1)
            add_shared(G - 2)
            sort_rows(G - 1)
            add_shared(G - 1)
            pool.wait_ge(s["plan_ready"], 1)

            def results(i):
                pool.wait_ge(s["y_out"], SHARED + 1 + i)
                apart(pool)
                for r in range(TR):
                    pool.indirect_dma_start(
                        out=result_dram, out_offset=bass.IndirectOffsetOnAxis(
                            ap=aux_d[:, 0, r:r + 1].bitcast(U32), axis=0),
                        in_=y_rows[:, r, :], in_offset=None, bounds_check=2 * TOKENS - 1,
                        oob_is_err=False).then_inc(s["results_out"], 16)

            def expert(e, buf, more):
                tiles, first = tiles_of(pool, e)
                if more:
                    pool.wait_ge(s["y_bank_done"], SHARED + first)
                    split_hi(e + 2, 1 - buf)
                    split_lo(e + 2, 1 - buf)
                with pool.Fori(0, tiles) as t:
                    results(first + t + 1)

            results(0)
            with pool.Fori(0, E // 2 - 1) as k:
                expert(2 * k, 1, True)
                expert(2 * k + 1, 0, True)
            expert(E - 2, 1, True)
            expert(E - 1, 0, False)

        @block.tensor
        def _(pe):
            def mm(out, lhsT, rhs, start=True, stop=True, **k):
                return nc.tensor.matmul(out, lhsT, rhs, start=start, stop=stop, **k)

            def turn(out, src):
                return nc.tensor.transpose(out, src, M["ident"])

            def three(out, lo, hi, w0, wn, rl, rh, start, stop):
                mm(out, lo[:, w0:w0 + wn], rh, start, False)
                mm(out, hi[:, w0:w0 + wn], rl, False, False)
                return mm(out, hi[:, w0:w0 + wn], rh, False, stop)

            def gate_up(buf, I, c, where):
                lo, hi = w_lo[buf], w_hi[buf]
                if where is NARROW:
                    if c == 0:
                        pe.wait_ge(s["y_out"], I)
                    else:
                        pe.wait_ge(s["silu_done"], I * FC + c)
                three(bank("gate", where, c), lo, hi, c * P, P, xl[:], xh[:], True, True).then_inc(s["gate_done"], 1)
                if where is NARROW and c:
                    pe.wait_ge(s["prod_done"], I * FC + c)
                three(bank("up", where, c), lo, hi, (FC + c) * P, P, xl[:], xh[:], True, True).then_inc(
                    s["up_done"], 1)

            def down(buf, c, I, where):
                pe.wait_ge(s["ah_ready"], I * FC + c + 1)
                pe.wait_ge(s["al_ready"], I * FC + c + 1)
                last = three(bank("down", where), w_lo[buf], w_hi[buf], (2 * FC + c) * P, P, al[:, c % 3, :],
                             ah[:, c % 3, :], c == 0, c == FC - 1)
                if c == FC - 1:
                    last.then_inc(s["y_bank_done"], 1)

            def turn_result(I, where):
                pe.wait_ge(s["y_sb_ready"], I + 1)
                out = bank("turn", where)
                for r in range(TR):
                    last = turn(out[:, r * P:(r + 1) * P], y_sb[:, r * P:(r + 1) * P])
                last.then_inc(s["yt_done"], 1)

            def turn_x(g, tailed):
                pe.wait_ge(s["nx_ready"], g + 1)
                if tailed:
                    pe.wait_ge(s["xl_ready"], g - 1)
                for j in range(GC):
                    last = turn(PS[:, 0, j * P:(j + 1) * P], nx_a[:, j, :])
                last.then_inc(s["nxT_done"], 1)

            def project_in(g, m, tailed):
                if m == 0 and tailed:
                    pe.wait_ge(s["lg_ready"], g - 1)
                if m < 2:
                    pe.wait_ge(s["hT_ready"], g + 1)
                else:
                    pe.wait_ge(s["tap_ready"], 2 * g + m - 1)
                mm(PS[:, (m + 1) % 2, :], w_in[:, m, :], hT[:]).then_inc(s["xz_done"], 1)

            def project_x(g):
                pe.wait_ge(s["xs_ready"], 2 * g + 2)
                for j in range(GC):
                    for h in range(2):
                        last = mm(PS[:, 2, j * XD:(j + 1) * XD], xsT[:, h, j * P:(j + 1) * P], w_x[:, h, :],
                                  h == 0, h == 1)
                last.then_inc(s["dbc_done"], 1)

            def turn_xs(g, first):
                if not first:
                    pe.wait_ge(s["y_ready"], 2 * g)
                for j in range(GC):
                    for h in range(2):
                        c0 = (j % 2) * DI + h * P
                        last = turn(PS[:, 3 + j // 2, c0:c0 + P], xsT[:, h, j * P:(j + 1) * P])
                    if j % 2:
                        last.then_inc(s["xst_done"], 1)

            def gather_c(g):
                pe.wait_ge(s["cexp_ready"], g + 1)
                pe.wait_ge(s["xst_ready"], 2 * g + 2)
                for k in range(2):
                    mm(PS[:, 3 + k, :], M["upto16"], c_exp[:, 2 * k:2 * k + 2].rearrange("p j a n -> p (j a n)")
                       ).then_inc(s["cg_done"], 1)

            def sum_spans(g):
                pe.wait_ge(s["delta_ready"], g + 1)
                out = PS[:, 2, 256:256 + 4 * GC].rearrange("p (l j) -> p l j", l=4)
                mm(out[:, 0, 0::2], M["below7"], delta[:, 0::2])
                mm(out[:, 0, 1::2], M["above7"], delta[:, 1::2])
                for k, n in enumerate(("lvl6", "lvl5", "lvl4")):
                    mm(out[:, k + 1, :], M[n], delta[:])
                mm(PS[:, 2, 320:320 + GC * BLK], M["later16"], dl_upto[:].rearrange("p j a -> p (j a)")).then_inc(
                    s["spans_done"], 1)

            def turn_factors(g):
                pe.wait_ge(s["pq_ready"], g + 1)
                pe.wait_ge(s["cg_used"], 2 * g + 2)
                for k in range(2):
                    for j in range(GC):
                        last = turn(PS[:, 3 + k, j * P:(j + 1) * P], pq[:, k, j, :])
                    last.then_inc(s["pqT_done"], 1)

            def weigh(g):
                pe.wait_ge(s["pqT_ready"], 2 * g + 2)
                for q in range(GS):
                    mm(PS[:, 2, q * P:(q + 1) * P], pqT[0:NS, 1, 2 * q, :], pqT[0:NS, 0, 2 * q + 1, :])
                for j in range(GC):
                    last = mm(PS[:, 3, j * P:(j + 1) * P], pqT[:, 1, j, :], pqT[:, 0, j, :])
                last.then_inc(s["m_done"], 1)

            def mix(g):
                pe.wait_ge(s["mT_ready"], g + 1)
                pe.wait_ge(s["mo_ready"], g + 1)
                for h in range(2):
                    for q in range(GS):
                        o = PS[:, 3 + h, q * SEQ:(q + 1) * SEQ]
                        mm(o, xs_tok[:, 2 * q, h * P:(h + 1) * P], mT[:, q, 0:2, :].rearrange("p k t -> p (k t)"))
                        last = mm(o[:, P:SEQ], xs_tok[:, 2 * q + 1, h * P:(h + 1) * P], mT[:, q, 2, :], False, True,
                                  skip_group_check=True)
                    last.then_inc(s["y_done"], 1)

            def project_out(g, more):
                pe.wait_ge(s["y_ready"], 2 * g + 2)
                if more:
                    pe.wait_ge(s["sz_ready"], 2 * g + 3)
                for j in range(GC):
                    for h in range(2):
                        last = mm(PS[:, 1, j * P:(j + 1) * P], yT[:, h, j * P:(j + 1) * P], w_out[:, h, :],
                                  h == 0, h == 1)
                last.then_inc(s["o_done"], 1)

            def turn_h2(g, more):
                pe.wait_ge(s["h2_ready"], g + 1)
                if more:
                    pe.wait_ge(s["sz_ready"], 2 * g + 4)
                for j in range(GC):
                    last = turn(PS[:, 0, j * P:(j + 1) * P], h2[:, 0, j, 0:P])
                last.then_inc(s["h2T_done"], 1)

            def route(g):
                pe.wait_ge(s["xh_ready"], g + 1)
                pe.wait_ge(s["xl_ready"], g + 1)
                for j in range(GC):
                    o = PS[:, 1, j * E:(j + 1) * E]
                    mm(o, xl[:, j * P:(j + 1) * P], gate_hi[:], True, False)
                    mm(o, xh[:, j * P:(j + 1) * P], gate_lo[:], False, False)
                    last = mm(o, xh[:, j * P:(j + 1) * P], gate_hi[:], False, True)
                last.then_inc(s["logits_done"], 1)

            def count_picks(g):
                pe.wait_ge(s["picked_ready"], g + 1)
                mm(PS[:, 7, 0:E], M["before"], ranks[:, :, GC - 1])
                mm(PS[:, 7, E:2 * E], M["ones"], ranks[:, :, GC - 1]).then_inc(s["counts_done"], 1)

            pe.wait_ge(s["c_in"], 32)
            pe.wait_ge(s["silu_c"], 1)
            mm(PS[:, 2, 0:SEQS], stage[:, 0:P], sc_t[:])
            mm(PS[:, 2, SEQS:2 * SEQS], stage[:, P:2 * P], sc_t[:])
            mm(PS[0:SEQS, 1, :], sc_t[:], stage[:, 2 * P:6 * P]).then_inc(s["mods_pe"], 1)
            pe.wait_ge(s["consts_in"], 16 * NCONST)
            turn_x(0, False)
            pe.wait_ge(s["mods_rows"], 1)
            for m in range(4):
                project_in(0, m, False)

            def step(I, c):
                if c < FC:
                    gate_up(0, I, c, NARROW)
                if c == 1:
                    pe.wait_ge(s["counts_read"], I + 1)
                if c:
                    down(0, c - 1, I, NARROW)

            def body(g, head, prev, prev2):
                if prev2:
                    step(g - 2, CUT)
                if prev:
                    project_out(g - 1, True)
                project_x(g)
                if prev2:
                    step(g - 2, CUT + 1)
                turn_xs(g, not prev)
                if prev2:
                    step(g - 2, CUT + 2)
                sum_spans(g)
                if prev2:
                    step(g - 2, CUT + 3)
                if prev:
                    turn_h2(g - 1, True)
                gather_c(g)
                if prev2:
                    step(g - 2, FC)
                if prev:
                    route(g - 1)
                if prev2:
                    turn_result(g - 2, NARROW)
                if head:
                    turn_x(g + 1, prev)
                turn_factors(g)
                if prev:
                    pe.wait_ge(s["split_done"], 1)
                    apart(pe)
                    step(g - 1, 0)
                weigh(g)
                if prev:
                    count_picks(g - 1)
                if head:
                    project_in(g + 1, 0, prev)
                    project_in(g + 1, 1, prev)
                if prev:
                    step(g - 1, 1)
                mix(g)
                if prev:
                    step(g - 1, 2)
                if head:
                    project_in(g + 1, 2, prev)
                    project_in(g + 1, 3, prev)
                if prev:
                    step(g - 1, 3)

            body(0, True, False, False)
            body(1, True, True, False)
            with pe.Fori(2, G - 1) as g:
                body(g, True, True, True)
            body(G - 1, False, True, True)
            project_out(G - 1, False)
            for c in range(CUT, FC + 1):
                step(G - 2, c)
            turn_h2(G - 1, False)
            turn_result(G - 2, NARROW)
            route(G - 1)
            for c in range(FC + 2):
                if c == 1:
                    pe.wait_ge(s["lg_ready"], G)
                if c == 2:
                    count_picks(G - 1)
                if c < FC:
                    gate_up(0, G - 1, c, WIDE)
                if c >= 2:
                    down(0, c - 2, G - 1, WIDE)
            pe.wait_ge(s["counts_read"], G)
            turn_result(G - 1, WIDE)

            def turn_tile(i):
                pe.wait_ge(s["tile_in"], 16 * (i + 1))
                for r in range(TR):
                    last = turn(PS[:, 7, r * P:(r + 1) * P], xin[:, r, 0:P])
                last.then_inc(s["xt_done"], 1)

            pe.wait_ge(s["plan_ready"], 1)
            pe.wait_ge(s["y_out"], SHARED)
            turn_tile(0)

            def tile_body(buf, i):
                I = SHARED + i
                pe.wait_ge(s["rh_ready"], i + 1)
                pe.wait_ge(s["rl_ready"], i + 1)
                for c in range(FC):
                    gate_up(buf, I, c, WIDE)
                    if c == 0:
                        turn_result(I - 1, WIDE)
                    if c >= 2:
                        down(buf, c - 2, I, WIDE)
                pe.wait_ge(s["y_out"], I + 1)
                turn_tile(i + 1)
                down(buf, FC - 2, I, WIDE)
                down(buf, FC - 1, I, WIDE)

            def expert(e, buf):
                tiles, first = tiles_of(pe, e)
                pe.wait_ge(s["split_done"], e + 2)
                apart(pe)
                with pe.Fori(0, tiles) as t:
                    tile_body(buf, first + t)
                return first + tiles

            with pe.Fori(0, E // 2 - 1) as k:
                expert(2 * k, 1)
                expert(2 * k + 1, 0)
            expert(E - 2, 1)
            count = expert(E - 1, 0)
            pe.wait_ge(s["rl_ready"], count + 1)
            turn_result(SHARED + count - 1, WIDE)

        @block.scalar
        def _(act):
            A = nc.scalar

            def silu(I, c, where):
                act.wait_ge(s["gate_done"], I * FC + c + 1)
                A.activation(sg[:, c % 3, :], bank("gate", where, c), ACT.Silu).then_inc(s["silu_done"], 1)

            def high(I, c):
                act.wait_ge(s["prod_done"], I * FC + c + 1)
                A.copy(ah[:, c % 3, :], prod[:, c % 3, :]).then_inc(s["ah_ready"], 1)

            def keep_result(I, where):
                act.wait_ge(s["y_bank_done"], I + 1)
                A.copy(y_sb[:], bank("down", where)).then_inc(s["y_sb_ready"], 1)

            def modulate(g):
                act.wait_ge(s["nxT_done"], g + 1)
                for q in range(GS):
                    last = A.activation(hT[:, q * SEQ:(q + 1) * SEQ], PS[:, 0, q * SEQ:(q + 1) * SEQ],
                                        ACT.Identity, bias=shift_a[:, bass.ds(g * GS + q, 1)],
                                        scale=scale_a[:, bass.ds(g * GS + q, 1)])
                last.then_inc(s["hT_ready"], 1)

            def last_tap(g, h):
                act.wait_ge(s["xz_done"], 4 * g + h + 1)
                src = PS[:, (h + 1) % 2, :]
                A.copy(xcp[:, h, :, TAPS - 1:], src.rearrange("p (q t) -> p q t", q=GS))
                A.activation(acc[:, h, :], src, ACT.Identity, bias=cols[:, h, TAPS:TAPS + 1],
                             scale=cols[:, h, TAPS - 1:TAPS]).then_inc(s["tap_ready"], 1)

            def silu_z(g, h, first):
                act.wait_ge(s["xz_done"], 4 * g + h + 3)
                if not first:
                    act.wait_ge(s["y_ready"], 2 * g)
                A.activation(sz[:, h, :], PS[:, (h + 1) % 2, :], ACT.Silu).then_inc(s["sz_ready"], 1)

            def silu_x(g, h):
                act.wait_ge(s["conv_done"], 2 * g + h + 1)
                A.activation(xsT[:, h, :], acc[:, h, :], ACT.Silu).then_inc(s["xs_ready"], 1)

            def softplus(g):
                act.wait_ge(s["nabs_ready"], g + 1)
                A.activation(sp1[:], sp0[:], ACT.Exp).then_inc(s["exp1_done"], 1)
                act.wait_ge(s["exp1_done"], g + 1)
                A.activation(sp2[:], sp1[:], ACT.Ln, bias=1.0).then_inc(s["soft_ready"], 1)

            def keep_xs(g):
                for k in range(2):
                    act.wait_ge(s["xst_done"], 2 * g + k + 1)
                    A.copy(xs_tok[:, 2 * k:2 * k + 2, :].rearrange("p j d -> p (j d)"), PS[:, 3 + k, :]).then_inc(
                        s["xst_ready"], 1)

            def decays(g):
                act.wait_ge(s["levels_in"], g + 1)
                A.activation(lev[:], lev[:], ACT.Exp).then_inc(s["levels_exp"], 1)
                for k in range(2):
                    act.wait_ge(s["pairs_in"], 2 * g + k + 1)
                    v = pair[:, 2 * k:2 * k + 2].rearrange("p j a n -> p (j a n)")
                    A.activation(v, v, ACT.Exp).then_inc(s["pairs_exp"], 1)

            def keep_factors(g):
                for k in range(2):
                    act.wait_ge(s["pqT_done"], 2 * g + k + 1)
                    A.copy(pqT[:, k].rearrange("p j t -> p (j t)"), PS[:, 3 + k, :]).then_inc(s["pqT_ready"], 1)

            def keep_next(g):
                act.wait_ge(s["m_done"], g + 1)
                A.copy(mT[:, :, 1, :], PS[:, 2, 0:GS * P].rearrange("p (q t) -> p q t", q=GS)).then_inc(
                    s["mo_ready"], 1)

            def keep_h2(g, first):
                act.wait_ge(s["h2T_done"], g + 1)
                if not first:
                    act.wait_ge(s["up_done"], FC * g)
                A.copy(xh[:], PS[:, 0, :]).then_inc(s["xh_ready"], 1)
                A.copy(h2[:, 1, :, 0:P], h2[:, 0, :, 0:P]).then_inc(s["h2_both"], 1)

            def router_exp(g):
                act.wait_ge(s["soft_in"], g + 1)
                A.activation(ex[:], ex[:], ACT.Exp).then_inc(s["soft_out"], 1)

            act.wait_ge(s["c_in"], 32)
            A.activation(sc_t[:], c_t[:], ACT.Silu).then_inc(s["silu_c"], 1)
            act.wait_ge(s["consts_in"], 16 * NCONST)
            act.wait_ge(s["mods_rows"], 1)
            modulate(0)
            last_tap(0, 0)
            last_tap(0, 1)
            silu_z(0, 0, True)
            silu_z(0, 1, True)
            silu_x(0, 0)
            silu_x(0, 1)
            A.activation(a_neg[:], a_log[:], ACT.Exp).then_inc(s["a_neg_ready"], 1)

            def step(I, c):
                silu(I, c, NARROW)
                high(I, c)

            def body(g, head, prev, prev2, first):
                if not first:
                    silu_z(g, 0, first)
                    silu_z(g, 1, first)
                    silu_x(g, 0)
                    silu_x(g, 1)
                if prev2:
                    step(g - 2, CUT)
                    step(g - 2, CUT + 1)
                keep_xs(g)
                softplus(g)
                if prev2:
                    step(g - 2, CUT + 2)
                decays(g)
                if prev2:
                    step(g - 2, CUT + 3)
                if prev:
                    keep_h2(g - 1, not prev2)
                if prev2:
                    keep_result(g - 2, NARROW)
                if prev:
                    router_exp(g - 1)
                if head:
                    modulate(g + 1)
                keep_factors(g)
                if prev:
                    step(g - 1, 0)
                keep_next(g)
                if head:
                    last_tap(g + 1, 0)
                    last_tap(g + 1, 1)
                if prev:
                    step(g - 1, 1)
                    step(g - 1, 2)
                    step(g - 1, 3)

            body(0, True, False, False, True)
            body(1, True, True, False, False)
            with act.Fori(2, G - 1) as g:
                body(g, True, True, True, False)
            body(G - 1, False, True, True, False)
            for c in range(CUT, FC):
                step(G - 2, c)
            keep_h2(G - 1, False)
            keep_result(G - 2, NARROW)
            for c in range(FC):
                if c == 2:
                    router_exp(G - 1)
                silu(G - 1, c, WIDE)
                high(G - 1, c)
            keep_result(G - 1, WIDE)

            act.wait_ge(s["plan_ready"], 1)

            def split_tile(i):
                act.wait_ge(s["xt_done"], i + 1)
                A.copy(xh[:], PS[:, 7, :]).then_inc(s["rh_ready"], 1)

            split_tile(0)
            with act.Fori(0, E) as e:
                tiles, first = tiles_of(act, e)
                with act.Fori(0, tiles) as t:
                    i = first + t
                    for c in range(FC):
                        silu(SHARED + i, c, WIDE)
                        high(SHARED + i, c)
                    split_tile(i + 1)
                    keep_result(SHARED + i, WIDE)

        @block.vector
        def _(dve):
            V = nc.vector
            PER_BODY = 40
            chain = {"base": 0, "n": 0}

            def link(ins):
                ins.then_inc(s["dve_chain"], 1)
                chain["n"] += 1
                dve.wait_ge(s["dve_chain"], chain["base"] + chain["n"])

            def bc(ap, shape):
                return ap.to_broadcast(shape)

            def by_seq(ap):
                return ap.rearrange("p (q k) d -> p q k d", k=2)

            def chunk(g):
                return lambda j: X[:, bass.ds(g * GC + j, 1), :].rearrange("p o d -> p (o d)")

            def moments(src, stats, mv, done):
                apart(dve)
                for j in range(GC):
                    last = V.bn_stats(stats[:, j, :], src(j))
                link(last)
                apart(dve)
                for j in range(GC):
                    last = V.bn_aggr(mv[:, j, :], stats[:, j, :])
                last.then_inc(done, 1)

            def norm(src, mv, rstd, out):
                for j in range(GC):
                    last = V.tensor_scalar(out[:, j, :], src(j), mv[:, j, 0:1], rstd[:, j:j + 1],
                                           ALU.subtract, ALU.mult)
                return last

            def product(I, c, where):
                dve.wait_ge(s["silu_done"], I * FC + c + 1)
                dve.wait_ge(s["up_done"], I * FC + c + 1)
                V.tensor_tensor(prod[:, c % 3, :], bank("up", where, c), sg[:, c % 3, :], ALU.mult).then_inc(
                    s["prod_done"], 1)

            def low(I, c):
                dve.wait_ge(s["ah_ready"], I * FC + c + 1)
                V.tensor_tensor(al[:, c % 3, :], prod[:, c % 3, :], ah[:, c % 3, :].bitcast(F32),
                                ALU.subtract).then_inc(s["al_ready"], 1)

            def head_moments(g):
                moments(chunk(g), stats_a, mv_a, s["var_a"])

            def head_norm(g):
                dve.wait_ge(s["rstd_a"], g + 1)
                norm(chunk(g), mv_a, rstd_a, nx_a).then_inc(s["nx_ready"], 1)

            def conv(g, h):
                dve.wait_ge(s["tap_ready"], 2 * g + h + 1)
                o = acc[:, h, :].rearrange("p (q t) -> p q t", q=GS)
                for k in range(TAPS - 1):
                    last = V.scalar_tensor_tensor(o, xcp[:, h, :, k:k + SEQ], cols[:, h, k:k + 1], o,
                                                  ALU.mult, ALU.add)
                    if k < TAPS - 2:
                        link(last)
                last.then_inc(s["conv_done"], 1)

            Bp, Cp = dbc[:, :, 1:1 + NS], dbc[:, :, 1 + NS:XD]
            lv = [P, GC, 4, NS]

            def take_dbc(g):
                dve.wait_ge(s["dbc_done"], g + 1)
                V.tensor_copy(dbc[:].rearrange("p j n -> p (j n)"), PS[:, 2, 0:GC * XD]).then_inc(s["dbc_ready"], 1)
                dve.wait_ge(s["dbc_ready"], g + 1)
                V.scalar_tensor_tensor(sp0[:], dbc[:, :, 0], -1.0, dbc[:, :, 0], ALU.mult, ALU.min).then_inc(
                    s["nabs_ready"], 1)

            def make_delta(g):
                dve.wait_ge(s["soft_ready"], g + 1)
                link(V.scalar_tensor_tensor(delta[:], dbc[:, :, 0], 0.0, sp2[:], ALU.max, ALU.add))
                V.tensor_tensor(dl_upto[:], bc(delta[:].unsqueeze(2), [P, GC, BLK]),
                                bc(S["upto"].unsqueeze(1), [P, GC, BLK]), ALU.mult).then_inc(s["delta_ready"], 1)
                link(V.tensor_tensor(dB[:], bc(delta[:].unsqueeze(2), [P, GC, NS]), Bp, ALU.mult))

            def exponents(g):
                dve.wait_ge(s["spans_done"], g + 1)
                spans = PS[:, 2, 256:256 + 4 * GC].rearrange("p (l j) -> p j l", l=4)
                V.tensor_tensor(lev[:], bc(spans.unsqueeze(3), lv), bc(a_neg[:].unsqueeze(1).unsqueeze(1), lv),
                                ALU.mult).then_inc(s["levels_in"], 1)
                within = PS[:, 2, 320:320 + GC * BLK].rearrange("p (j a) -> p j a", j=GC)
                half = [P, GC // 2, BLK, NS]
                for k in range(2):
                    j0, j1 = k * GC // 2, (k + 1) * GC // 2
                    V.tensor_tensor(pair[:, j0:j1], bc(within[:, j0:j1].unsqueeze(3), half),
                                    bc(a_neg[:].unsqueeze(1).unsqueeze(1), half), ALU.mult).then_inc(
                        s["pairs_in"], 1)

            def factors(g):
                dve.wait_ge(s["levels_exp"], g + 1)
                V.tensor_tensor(lev_c[:], lev[:], bc(Cp.unsqueeze(2), lv), ALU.mult)
                link(V.tensor_tensor(lev_b[:], lev[:], bc(dB[:].unsqueeze(2), lv), ALU.mult))
                for k, (src, role) in enumerate(((lev_c, "upper"), (lev_b, "lower"))):
                    pv = pq[:, k].rearrange("p j (b n) -> p j b n", n=NS)
                    role7 = S[role][:, 0:2].unsqueeze(1).unsqueeze(3)
                    V.tensor_tensor(pv[:, :, 0, :].rearrange("p (q k) n -> p q k n", k=2),
                                    src[:, :, 0, :].rearrange("p (q k) n -> p q k n", k=2),
                                    bc(role7, [P, GS, 2, NS]), ALU.mult)
                    b0 = 1
                    for l in range(1, 4):
                        nb = 1 << (l - 1)
                        sh = [P, GC, nb, NS]
                        last = V.tensor_tensor(pv[:, :, b0:b0 + nb, :], bc(src[:, :, l, :].unsqueeze(2), sh),
                                               bc(S[role][:, b0 + 1:b0 + 1 + nb].unsqueeze(1).unsqueeze(3), sh),
                                               ALU.mult)
                        b0 += nb
                last.then_inc(s["pq_ready"], 1)

            def pairs_by_c(g):
                for k in range(2):
                    dve.wait_ge(s["pairs_exp"], 2 * g + k + 1)
                    dve.wait_ge(s["cg_done"], 2 * g + k + 1)
                    v = pair[:, 2 * k:2 * k + 2].rearrange("p j a n -> p (j a n)")
                    V.tensor_tensor(v, v, PS[:, 3 + k, :], ALU.mult).then_inc(s["cg_used"], 1)

            def sum_pairs(g):
                dve.wait_ge(s["pairs_ready"], 2 * g + 2)
                link(V.tensor_reduce(wd[:], pair[:], AX.X, ALU.add))
                sh = [P, GC, NB, BLK]
                V.tensor_tensor(diag[:].rearrange("p j (b a) -> p j b a", a=BLK), bc(wd[:].unsqueeze(2), sh),
                                bc(S["block"].unsqueeze(1).unsqueeze(3), sh), ALU.mult).then_inc(s["dve_chain"], 1)
                chain["n"] += 1

            def add_pairs(g):
                dve.wait_ge(s["dve_chain"], chain["base"] + chain["n"])
                dve.wait_ge(s["m_done"], g + 1)
                V.tensor_tensor(mT[:, :, 0:3:2, :], PS[:, 3, :].rearrange("p (q k t) -> p q k t", q=GS, k=2),
                                by_seq(diag[:]), ALU.add).then_inc(s["mT_ready"], 1)

            def gate_y(g, h):
                dve.wait_ge(s["y_done"], 2 * g + h + 1)
                link(V.scalar_tensor_tensor(yT[:, h, :], xsT[:, h, :], cols[:, h, TAPS + 1:TAPS + 2],
                                            PS[:, 3 + h, :], ALU.mult, ALU.add))
                V.tensor_tensor(yT[:, h, :], yT[:, h, :], sz[:, h, :], ALU.mult).then_inc(s["y_ready"], 1)

            def residual(g):
                dve.wait_ge(s["o_done"], g + 1)
                dve.wait_ge(s["tab_in"], 16 * (g + 1))
                seq = [P, GS, 2, P]
                xg = X[:, bass.ds(g * GC, GC), :]
                link(V.tensor_tensor(by_seq(nx_b[:]), PS[:, 1, :].rearrange("p (q k d) -> p q k d", q=GS, k=2),
                                     bc(tab[:, :, 0:1, :], seq), ALU.mult))
                link(V.tensor_tensor(xg, xg, nx_b[:], ALU.add))
                moments(chunk(g), stats_b, mv_b, s["var_b"])

            def second_norm(g, first):
                seq = [P, GS, 2, P]
                dve.wait_ge(s["rstd_b"], g + 1)
                link(norm(chunk(g), mv_b, rstd_b, nx_b))
                link(V.tensor_tensor(by_seq(nx_b[:]), by_seq(nx_b[:]), bc(tab[:, :, 2:3, :], seq), ALU.mult))
                if not first:
                    dve.wait_ge(s["sorted_out"], 16 * 2 * GC * g)
                V.tensor_tensor(by_seq(h2[:, 0, :, 0:P]), by_seq(nx_b[:]), bc(tab[:, :, 1:2, :], seq),
                                ALU.add).then_inc(s["h2_ready"], 1)
                dve.wait_ge(s["h2_ready"], g + 1)
                apart(dve)
                V.engine_nop().then_inc(s["tab_free"], 1)

            def low_x(g):
                dve.wait_ge(s["xh_ready"], g + 1)
                V.tensor_tensor(xl[:], PS[:, 0, :], xh[:].bitcast(F32), ALU.subtract).then_inc(s["xl_ready"], 1)

            def take_logits(g):
                dve.wait_ge(s["logits_done"], g + 1)
                V.tensor_copy(lg[:].rearrange("p j e -> p (j e)"), PS[:, 1, 0:GC * E]).then_inc(s["lg_ready"], 1)
                dve.wait_ge(s["lg_ready"], g + 1)

            ge = [P, GC, E]

            def pick(g):
                rev = bc(S["rev"].unsqueeze(1), ge)
                for k in range(2):
                    src = lg if k == 0 else r2
                    link(V.tensor_reduce(top[:, k, :], src[:], AX.X, ALU.max))
                    if k == 0:
                        V.tensor_tensor(ex[:], lg[:], bc(top[:, 0, :].unsqueeze(2), ge), ALU.subtract).then_inc(
                            s["soft_in"], 1)
                    link(V.tensor_tensor(r1[:], src[:], bc(top[:, k, :].unsqueeze(2), ge), ALU.is_equal))
                    link(V.tensor_tensor(r1[:], r1[:], rev, ALU.mult))
                    link(V.tensor_reduce(top[:, 2, :], r1[:], AX.X, ALU.max))
                    link(V.tensor_tensor(oh[:, k], r1[:], bc(top[:, 2, :].unsqueeze(2), ge), ALU.is_equal))
                    if k == 0:
                        link(V.scalar_tensor_tensor(r2[:], oh[:, 0], -3.0e38, lg[:], ALU.mult, ALU.add))
                link(V.tensor_tensor(picked[:].rearrange("p e j -> p j e"), oh[:, 0], oh[:, 1], ALU.add))
                V.tensor_tensor_scan(ranks[:].rearrange("p e j -> p (e j)"), S["seg"],
                                     picked[:].rearrange("p e j -> p (e j)"), 0.0, ALU.mult, ALU.add).then_inc(
                    s["picked_ready"], 1)

            def weights(g):
                dve.wait_ge(s["soft_out"], g + 1)
                link(V.tensor_reduce(top[:, 3, :], ex[:], AX.X, ALU.add))
                V.reciprocal(top[:, 4, :], top[:, 3, :])
                link(V.tensor_tensor(r1[:], ex[:], oh[:, 1], ALU.mult))
                link(V.tensor_reduce(top[:, 5, :], r1[:], AX.X, ALU.add))
                link(V.tensor_tensor(top[:, 5, :], top[:, 5, :], top[:, 4, :], ALU.mult))
                link(V.scalar_tensor_tensor(top[:, 6, :], top[:, 4, :], 1e-8, top[:, 5, :], ALU.add, ALU.add))
                link(V.reciprocal(top[:, 7, :], top[:, 6, :]))

            def place(g):
                dve.wait_ge(s["counts_done"], g + 1)
                dve.wait_ge(s["picked_ready"], g + 1)
                link(V.tensor_tensor(base2[:], base[:], PS[:, 7, 0:E], ALU.add))
                V.tensor_tensor(base[:], base[:], PS[:, 7, E:2 * E], ALU.add).then_inc(s["counts_read"], 1)
                link(V.tensor_tensor(ranks[:], ranks[:], picked[:], ALU.subtract))
                link(V.tensor_tensor(ranks[:], ranks[:], bc(base2[:].unsqueeze(2), [P, E, GC]), ALU.add))
                dve.wait_ge(s["h2_both"], g + 1)
                for k in range(2):
                    V.tensor_tensor(h2[:, k, :, P], top[:, 4 + k, :], top[:, 7, :], ALU.mult)
                    V.tensor_copy(h2[:, k, :, P + 1].bitcast(I32),
                                  token2[:, bass.ds(g * GC, GC), k:k + 1].rearrange("p j o -> p (j o)"))
                    last = V.tensor_tensor(oh[:, k], oh[:, k], ranks[:].rearrange("p e j -> p j e"), ALU.mult)
                link(last)
                link(V.tensor_reduce(top[:, 8:10, :], oh[:], AX.X, ALU.add))
                V.tensor_copy(slot[:], top[:, 8:10, :]).then_inc(s["rows_ready"], 1)

            def gate_shared(g, where):
                dve.wait_ge(s["yt_done"], g + 1)
                dve.wait_ge(s["tab_g_in"], 16 * (g + 1))
                dve.wait_ge(s["gated_free"], g + 1)
                seq = [P, GS, 2, P]
                V.tensor_tensor(gated[:].rearrange("p (q k d) -> p q k d", q=GS, k=2),
                                bank("turn", where).rearrange("p (q k d) -> p q k d", q=GS, k=2),
                                bc(tab_g[:].unsqueeze(2), seq), ALU.mult).then_inc(s["y_out"], 1)
                dve.wait_ge(s["y_out"], g + 1)
                apart(dve)
                V.engine_nop().then_inc(s["tab_g_free"], 1)

            dve.wait_ge(s["x_in"], 16)
            head_moments(0)
            dve.wait_ge(s["mods_pe"], 1)
            V.tensor_copy(shift_a[:], PS[:, 2, 0:SEQS])
            V.tensor_scalar_add(scale_a[:], PS[:, 2, SEQS:2 * SEQS], 1.0)
            rows = PS[0:SEQS, 1, :].rearrange("p (m d) -> p m d", m=4)
            V.tensor_copy(mod_rows[:, 1, :], rows[:, 1, :])
            V.tensor_scalar_add(mod_rows[:, 2, :], rows[:, 2, :], 1.0)
            V.tensor_copy(mod_rows[:, 0, :], rows[:, 0, :])
            link(V.tensor_copy(mod_rows[:, 3, :], rows[:, 3, :]))
            for k, m in enumerate((0, 3)):
                V.tensor_scalar(mod_tmp[:, k, :], mod_rows[:, m, :], 0.0, 2.0, ALU.is_ge, ALU.mult)
                link(V.scalar_tensor_tensor(mod_rows[:, m, :], mod_rows[:, m, :], -1.0, mod_rows[:, m, :],
                                            ALU.mult, ALU.max))
            link(V.tensor_scalar_add(mod_tmp[:], mod_tmp[:], -1.0))
            for k, m in enumerate((0, 3)):
                last = V.scalar_tensor_tensor(mod_rows[:, m, :], mod_rows[:, m, :], 0.25, mod_tmp[:, k, :],
                                              ALU.max, ALU.mult)
            last.then_inc(s["mods_rows"], 1)
            head_norm(0)
            dve.wait_ge(s["consts_in"], 16 * NCONST)
            V.tensor_copy(base[:], S["region"])
            link(V.tensor_copy(gate_hi[:], gate_w[:]))
            link(V.tensor_tensor(gate_lo[:], gate_w[:], gate_hi[:].bitcast(F32), ALU.subtract))
            V.memset(aux_w[:], 0.0)
            link(V.memset(aux_d[:], NOWHERE))
            dve.wait_ge(s["setup_mem"], 2)
            conv(0, 0)
            conv(0, 1)
            dve.wait_ge(s["a_neg_ready"], 1)
            link(V.tensor_scalar_mul(a_neg[:], a_neg[:], -1.0))
            dve.wait_ge(s["x_in"], 32)

            def step(I, c):
                product(I, c, NARROW)
                low(I, c)

            def body(g, head, prev, prev2):
                if prev2:
                    step(g - 2, CUT)
                take_dbc(g)
                if prev:
                    residual(g - 1)
                if prev2:
                    step(g - 2, CUT + 1)
                make_delta(g)
                if prev:
                    second_norm(g - 1, not prev2)
                exponents(g)
                if prev2:
                    step(g - 2, CUT + 2)
                factors(g)
                if prev2:
                    step(g - 2, CUT + 3)
                if prev:
                    low_x(g - 1)
                if head:
                    head_moments(g + 1)
                pairs_by_c(g)
                if prev2:
                    gate_shared(g - 2, NARROW)
                if head:
                    head_norm(g + 1)
                if prev:
                    take_logits(g - 1)
                    pick(g - 1)
                    step(g - 1, 0)
                sum_pairs(g)
                add_pairs(g)
                if prev:
                    weights(g - 1)
                    place(g - 1)
                if head:
                    conv(g + 1, 0)
                if prev:
                    step(g - 1, 1)
                if head:
                    conv(g + 1, 1)
                if prev:
                    step(g - 1, 2)
                gate_y(g, 0)
                gate_y(g, 1)
                if prev:
                    step(g - 1, 3)

            body(0, True, False, False)
            body(1, True, True, False)
            before = chain["n"]
            with dve.Fori(2, G - 1) as g:
                chain["base"], chain["n"] = (g - 2) * PER_BODY + before, 0
                body(g, True, True, True)
                assert chain["n"] == PER_BODY, chain["n"]
            chain["base"], chain["n"] = (G - 3) * PER_BODY + before, 0
            body(G - 1, False, True, True)
            residual(G - 1)
            step(G - 2, CUT)
            second_norm(G - 1, False)
            for c in range(CUT + 1, FC):
                step(G - 2, c)
            low_x(G - 1)
            gate_shared(G - 2, NARROW)
            take_logits(G - 1)
            g = G - 1
            pick(g)
            for c in range(2):
                product(g, c, WIDE)
                low(g, c)
            weights(g)
            place(g)
            dve.wait_ge(s["counts_read"], G)
            link(V.tensor_tensor(plan_f[:, 3, :], base[:], S["region"], ALU.subtract))
            link(V.tensor_tensor(cmp[:], bc(plan_f[:, 3, :].unsqueeze(2), [P, E, E]),
                                 bc(S["many"].unsqueeze(1), [P, E, E]), ALU.is_gt))
            link(V.tensor_reduce(plan_f[:, 0, :], cmp[:], AX.X, ALU.add))
            link(V.tensor_scalar(plan_f[:, 0, :], plan_f[:, 0, :], 1.0, None, ALU.max))
            link(V.tensor_tensor_scan(plan_f[:, 1, :], M["ones"][:, 0:E], plan_f[:, 0, :], 0.0, ALU.mult, ALU.add))
            link(V.tensor_tensor(plan_f[:, 1, :], plan_f[:, 1, :], plan_f[:, 0, :], ALU.subtract))
            V.tensor_copy(plan[:, 2, :], base[:])
            V.tensor_copy(plan[:, 0:2, :], plan_f[:, 0:2, :]).then_inc(s["plan_ready"], 1)
            V.engine_nop().then_inc(s["aux_read"], 1)
            for c in range(2, FC):
                product(g, c, WIDE)
                low(g, c)
            gate_shared(g, WIDE)

            def take_tile(i):
                dve.wait_ge(s["rh_ready"], i + 1)
                V.tensor_tensor(xl[:], PS[:, 7, :], xh[:].bitcast(F32), ALU.subtract).then_inc(s["rl_ready"], 1)
                V.tensor_copy(aux_w[:, 1, :], xin[:, :, P])
                V.tensor_copy(aux_d[:, 1, :], xin[:, :, P + 1].bitcast(I32)).then_inc(s["aux_read"], 1)

            dve.wait_ge(s["plan_ready"], 1)
            take_tile(0)

            def give_rows(i):
                dve.wait_ge(s["yt_done"], SHARED + 1 + i)
                V.tensor_tensor(y_rows[:], PS[:, 7, :].rearrange("p (r d) -> p r d", r=TR),
                                bc(aux_w[:, 0, :].unsqueeze(2), [P, TR, P]), ALU.mult).then_inc(s["y_out"], 1)

            with dve.Fori(0, E) as e:
                tiles, first = tiles_of(dve, e)
                with dve.Fori(0, tiles) as t:
                    i = first + t
                    for c in range(FC):
                        product(SHARED + i, c, WIDE)
                        if c == 0:
                            give_rows(i)
                        low(SHARED + i, c)
                    dve.wait_ge(s["rh_ready"], i + 2)
                    dve.wait_ge(s["results_out"], 64 * (i + 1))
                    dve.wait_ge(s["aux_read"], i + 2)
                    V.tensor_copy(aux_w[:, 0, :], aux_w[:, 1, :])
                    V.tensor_copy(aux_d[:, 0, :], aux_d[:, 1, :]).then_inc(s["aux_moved"], 1)
                    dve.wait_ge(s["aux_moved"], i + 1)
                    take_tile(i + 1)
            last_tiles, last_first = tiles_of(dve, E - 1)
            give_rows(last_first + last_tiles)
            dve.wait_ge(s["gb_in"], 16)
            for g in range(G):
                dve.wait_ge(s[f"final_in{g % 2}"], 16 * (g // 2 + 1))
                f = fin[g % 2]
                link(V.tensor_tensor(f[:, :, 0, :], f[:, :, 0, :], f[:, :, 1, :], ALU.add))
                f0 = by_seq(f[:, :, 0, :])
                link(V.tensor_tensor(f0, f0, bc(gb_all[:, g * GS:(g + 1) * GS, :].unsqueeze(2), [P, GS, 2, P]),
                                     ALU.mult))
                xg = X[:, g * GC:(g + 1) * GC, :]
                V.tensor_tensor(xg, xg, f[:, :, 0, :], ALU.add).then_inc(s["final_ready"], 1)


def kernel(L0_attn_x, L0_attn_W_in, L0_attn_conv_w, L0_attn_conv_b, L0_attn_W_x, L0_attn_A_log, L0_attn_D,
           L0_attn_W_out, L0_ffn_gate_weight, L0_ffn_shared_gate_up, L0_ffn_shared_down,
           L0_ffn_experts_gate_up, L0_ffn_experts_down, L0_c, L0_wmod):
    import concourse.bacc as bacc
    from concourse.bass_utils import run_bass_kernel_spmd

    n = np.asarray
    big, small, token = constants()
    arrays = {
        "x": n(L0_attn_x).reshape(TOKENS, P),
        "L0_attn_W_in": n(L0_attn_W_in),
        "L0_attn_W_out": n(L0_attn_W_out),
        "L0_attn_W_x": n(L0_attn_W_x),
        "a_log": n(L0_attn_A_log).reshape(1, NS),
        "cols": np.concatenate([n(L0_attn_conv_w).reshape(DI, TAPS), n(L0_attn_conv_b)[:, None],
                                n(L0_attn_D)[:, None]], 1),
        "gate_t": n(L0_ffn_gate_weight).T,
        "c_t": n(L0_c).T,
        "L0_wmod": n(L0_wmod),
        "w_gu": np.concatenate([n(L0_ffn_shared_gate_up)[None], n(L0_ffn_experts_gate_up)], 0).transpose(0, 2, 1),
        "w_dn": np.concatenate([n(L0_ffn_shared_down)[None], n(L0_ffn_experts_down)], 0).transpose(0, 2, 1),
        "big": big, "small": small, "token": token,
    }
    arrays = {k: np.ascontiguousarray(v) for k, v in arrays.items()}
    nc = bacc.Bacc("TRN2", target_bir_lowering=False, num_devices=1)
    aps = {k: nc.dram_tensor("in_" + k, v.shape, mybir.dt.from_np(v.dtype), kind="ExternalInput").ap()
           for k, v in arrays.items()}
    aps["out"] = nc.dram_tensor("out", (TOKENS, P), F32, kind="ExternalOutput").ap()
    adaln_block(nc, aps)
    r = run_bass_kernel_spmd(nc, [{"in_" + k: v for k, v in arrays.items()}], core_ids=[0])
    return r.results[0]["out"].reshape(SEQS, SEQ, P)
```

```python
from contextlib import ExitStack

import numpy as np
import concourse.bass as bass
from concourse import mybir

F32 = mybir.dt.float32
F32R = mybir.dt.float32r
I32 = mybir.dt.int32
U32 = mybir.dt.uint32
ALU = mybir.AluOpType
ACT = mybir.ActivationFunctionType
AX = mybir.AxisListType

P = 128
SEQS = 16
SEQ = 256
TOKENS = SEQS * SEQ
CH = TOKENS // P
G = 8
GC = CH // G
GS = SEQS // G
GT = GC * P
DI = 2 * P
NS = 16
XD = 2 * NS + 1
TAPS = 4
BLK = 16
NB = P // BLK
LEVELS = (128, 64, 32, 16)
E = 8
FF = 938
FC = 8
FL = FF - (FC - 1) * P
WC = 3 * FC * P
TILE = 512
TR = TILE // P
REGION = TOKENS + TILE
ROW = P + 2
NOWHERE = 4 * TOKENS
SHARED = TOKENS // TILE
EPS = 1e-5

CONST = ("ident", "below7", "above7", "lvl6", "lvl5", "lvl4", "later16", "upto16", "before", "ones")


def constants():
    u = np.arange(P)[:, None]
    t = np.arange(P)[None, :]
    same = u // BLK == t // BLK

    def span(half):
        mid = t // (2 * half) * (2 * half) + half
        return np.where(t >= mid, (u >= mid) & (u <= t), (u > t) & (u < mid))

    mats = [u == t, u > t, u <= t, span(64), span(32), span(16), same & (u > t), same & (u >= t), u < t, u >= 0]
    tau = np.arange(BLK)[None, :]
    upto = u % BLK <= tau
    equal = u % BLK == tau
    block = u // BLK == np.arange(NB)[None, :]
    roles = []
    for want in (1, 0):
        cols = [np.full((P, 1), par == want) for par in (0, 1)]
        for half in LEVELS[1:]:
            for b in range(P // (2 * half)):
                cols.append((u // (2 * half) == b) & ((u // half) % 2 == want))
        roles.append(np.concatenate(cols, 1))
    expert = np.arange(E)[None, :] + 0 * u
    seg = np.tile(np.arange(GC) > 0, E)[None, :] & (u >= 0)
    many = np.arange(E)[None, :] * TILE + 0 * u
    small = np.concatenate([upto, equal, block, *roles, seg, E - expert, expert * REGION, many], 1)
    big = np.concatenate([np.broadcast_to(m, (P, P)) for m in mats], 1)
    token = (np.arange(CH)[None, :, None] * P + np.arange(P)[:, None, None]) * 2 + np.arange(2)[None, None, :]
    return (np.ascontiguousarray(big, np.float32), np.ascontiguousarray(small, np.float32),
            np.ascontiguousarray(token, np.int32))


SMALL = {}
_at = 0
for _name, _n in (("upto", BLK), ("equal", BLK), ("block", NB), ("upper", 9), ("lower", 9), ("seg", E * GC),
                  ("rev", E), ("region", E), ("many", E)):
    SMALL[_name] = (_at, _n)
    _at += _n
NSMALL = _at
NCONST = 9


def adaln_block(nc, a):
    ctx = ExitStack()
    with ctx:
        def sb(name, shape, dt=F32):
            return ctx.enter_context(nc.sbuf_tensor(name, shape, dt))

        def sem(name):
            return ctx.enter_context(nc.semaphore(name))

        mods_dram = nc.dram_tensor("mods_dram", (SEQS, 4, P), F32, kind="Internal").ap()
        sorted_dram = nc.dram_tensor("sorted_dram", (E * REGION, ROW), F32, kind="Internal").ap()
        result_dram = nc.dram_tensor("result_dram", (2 * TOKENS, P), F32, kind="Internal").ap()

        mats = sb("mats", [P, len(CONST), P])
        M = {n: mats[:, i, :] for i, n in enumerate(CONST)}
        small = sb("small", [P, NSMALL])
        S = {n: small[:, o:o + k] for n, (o, k) in SMALL.items()}
        token2 = sb("token2", [P, CH, 2], I32)
        w_in = sb("w_in", [P, 4, P])
        w_out = sb("w_out", [P, 2, P])
        w_x = sb("w_x", [P, 2, XD])
        cols = sb("cols", [P, 2, TAPS + 2])
        a_log = sb("a_log", [P, NS])
        a_neg = sb("a_neg", [P, NS])
        gate_w = sb("gate_w", [P, E])
        gate_hi = sb("gate_hi", [P, E], F32R)
        gate_lo = sb("gate_lo", [P, E], F32R)
        c_t = sb("c_t", [P, SEQS])
        sc_t = sb("sc_t", [P, SEQS])
        shift_a = sb("shift_a", [P, SEQS])
        scale_a = sb("scale_a", [P, SEQS])
        mod_rows = sb("mod_rows", [SEQS, 4, P])
        mod_tmp = sb("mod_tmp", [SEQS, 2, P])
        tab = sb("tab", [P, GS, 3, P])
        tab_g = sb("tab_g", [P, GS, P])
        gb_all = sb("gb_all", [P, SEQS, P])
        minus_half = sb("minus_half", [P, GC])

        X = sb("X", [P, CH, P])
        stats_a = sb("stats_a", [P, GC, 6])
        mv_a = sb("mv_a", [P, GC, 2])
        rstd_a = sb("rstd_a", [P, GC])
        nx_a = sb("nx_a", [P, GC, P])
        hT = sb("hT", [P, GT])
        xcp = sb("xcp", [P, 2, GS, SEQ + TAPS - 1])
        acc = sb("acc", [P, 2, GT])
        xsT = sb("xsT", [P, 2, GT])
        sz = sb("sz", [P, 2, GT])
        xs_tok = sb("xs_tok", [P, GC, DI])
        dbc = sb("dbc", [P, GC, XD])
        sp0 = sb("sp0", [P, GC])
        sp1 = sb("sp1", [P, GC])
        sp2 = sb("sp2", [P, GC])
        delta = sb("delta", [P, GC])
        dl_upto = sb("dl_upto", [P, GC, BLK])
        dB = sb("dB", [P, GC, NS])
        c_exp = sb("c_exp", [P, GC, BLK, NS])
        pq = sb("pq", [P, 2, GC, P])
        pqT = sb("pqT", [P, 2, GC, P])
        lev = sb("lev", [P, GC, 4, NS])
        lev_c = sb("lev_c", [P, GC, 4, NS])
        lev_b = sb("lev_b", [P, GC, 4, NS])
        pair = sb("pair", [P, GC, BLK, NS])
        wd = sb("wd", [P, GC, BLK])
        diag = sb("diag", [P, GC, P])
        mT = sb("mT", [P, GS, 3, P])
        yT = sb("yT", [P, 2, GT])
        nx_b = sb("nx_b", [P, GC, P])
        stats_b = sb("stats_b", [P, GC, 6])
        mv_b = sb("mv_b", [P, GC, 2])
        rstd_b = sb("rstd_b", [P, GC])
        h2 = sb("h2", [P, 2, GC, ROW])
        lg = sb("lg", [P, GC, E])
        r1 = sb("r1", [P, GC, E])
        r2 = sb("r2", [P, GC, E])
        oh = sb("oh", [P, 2, GC, E])
        ex = sb("ex", [P, GC, E])
        top = sb("top", [P, 10, GC])
        picked = sb("picked", [P, E, GC])
        ranks = sb("ranks", [P, E, GC])
        base = sb("base", [P, E])
        base2 = sb("base2", [P, E])
        slot = sb("slot", [P, 2, GC], I32)
        plan_f = sb("plan_f", [P, 4, E])
        plan = sb("plan", [P, 3, E], I32)
        cmp = sb("cmp", [P, E, E])
        pad = sb("pad", [P, TR, ROW])
        xh = sb("xh", [P, TILE], F32R)
        xl = sb("xl", [P, TILE], F32R)
        stage = sb("stage", [P, WC])
        w_hi = [sb(f"w_hi{i}", [P, WC], F32R) for i in range(2)]
        w_lo = [sb(f"w_lo{i}", [P, WC], F32R) for i in range(2)]
        sg = sb("sg", [P, 3, TILE])
        prod = sb("prod", [P, 3, TILE])
        ah = sb("ah", [P, 3, TILE], F32R)
        al = sb("al", [P, 3, TILE], F32R)
        y_sb = sb("y_sb", [P, TILE])
        gated = sb("gated", [P, TILE])
        xin = sb("xin", [P, TR, ROW])
        y_rows = sb("y_rows", [P, TR, P])
        aux_w = sb("aux_w", [P, 2, TR])
        aux_d = sb("aux_d", [P, 2, TR], I32)
        fin = [stage[:, k * GC * 2 * P:(k + 1) * GC * 2 * P] for k in range(3)]
        fin += [v[:].rearrange("p h t -> p (h t)") for v in (acc, xsT, sz, xs_tok, yT)]
        fin = [v.rearrange("p (j k d) -> p j k d", j=GC, k=2) for v in fin]

        PS = ctx.enter_context(nc.psum_tensor("PS", [P, 8, 512], F32))
        NARROW = {"gate": (5,), "up": (6,), "down": 7, "turn": 5}
        WIDE = {"gate": (0, 1, 2), "up": (3, 4, 5), "down": 6, "turn": 7}

        def bank(kind, where, c=0):
            b = where[kind]
            return PS[:, b if isinstance(b, int) else b[c % len(b)], :]

        names = """passed consts_in x_in c_in setup_mem stage_clear silu_c mods_pe mods_rows mods_out a_neg_ready
            tab_in tab_free tab_g_in tab_g_free
            var_a eps_a rstd_a nx_ready nxT_done hT_ready xz_done tap_ready conv_done sz_ready xs_ready
            dbc_done dbc_ready xst_done xst_ready nabs_ready exp1_done soft_ready delta_ready cexp_ready spans_done
            cg_done levels_in pairs_in levels_exp pairs_exp pq_ready pqT_done pqT_ready cg_used pairs_ready
            m_done mT_ready mo_ready y_done y_ready o_done var_b eps_b rstd_b h2_ready h2_both h2T_done
            xh_ready xl_ready logits_done lg_ready soft_in soft_out picked_ready counts_done counts_read
            rows_ready sorted_out dve_chain raw_in split_hi split_done piece_hi piece_done gate_done up_done silu_done prod_done
            ah_ready al_ready al_late y_bank_done y_sb_ready yt_done y_out gated_free tile_in xt_done rh_ready
            rl_ready aux_read aux_moved results_out plan_ready pads_out final_added final_gated final_sum final_ready_dve final_ready_pool
            out_done gb_in""".split()
        names += [f"final_in{g}" for g in range(G)]
        s = {n: sem("s_" + n) for n in names}
        block = ctx.enter_context(nc.Block())

        def apart(engine):
            engine.sem_inc(s["passed"], 1)

        CUT = FC // 2
        NRAW = 4
        MAX_TILES = TOKENS // TILE
        MAX_FIRST = 2 * TOKENS // TILE + E

        def tile_count(engine, e):
            return engine.value_load(plan[0:1, 0, bass.ds(e, 1)], min_val=1, max_val=MAX_TILES)

        def tiles_of(engine, e):
            tiles = tile_count(engine, e)
            first = engine.value_load(plan[0:1, 1, bass.ds(e, 1)], min_val=0, max_val=MAX_FIRST)
            return tiles, first

        @block.sync
        def _(sp):
            def load_raw(x):
                gu = a["w_gu"][bass.ds(x, 1)].rearrange("o d f -> (o d) f")
                dn = a["w_dn"][bass.ds(x, 1)].rearrange("o f d -> (o f) d")
                last = FC - 1
                sp.dma_start(stage[:, 0:FF], gu[:, 0:FF]).then_inc(s["raw_in"], 16)
                sp.dma_start(stage[:, FC * P:FC * P + FF], gu[:, FF:2 * FF]).then_inc(s["raw_in"], 16)
                sp.dma_start(stage[:, 2 * FC * P:2 * FC * P + last * P].rearrange("p (c d) -> p c d", d=P),
                             dn[0:last * P, :].rearrange("(c p) d -> p c d", p=P)).then_inc(s["raw_in"], 16)
                sp.dma_start(stage[0:FL, 2 * FC * P + last * P:WC], dn[last * P:FF, :]).then_inc(s["raw_in"], 16)

            x_view = a["x"].rearrange("(c p) d -> p c d", p=P)

            def load_x(c0, n):
                sp.dma_start(X[:, c0:c0 + n, :], x_view[:, c0:c0 + n, :]).then_inc(s["x_in"], 16)

            def const(dst, src):
                sp.dma_start(dst, src).then_inc(s["consts_in"], 16)

            load_x(0, GC)
            sp.wait_ge(s["x_in"], 16)
            sp.dma_start(c_t[:], a["c_t"]).then_inc(s["c_in"], 16)
            sp.dma_start(stage[:, 0:6 * P], a["L0_wmod"]).then_inc(s["c_in"], 16)
            const(mats[:].rearrange("p m t -> p (m t)"), a["big"])
            const(w_in[:].rearrange("p m t -> p (m t)"), a["L0_attn_W_in"])
            const(cols[:], a["cols"].rearrange("(h p) d -> p h d", p=P))
            const(small[:], a["small"])
            const(token2[:], a["token"])
            const(w_out[:], a["L0_attn_W_out"].rearrange("(h p) d -> p h d", p=P))
            const(w_x[:], a["L0_attn_W_x"].rearrange("(h p) d -> p h d", p=P))
            const(a_log[:], a["a_log"].to_broadcast([P, NS]))
            const(gate_w[:], a["gate_t"])
            load_x(GC, CH - GC)
            sp.wait_ge(s["mods_rows"], 1)
            sp.dma_start(mods_dram, mod_rows[:]).then_inc(s["mods_out"], 16)
            sp.wait_ge(s["stage_clear"], 1)
            load_raw(0)
            sp.wait_ge(s["mods_out"], 16)

            def load_tab(g):
                sp.dma_start(tab[:], mods_dram[bass.ds(g * GS, GS), 0:3, :].unsqueeze(0).to_broadcast(
                    [P, GS, 3, P])).then_inc(s["tab_in"], 16)

            def load_tab_g(g):
                sp.dma_start(tab_g[:], mods_dram[bass.ds(g * GS, GS), 3, :].unsqueeze(0).to_broadcast(
                    [P, GS, P])).then_inc(s["tab_g_in"], 16)

            load_tab(0)
            load_tab_g(0)
            sp.dma_start(gb_all[:], mods_dram[:, 3, :].unsqueeze(0).to_broadcast([P, SEQS, P])).then_inc(s["gb_in"], 16)
            sp.wait_ge(s["split_done"], 1)
            load_raw(1)
            with sp.Fori(1, G) as g:
                sp.wait_ge(s["tab_free"], g)
                load_tab(g)
                sp.wait_ge(s["tab_g_free"], g)
                load_tab_g(g)
            sp.wait_ge(s["plan_ready"], 1)
            sp.wait_ge(s["setup_mem"], 2)
            for e in range(E):
                row = sp.value_load(plan[0:1, 2, e:e + 1], min_val=e * REGION, max_val=e * REGION + TOKENS)
                sp.dma_start(sorted_dram[bass.ds(row, TILE)].rearrange("(p r) d -> p (r d)", p=P),
                             pad[:].rearrange("p r d -> p (r d)")).then_inc(s["pads_out"], 16)
            sp.wait_ge(s["pads_out"], 16 * E)
            sp.wait_ge(s["sorted_out"], 16 * 2 * CH)

            def load_tile(row, i):
                sp.wait_ge(s["aux_read"], i + 1)
                sp.dma_start(xin[:].rearrange("p r d -> p (r d)"),
                             sorted_dram[bass.ds(row, TILE)].rearrange("(p r) d -> p (r d)", p=P)).then_inc(
                    s["tile_in"], 16)

            def expert(e, more):
                tiles, first = tiles_of(sp, e)
                if more:
                    sp.wait_ge(s["split_done"], e + 2)
                    load_raw(e + 2)
                with sp.Fori(0, tiles) as t:
                    load_tile(e * REGION + t * TILE, first + t)
                return first + tiles

            with sp.Fori(0, E - 1) as e:
                expert(e, True)
            count = expert(E - 1, False)
            load_tile(0, count)
            sp.wait_ge(s["results_out"], 64 * (count + 1))
            res = result_dram.rearrange("(c p k) d -> p c k d", p=P, k=2)
            out_view = a["out"].rearrange("(c p) d -> p c d", p=P)
            for g in range(G):
                sp.dma_start(fin[g], res[:, g * GC:(g + 1) * GC]).then_inc(s[f"final_in{g}"], 16)
            for q in range(G // 2):
                sp.wait_ge(s["final_ready_dve"], q + 1)
                apart(sp)
                sp.wait_ge(s["final_ready_pool"], q + 1)
                sp.dma_start(out_view[:, q * 2 * GC:(q + 1) * 2 * GC, :], X[:, q * 2 * GC:(q + 1) * 2 * GC, :]).then_inc(
                    s["out_done"], 16)
            sp.wait_ge(s["tile_in"], 16 * (count + 1))
            apart(sp)
            sp.wait_ge(s["out_done"], 16 * G // 2)

        @block.gpsimd
        def _(pool):
            V = nc.gpsimd

            def split_hi(x, buf):
                pool.wait_ge(s["raw_in"], 16 * NRAW * (x + 1))
                apart(pool)
                V.tensor_tensor(w_hi[buf][:], stage[:], M["ones"][:, 0:1].to_broadcast([P, WC]), ALU.mult).then_inc(
                    s["split_hi"], 1)

            def split_lo(x, buf):
                pool.wait_ge(s["split_hi"], x + 1)
                V.tensor_tensor(w_lo[buf][:], stage[:], w_hi[buf][:].bitcast(F32), ALU.subtract).then_inc(
                    s["split_done"], 1)

            def split_piece(g):
                n = WC // (G - 2)
                at = bass.ds((g - 2) * n, n)
                pool.wait_ge(s["raw_in"], 16 * NRAW * 2)
                apart(pool)
                V.tensor_tensor(w_hi[1][:, at], stage[:, at], M["ones"][:, 0:1].to_broadcast([P, n]),
                                ALU.mult).then_inc(s["piece_hi"], 1)
                pool.wait_ge(s["piece_hi"], g - 1)
                V.tensor_tensor(w_lo[1][:, at], stage[:, at], w_hi[1][:, at].bitcast(F32), ALU.subtract).then_inc(
                    s["piece_done"], 1)

            def low(I, c):
                pool.wait_ge(s["ah_ready"], I * FC + c + 1)
                V.tensor_tensor(al[:, c % 3, :], prod[:, c % 3, :], ah[:, c % 3, :].bitcast(F32),
                                ALU.subtract).then_inc(s["al_late"], 1)

            def inverse_root(g, mv, rstd, k):
                pool.wait_ge(s["var_" + k], g + 1)
                apart(pool)
                V.tensor_scalar_add(rstd[:], mv[:, :, 1], EPS).then_inc(s["eps_" + k], 1)
                pool.wait_ge(s["eps_" + k], g + 1)
                V.tensor_tensor(rstd[:], rstd[:], minus_half[:], ALU.pow).then_inc(s["rstd_" + k], 1)

            def expand_c(g):
                full = [P, GC, BLK, NS]
                pool.wait_ge(s["dbc_ready"], g + 1)
                V.tensor_tensor(c_exp[:], dbc[:, :, 1 + NS:XD].unsqueeze(2).to_broadcast(full),
                                S["equal"].unsqueeze(1).unsqueeze(3).to_broadcast(full), ALU.mult).then_inc(
                    s["cexp_ready"], 1)

            def pairs_by_b(g):
                for k in range(2):
                    j0, j1 = k * GC // 2, (k + 1) * GC // 2
                    pool.wait_ge(s["cg_used"], 2 * g + k + 1)
                    V.tensor_tensor(pair[:, j0:j1], pair[:, j0:j1],
                                    dB[:, j0:j1].unsqueeze(2).to_broadcast([P, GC // 2, BLK, NS]),
                                    ALU.mult).then_inc(s["pairs_ready"], 1)

            def sort_rows(g):
                pool.wait_ge(s["rows_ready"], g + 1)
                apart(pool)
                for k in range(2):
                    for j in range(GC):
                        pool.indirect_dma_start(
                            out=sorted_dram, out_offset=bass.IndirectOffsetOnAxis(
                                ap=slot[:, k, j:j + 1].bitcast(U32), axis=0),
                            in_=h2[:, k, j, :], in_offset=None, bounds_check=E * REGION - 1,
                            oob_is_err=False).then_inc(s["sorted_out"], 16)

            def add_shared(g):
                pool.wait_ge(s["y_out"], g + 1)
                x = X[:, bass.ds(g * GC, GC), :].rearrange("p j d -> p (j d)")
                V.tensor_tensor(x, x, gated[:], ALU.add).then_inc(s["gated_free"], 1)

            V.memset(minus_half[:], -0.5)
            V.memset(gated[:], 0.0).then_inc(s["gated_free"], 1)
            V.memset(pad[:], 0.0).then_inc(s["setup_mem"], 1)
            V.memset(xcp[:, :, :, 0:TAPS - 1], 0.0)
            pool.wait_ge(s["setup_mem"], 1)
            V.memset(pad[:, :, P + 1:P + 2].bitcast(I32), NOWHERE).then_inc(s["setup_mem"], 1)
            pool.wait_ge(s["setup_mem"], 2)
            inverse_root(0, mv_a, rstd_a, "a")
            pool.wait_ge(s["mods_pe"], 1)
            V.memset(stage[:], 0.0).then_inc(s["stage_clear"], 1)
            pool.wait_ge(s["consts_in"], 16 * NCONST)
            split_hi(0, 0)

            def body(g, head, prev, prev2):
                if prev2:
                    low(g - 2, CUT)
                if prev:
                    inverse_root(g - 1, mv_b, rstd_b, "b")
                if prev2:
                    low(g - 2, CUT + 1)
                    low(g - 2, CUT + 2)
                expand_c(g)
                if prev2:
                    low(g - 2, CUT + 3)
                if head:
                    inverse_root(g + 1, mv_a, rstd_a, "a")
                pairs_by_b(g)
                if prev2:
                    split_piece(g)
                if prev:
                    sort_rows(g - 1)
                if prev2:
                    add_shared(g - 2)

            body(0, True, False, False)
            split_lo(0, 0)
            body(1, True, True, False)
            with pool.Fori(2, G - 1) as g:
                body(g, True, True, True)
            body(G - 1, False, True, True)
            low(G - 2, CUT)
            inverse_root(G - 1, mv_b, rstd_b, "b")
            for c in range(CUT + 1, FC):
                low(G - 2, c)
            pool.wait_ge(s["piece_done"], G - 2)
            apart(pool)
            pool.sem_inc(s["split_hi"], 1)
            pool.sem_inc(s["split_done"], 1)
            add_shared(G - 2)
            sort_rows(G - 1)
            add_shared(G - 1)
            pool.wait_ge(s["plan_ready"], 1)

            def results(i):
                pool.wait_ge(s["y_out"], SHARED + 1 + i)
                apart(pool)
                for r in range(TR):
                    pool.indirect_dma_start(
                        out=result_dram, out_offset=bass.IndirectOffsetOnAxis(
                            ap=aux_d[:, 0, r:r + 1].bitcast(U32), axis=0),
                        in_=y_rows[:, r, :], in_offset=None, bounds_check=2 * TOKENS - 1,
                        oob_is_err=False).then_inc(s["results_out"], 16)

            def expert(e, buf, more):
                tiles, first = tiles_of(pool, e)
                if more:
                    pool.wait_ge(s["y_bank_done"], SHARED + first)
                    split_hi(e + 2, 1 - buf)
                    split_lo(e + 2, 1 - buf)
                with pool.Fori(0, tiles) as t:
                    results(first + t + 1)

            results(0)
            with pool.Fori(0, E // 2 - 1) as k:
                expert(2 * k, 1, True)
                expert(2 * k + 1, 0, True)
            expert(E - 2, 1, True)
            expert(E - 1, 0, False)
            pool.wait_ge(s["gb_in"], 16)
            for g in range(G):
                pool.wait_ge(s[f"final_in{g}"], 16)
                f = fin[g][:, GC - 1, 0, :]
                V.tensor_tensor(f, f, fin[g][:, GC - 1, 1, :], ALU.add).then_inc(s["final_sum"], 1)
                pool.wait_ge(s["final_sum"], 2 * g + 1)
                V.tensor_tensor(f, f, gb_all[:, (g + 1) * GS - 1, :], ALU.mult).then_inc(s["final_sum"], 1)
                pool.wait_ge(s["final_sum"], 2 * g + 2)
                xg = X[:, (g + 1) * GC - 1, :]
                last = V.tensor_tensor(xg, xg, f, ALU.add)
                if g % 2:
                    last.then_inc(s["final_ready_pool"], 1)

        @block.tensor
        def _(pe):
            def mm(out, lhsT, rhs, start=True, stop=True, **k):
                return nc.tensor.matmul(out, lhsT, rhs, start=start, stop=stop, **k)

            def turn(out, src):
                return nc.tensor.transpose(out, src, M["ident"])

            def high_part(out, buf, w0, rh, start):
                mm(out, w_lo[buf][:, w0:w0 + P], rh, start, False)
                mm(out, w_hi[buf][:, w0:w0 + P], rh, False, False)

            def low_part(out, buf, w0, rl, stop):
                return mm(out, w_hi[buf][:, w0:w0 + P], rl, False, stop)

            def gate_up(buf, I, c, where, low_ready=None):
                gate, up = bank("gate", where, c), bank("up", where, c)
                if where is NARROW:
                    if c == 0:
                        pe.wait_ge(s["y_out"], I)
                    else:
                        pe.wait_ge(s["silu_done"], I * FC + c)
                high_part(gate, buf, c * P, xh[:], True)
                if low_ready is not None:
                    pe.wait_ge(*low_ready)
                low_part(gate, buf, c * P, xl[:], True).then_inc(s["gate_done"], 1)
                if where is NARROW and c:
                    pe.wait_ge(s["prod_done"], I * FC + c)
                high_part(up, buf, (FC + c) * P, xh[:], True)
                low_part(up, buf, (FC + c) * P, xl[:], True).then_inc(s["up_done"], 1)

            def down(buf, I, c, where):
                if c == 0 and where is NARROW:
                    pe.wait_ge(s["counts_read"], I + 1)
                pe.wait_ge(s["ah_ready"], I * FC + c + 1)
                out, w0 = bank("down", where), (2 * FC + c) * P
                high_part(out, buf, w0, ah[:, c % 3, :], c == 0)
                if where is WIDE:
                    pe.wait_ge(s["al_ready"], I * FC + c + 1 - (FC - CUT) * (G - 1))
                elif c < CUT:
                    pe.wait_ge(s["al_ready"], I * CUT + c + 1)
                else:
                    pe.wait_ge(s["al_late"], I * (FC - CUT) + c - CUT + 1)
                last = low_part(out, buf, w0, al[:, c % 3, :], c == FC - 1)
                if c == FC - 1:
                    last.then_inc(s["y_bank_done"], 1)

            def turn_result(I, where):
                pe.wait_ge(s["y_sb_ready"], I + 1)
                out = bank("turn", where)
                for r in range(TR):
                    last = turn(out[:, r * P:(r + 1) * P], y_sb[:, r * P:(r + 1) * P])
                last.then_inc(s["yt_done"], 1)

            def turn_x(g, tailed):
                pe.wait_ge(s["nx_ready"], g + 1)
                if tailed:
                    pe.wait_ge(s["xl_ready"], g - 1)
                for j in range(GC):
                    last = turn(PS[:, 0, j * P:(j + 1) * P], nx_a[:, j, :])
                last.then_inc(s["nxT_done"], 1)

            def project_in(g, m, tailed):
                if m == 0 and tailed:
                    pe.wait_ge(s["lg_ready"], g - 1)
                if m < 2:
                    pe.wait_ge(s["hT_ready"], g + 1)
                else:
                    pe.wait_ge(s["tap_ready"], 2 * g + m - 1)
                mm(PS[:, (m + 1) % 2, :], w_in[:, m, :], hT[:]).then_inc(s["xz_done"], 1)

            def project_x(g):
                pe.wait_ge(s["xs_ready"], 2 * g + 2)
                for j in range(GC):
                    for h in range(2):
                        last = mm(PS[:, 2, j * XD:(j + 1) * XD], xsT[:, h, j * P:(j + 1) * P], w_x[:, h, :],
                                  h == 0, h == 1)
                last.then_inc(s["dbc_done"], 1)

            def turn_xs(g, first):
                if not first:
                    pe.wait_ge(s["y_ready"], 2 * g)
                for j in range(GC):
                    for h in range(2):
                        c0 = (j % 2) * DI + h * P
                        last = turn(PS[:, 3 + j // 2, c0:c0 + P], xsT[:, h, j * P:(j + 1) * P])
                    if j % 2:
                        last.then_inc(s["xst_done"], 1)

            def gather_c(g):
                pe.wait_ge(s["cexp_ready"], g + 1)
                pe.wait_ge(s["xst_ready"], 2 * g + 2)
                for k in range(2):
                    mm(PS[:, 3 + k, :], M["upto16"], c_exp[:, 2 * k:2 * k + 2].rearrange("p j a n -> p (j a n)")
                       ).then_inc(s["cg_done"], 1)

            def sum_spans(g):
                pe.wait_ge(s["delta_ready"], g + 1)
                out = PS[:, 2, 256:256 + 4 * GC].rearrange("p (l j) -> p l j", l=4)
                mm(out[:, 0, 0::2], M["below7"], delta[:, 0::2])
                mm(out[:, 0, 1::2], M["above7"], delta[:, 1::2])
                for k, n in enumerate(("lvl6", "lvl5", "lvl4")):
                    mm(out[:, k + 1, :], M[n], delta[:])
                mm(PS[:, 2, 320:320 + GC * BLK], M["later16"], dl_upto[:].rearrange("p j a -> p (j a)")).then_inc(
                    s["spans_done"], 1)

            def turn_factors(g):
                pe.wait_ge(s["pq_ready"], g + 1)
                pe.wait_ge(s["cg_used"], 2 * g + 2)
                for k in range(2):
                    for j in range(GC):
                        last = turn(PS[:, 3 + k, j * P:(j + 1) * P], pq[:, k, j, :])
                    last.then_inc(s["pqT_done"], 1)

            def weigh(g):
                pe.wait_ge(s["pqT_ready"], 2 * g + 2)
                for q in range(GS):
                    mm(PS[:, 2, q * P:(q + 1) * P], pqT[0:NS, 1, 2 * q, :], pqT[0:NS, 0, 2 * q + 1, :])
                for j in range(GC):
                    last = mm(PS[:, 3, j * P:(j + 1) * P], pqT[:, 1, j, :], pqT[:, 0, j, :])
                last.then_inc(s["m_done"], 1)

            def mix(g):
                pe.wait_ge(s["mT_ready"], g + 1)
                pe.wait_ge(s["mo_ready"], g + 1)
                for h in range(2):
                    for q in range(GS):
                        o = PS[:, 3 + h, q * SEQ:(q + 1) * SEQ]
                        mm(o, xs_tok[:, 2 * q, h * P:(h + 1) * P], mT[:, q, 0:2, :].rearrange("p k t -> p (k t)"))
                        last = mm(o[:, P:SEQ], xs_tok[:, 2 * q + 1, h * P:(h + 1) * P], mT[:, q, 2, :], False, True,
                                  skip_group_check=True)
                    last.then_inc(s["y_done"], 1)

            def project_out(g, more):
                pe.wait_ge(s["y_ready"], 2 * g + 2)
                if more:
                    pe.wait_ge(s["sz_ready"], 2 * g + 3)
                for j in range(GC):
                    for h in range(2):
                        last = mm(PS[:, 1, j * P:(j + 1) * P], yT[:, h, j * P:(j + 1) * P], w_out[:, h, :],
                                  h == 0, h == 1)
                last.then_inc(s["o_done"], 1)

            def turn_h2(g, more):
                pe.wait_ge(s["h2_ready"], g + 1)
                if more:
                    pe.wait_ge(s["sz_ready"], 2 * g + 4)
                for j in range(GC):
                    last = turn(PS[:, 0, j * P:(j + 1) * P], h2[:, 0, j, 0:P])
                last.then_inc(s["h2T_done"], 1)

            def route(g):
                pe.wait_ge(s["xh_ready"], g + 1)
                pe.wait_ge(s["xl_ready"], g + 1)
                for j in range(GC):
                    o = PS[:, 1, j * E:(j + 1) * E]
                    mm(o, xl[:, j * P:(j + 1) * P], gate_hi[:], True, False)
                    mm(o, xh[:, j * P:(j + 1) * P], gate_lo[:], False, False)
                    last = mm(o, xh[:, j * P:(j + 1) * P], gate_hi[:], False, True)
                last.then_inc(s["logits_done"], 1)

            def count_picks(g):
                pe.wait_ge(s["picked_ready"], g + 1)
                mm(PS[:, 7, 0:E], M["before"], ranks[:, :, GC - 1])
                mm(PS[:, 7, E:2 * E], M["ones"], ranks[:, :, GC - 1]).then_inc(s["counts_done"], 1)

            pe.wait_ge(s["c_in"], 32)
            pe.wait_ge(s["silu_c"], 1)
            mm(PS[:, 2, 0:SEQS], stage[:, 0:P], sc_t[:])
            mm(PS[:, 2, SEQS:2 * SEQS], stage[:, P:2 * P], sc_t[:])
            mm(PS[0:SEQS, 1, :], sc_t[:], stage[:, 2 * P:6 * P]).then_inc(s["mods_pe"], 1)
            pe.wait_ge(s["consts_in"], 16 * NCONST)
            turn_x(0, False)
            pe.wait_ge(s["mods_rows"], 1)
            for m in range(4):
                project_in(0, m, False)

            def step(I, c):
                if c < FC:
                    gate_up(0, I, c, NARROW)
                if c:
                    down(0, I, c - 1, NARROW)

            def body(g, head, prev, prev2):
                if prev2:
                    gate_up(0, g - 2, CUT, NARROW)
                project_x(g)
                if prev:
                    project_out(g - 1, True)
                if prev2:
                    gate_up(0, g - 2, CUT + 1, NARROW)
                    down(0, g - 2, CUT - 1, NARROW)
                turn_xs(g, not prev)
                if prev2:
                    down(0, g - 2, CUT, NARROW)
                sum_spans(g)
                if prev2:
                    gate_up(0, g - 2, CUT + 2, NARROW)
                    down(0, g - 2, CUT + 1, NARROW)
                    gate_up(0, g - 2, CUT + 3, NARROW)
                    down(0, g - 2, CUT + 2, NARROW)
                gather_c(g)
                if prev:
                    turn_h2(g - 1, True)
                if prev2:
                    down(0, g - 2, CUT + 3, NARROW)
                if prev:
                    route(g - 1)
                if prev2:
                    turn_result(g - 2, NARROW)
                turn_factors(g)
                if prev:
                    pe.wait_ge(s["split_done"], 1)
                    apart(pe)
                    gate_up(0, g - 1, 0, NARROW)
                weigh(g)
                if head:
                    turn_x(g + 1, prev)
                if prev:
                    count_picks(g - 1)
                    gate_up(0, g - 1, 1, NARROW)
                if head:
                    project_in(g + 1, 0, prev)
                    project_in(g + 1, 1, prev)
                    project_in(g + 1, 2, prev)
                if prev:
                    down(0, g - 1, 0, NARROW)
                mix(g)
                if prev:
                    gate_up(0, g - 1, 2, NARROW)
                    gate_up(0, g - 1, 3, NARROW)
                    down(0, g - 1, 1, NARROW)
                if head:
                    project_in(g + 1, 3, prev)
                if prev:
                    down(0, g - 1, 2, NARROW)

            body(0, True, False, False)
            body(1, True, True, False)
            with pe.Fori(2, G - 1) as g:
                body(g, True, True, True)
            body(G - 1, False, True, True)
            project_out(G - 1, False)
            for c in range(CUT, FC):
                step(G - 2, c)
            turn_h2(G - 1, False)
            step(G - 2, FC)
            turn_result(G - 2, NARROW)
            route(G - 1)
            for c in range(FC + 2):
                if c == 1:
                    pe.wait_ge(s["lg_ready"], G)
                if c == 1:
                    count_picks(G - 1)
                if c < FC:
                    gate_up(0, G - 1, c, WIDE)
                if c >= 2:
                    down(0, G - 1, c - 2, WIDE)
            pe.wait_ge(s["counts_read"], G)
            turn_result(G - 1, WIDE)

            def turn_tile(i):
                pe.wait_ge(s["tile_in"], 16 * (i + 1))
                for r in range(TR):
                    last = turn(PS[:, 7, r * P:(r + 1) * P], xin[:, r, 0:P])
                last.then_inc(s["xt_done"], 1)

            pe.wait_ge(s["plan_ready"], 1)
            pe.wait_ge(s["y_out"], SHARED)
            turn_tile(0)

            def tile_body(buf, i):
                I = SHARED + i
                pe.wait_ge(s["rh_ready"], i + 1)
                for c in range(FC):
                    gate_up(buf, I, c, WIDE, (s["rl_ready"], i + 1) if c == 0 else None)
                    if c == 1:
                        turn_result(I - 1, WIDE)
                    if c >= 2:
                        down(buf, I, c - 2, WIDE)
                pe.wait_ge(s["y_out"], I + 1)
                turn_tile(i + 1)
                down(buf, I, FC - 2, WIDE)
                down(buf, I, FC - 1, WIDE)

            def expert(e, buf, first=None):
                if first is None:
                    tiles, first = tiles_of(pe, e)
                else:
                    tiles = tile_count(pe, e)
                pe.wait_ge(s["split_done"], e + 2)
                apart(pe)
                with pe.Fori(0, tiles) as t:
                    tile_body(buf, first + t)
                return first + tiles

            with pe.Fori(0, E // 2 - 1) as k:
                expert(2 * k + 1, 0, expert(2 * k, 1))
            count = expert(E - 1, 0, expert(E - 2, 1))
            pe.wait_ge(s["rl_ready"], count + 1)
            turn_result(SHARED + count - 1, WIDE)

        @block.scalar
        def _(act):
            A = nc.scalar

            def silu(I, c, where):
                act.wait_ge(s["gate_done"], I * FC + c + 1)
                A.activation(sg[:, c % 3, :], bank("gate", where, c), ACT.Silu).then_inc(s["silu_done"], 1)

            def high(I, c):
                act.wait_ge(s["prod_done"], I * FC + c + 1)
                A.copy(ah[:, c % 3, :], prod[:, c % 3, :]).then_inc(s["ah_ready"], 1)

            def keep_result(I, where):
                act.wait_ge(s["y_bank_done"], I + 1)
                A.copy(y_sb[:], bank("down", where)).then_inc(s["y_sb_ready"], 1)

            def modulate(g):
                act.wait_ge(s["nxT_done"], g + 1)
                for q in range(GS):
                    last = A.activation(hT[:, q * SEQ:(q + 1) * SEQ], PS[:, 0, q * SEQ:(q + 1) * SEQ],
                                        ACT.Identity, bias=shift_a[:, bass.ds(g * GS + q, 1)],
                                        scale=scale_a[:, bass.ds(g * GS + q, 1)])
                last.then_inc(s["hT_ready"], 1)

            def last_tap(g, h):
                act.wait_ge(s["xz_done"], 4 * g + h + 1)
                src = PS[:, (h + 1) % 2, :]
                A.copy(xcp[:, h, :, TAPS - 1:], src.rearrange("p (q t) -> p q t", q=GS))
                A.activation(acc[:, h, :], src, ACT.Identity, bias=cols[:, h, TAPS:TAPS + 1],
                             scale=cols[:, h, TAPS - 1:TAPS]).then_inc(s["tap_ready"], 1)

            def silu_z(g, h):
                act.wait_ge(s["xz_done"], 4 * g + h + 3)
                A.activation(sz[:, h, :], PS[:, (h + 1) % 2, :], ACT.Silu).then_inc(s["sz_ready"], 1)

            def silu_x(g, h, first=False):
                act.wait_ge(s["conv_done"], 2 * g + h + 1)
                if not first:
                    act.wait_ge(s["y_ready"], 2 * g)
                A.activation(xsT[:, h, :], acc[:, h, :], ACT.Silu).then_inc(s["xs_ready"], 1)

            def softplus(g):
                act.wait_ge(s["nabs_ready"], g + 1)
                A.activation(sp1[:], sp0[:], ACT.Exp).then_inc(s["exp1_done"], 1)
                act.wait_ge(s["exp1_done"], g + 1)
                A.activation(sp2[:], sp1[:], ACT.Ln, bias=1.0).then_inc(s["soft_ready"], 1)

            def keep_xs(g):
                for k in range(2):
                    act.wait_ge(s["xst_done"], 2 * g + k + 1)
                    A.copy(xs_tok[:, 2 * k:2 * k + 2, :].rearrange("p j d -> p (j d)"), PS[:, 3 + k, :]).then_inc(
                        s["xst_ready"], 1)

            def decays(g):
                act.wait_ge(s["levels_in"], g + 1)
                A.activation(lev[:], lev[:], ACT.Exp).then_inc(s["levels_exp"], 1)
                for k in range(2):
                    act.wait_ge(s["pairs_in"], 2 * g + k + 1)
                    v = pair[:, 2 * k:2 * k + 2].rearrange("p j a n -> p (j a n)")
                    A.activation(v, v, ACT.Exp).then_inc(s["pairs_exp"], 1)

            def keep_factors(g):
                for k in range(2):
                    act.wait_ge(s["pqT_done"], 2 * g + k + 1)
                    A.copy(pqT[:, k].rearrange("p j t -> p (j t)"), PS[:, 3 + k, :]).then_inc(s["pqT_ready"], 1)

            def keep_next(g):
                act.wait_ge(s["m_done"], g + 1)
                A.copy(mT[:, :, 1, :], PS[:, 2, 0:GS * P].rearrange("p (q t) -> p q t", q=GS)).then_inc(
                    s["mo_ready"], 1)

            def keep_h2(g, first):
                act.wait_ge(s["h2T_done"], g + 1)
                if not first:
                    act.wait_ge(s["up_done"], FC * g)
                A.copy(xh[:], PS[:, 0, :]).then_inc(s["xh_ready"], 1)
                A.copy(h2[:, 1, :, 0:P], h2[:, 0, :, 0:P]).then_inc(s["h2_both"], 1)

            def router_exp(g):
                act.wait_ge(s["soft_in"], g + 1)
                A.activation(ex[:], ex[:], ACT.Exp).then_inc(s["soft_out"], 1)

            act.wait_ge(s["c_in"], 32)
            A.activation(sc_t[:], c_t[:], ACT.Silu).then_inc(s["silu_c"], 1)
            act.wait_ge(s["consts_in"], 16 * NCONST)
            act.wait_ge(s["mods_rows"], 1)
            modulate(0)
            last_tap(0, 0)
            last_tap(0, 1)
            silu_z(0, 0)
            silu_z(0, 1)
            silu_x(0, 0, True)
            silu_x(0, 1, True)
            A.activation(a_neg[:], a_log[:], ACT.Exp).then_inc(s["a_neg_ready"], 1)

            def step(I, c):
                silu(I, c, NARROW)
                high(I, c)

            def body(g, head, prev, prev2, first):
                if not first:
                    silu_x(g, 0)
                    silu_x(g, 1)
                    silu_z(g, 0)
                    silu_z(g, 1)
                if prev2:
                    silu(g - 2, CUT, NARROW)
                    high(g - 2, CUT)
                softplus(g)
                if prev2:
                    silu(g - 2, CUT + 1, NARROW)
                    high(g - 2, CUT + 1)
                keep_xs(g)
                if prev2:
                    silu(g - 2, CUT + 2, NARROW)
                    high(g - 2, CUT + 2)
                decays(g)
                if prev2:
                    silu(g - 2, CUT + 3, NARROW)
                    high(g - 2, CUT + 3)
                if prev:
                    keep_h2(g - 1, not prev2)
                if prev2:
                    keep_result(g - 2, NARROW)
                keep_factors(g)
                if prev:
                    silu(g - 1, 0, NARROW)
                    router_exp(g - 1)
                    high(g - 1, 0)
                keep_next(g)
                if head:
                    modulate(g + 1)
                    last_tap(g + 1, 0)
                    last_tap(g + 1, 1)
                if prev:
                    silu(g - 1, 1, NARROW)
                    high(g - 1, 1)
                    silu(g - 1, 2, NARROW)
                    high(g - 1, 2)
                    silu(g - 1, 3, NARROW)
                    high(g - 1, 3)

            body(0, True, False, False, True)
            body(1, True, True, False, False)
            with act.Fori(2, G - 1) as g:
                body(g, True, True, True, False)
            body(G - 1, False, True, True, False)
            for c in range(CUT, FC):
                step(G - 2, c)
            keep_h2(G - 1, False)
            keep_result(G - 2, NARROW)
            for c in range(FC):
                if c == 1:
                    router_exp(G - 1)
                silu(G - 1, c, WIDE)
                high(G - 1, c)
            keep_result(G - 1, WIDE)

            act.wait_ge(s["plan_ready"], 1)

            def split_tile(i):
                act.wait_ge(s["xt_done"], i + 1)
                A.copy(xh[:], PS[:, 7, :]).then_inc(s["rh_ready"], 1)

            split_tile(0)
            with act.Fori(0, E) as e:
                tiles, first = tiles_of(act, e)
                with act.Fori(0, tiles) as t:
                    i = first + t
                    silu(SHARED + i, 0, WIDE)
                    for c in range(FC):
                        if c + 1 < FC:
                            silu(SHARED + i, c + 1, WIDE)
                        high(SHARED + i, c)
                    split_tile(i + 1)
                    keep_result(SHARED + i, WIDE)

        @block.vector
        def _(dve):
            V = nc.vector
            PER_BODY = 40
            chain = {"base": 0, "n": 0}

            def link(ins):
                ins.then_inc(s["dve_chain"], 1)
                chain["n"] += 1
                dve.wait_ge(s["dve_chain"], chain["base"] + chain["n"])

            def bc(ap, shape):
                return ap.to_broadcast(shape)

            def by_seq(ap):
                return ap.rearrange("p (q k) d -> p q k d", k=2)

            def chunk(g):
                return lambda j: X[:, bass.ds(g * GC + j, 1), :].rearrange("p o d -> p (o d)")

            def moments(src, stats, mv, done):
                apart(dve)
                for j in range(GC):
                    last = V.bn_stats(stats[:, j, :], src(j))
                link(last)
                apart(dve)
                for j in range(GC):
                    last = V.bn_aggr(mv[:, j, :], stats[:, j, :])
                last.then_inc(done, 1)

            def norm(src, mv, rstd, out):
                for j in range(GC):
                    last = V.tensor_scalar(out[:, j, :], src(j), mv[:, j, 0:1], rstd[:, j:j + 1],
                                           ALU.subtract, ALU.mult)
                return last

            def product(I, c, where):
                dve.wait_ge(s["silu_done"], I * FC + c + 1)
                dve.wait_ge(s["up_done"], I * FC + c + 1)
                V.tensor_tensor(prod[:, c % 3, :], bank("up", where, c), sg[:, c % 3, :], ALU.mult).then_inc(
                    s["prod_done"], 1)

            def low(I, c):
                dve.wait_ge(s["ah_ready"], I * FC + c + 1)
                V.tensor_tensor(al[:, c % 3, :], prod[:, c % 3, :], ah[:, c % 3, :].bitcast(F32),
                                ALU.subtract).then_inc(s["al_ready"], 1)

            def head_moments(g):
                moments(chunk(g), stats_a, mv_a, s["var_a"])

            def head_norm(g):
                dve.wait_ge(s["rstd_a"], g + 1)
                norm(chunk(g), mv_a, rstd_a, nx_a).then_inc(s["nx_ready"], 1)

            def conv(g, h):
                dve.wait_ge(s["tap_ready"], 2 * g + h + 1)
                o = acc[:, h, :].rearrange("p (q t) -> p q t", q=GS)
                for k in range(TAPS - 1):
                    last = V.scalar_tensor_tensor(o, xcp[:, h, :, k:k + SEQ], cols[:, h, k:k + 1], o,
                                                  ALU.mult, ALU.add)
                    if k < TAPS - 2:
                        link(last)
                last.then_inc(s["conv_done"], 1)

            Bp, Cp = dbc[:, :, 1:1 + NS], dbc[:, :, 1 + NS:XD]
            lv = [P, GC, 4, NS]

            def take_dbc(g):
                dve.wait_ge(s["dbc_done"], g + 1)
                V.tensor_copy(dbc[:].rearrange("p j n -> p (j n)"), PS[:, 2, 0:GC * XD]).then_inc(s["dbc_ready"], 1)
                dve.wait_ge(s["dbc_ready"], g + 1)
                V.scalar_tensor_tensor(sp0[:], dbc[:, :, 0], -1.0, dbc[:, :, 0], ALU.mult, ALU.min).then_inc(
                    s["nabs_ready"], 1)

            def make_delta(g):
                dve.wait_ge(s["soft_ready"], g + 1)
                link(V.scalar_tensor_tensor(delta[:], dbc[:, :, 0], 0.0, sp2[:], ALU.max, ALU.add))
                V.tensor_tensor(dl_upto[:], bc(delta[:].unsqueeze(2), [P, GC, BLK]),
                                bc(S["upto"].unsqueeze(1), [P, GC, BLK]), ALU.mult).then_inc(s["delta_ready"], 1)
                link(V.tensor_tensor(dB[:], bc(delta[:].unsqueeze(2), [P, GC, NS]), Bp, ALU.mult))

            def exponents(g):
                dve.wait_ge(s["spans_done"], g + 1)
                spans = PS[:, 2, 256:256 + 4 * GC].rearrange("p (l j) -> p j l", l=4)
                V.tensor_tensor(lev[:], bc(spans.unsqueeze(3), lv), bc(a_neg[:].unsqueeze(1).unsqueeze(1), lv),
                                ALU.mult).then_inc(s["levels_in"], 1)
                within = PS[:, 2, 320:320 + GC * BLK].rearrange("p (j a) -> p j a", j=GC)
                half = [P, GC // 2, BLK, NS]
                for k in range(2):
                    j0, j1 = k * GC // 2, (k + 1) * GC // 2
                    V.tensor_tensor(pair[:, j0:j1], bc(within[:, j0:j1].unsqueeze(3), half),
                                    bc(a_neg[:].unsqueeze(1).unsqueeze(1), half), ALU.mult).then_inc(
                        s["pairs_in"], 1)

            def factors(g):
                dve.wait_ge(s["levels_exp"], g + 1)
                V.tensor_tensor(lev_c[:], lev[:], bc(Cp.unsqueeze(2), lv), ALU.mult)
                link(V.tensor_tensor(lev_b[:], lev[:], bc(dB[:].unsqueeze(2), lv), ALU.mult))
                for k, (src, role) in enumerate(((lev_c, "upper"), (lev_b, "lower"))):
                    pv = pq[:, k].rearrange("p j (b n) -> p j b n", n=NS)
                    role7 = S[role][:, 0:2].unsqueeze(1).unsqueeze(3)
                    V.tensor_tensor(pv[:, :, 0, :].rearrange("p (q k) n -> p q k n", k=2),
                                    src[:, :, 0, :].rearrange("p (q k) n -> p q k n", k=2),
                                    bc(role7, [P, GS, 2, NS]), ALU.mult)
                    b0 = 1
                    for l in range(1, 4):
                        nb = 1 << (l - 1)
                        sh = [P, GC, nb, NS]
                        last = V.tensor_tensor(pv[:, :, b0:b0 + nb, :], bc(src[:, :, l, :].unsqueeze(2), sh),
                                               bc(S[role][:, b0 + 1:b0 + 1 + nb].unsqueeze(1).unsqueeze(3), sh),
                                               ALU.mult)
                        b0 += nb
                last.then_inc(s["pq_ready"], 1)

            def pairs_by_c(g):
                for k in range(2):
                    dve.wait_ge(s["pairs_exp"], 2 * g + k + 1)
                    dve.wait_ge(s["cg_done"], 2 * g + k + 1)
                    v = pair[:, 2 * k:2 * k + 2].rearrange("p j a n -> p (j a n)")
                    V.tensor_tensor(v, v, PS[:, 3 + k, :], ALU.mult).then_inc(s["cg_used"], 1)

            def sum_pairs(g):
                dve.wait_ge(s["pairs_ready"], 2 * g + 2)
                link(V.tensor_reduce(wd[:], pair[:], AX.X, ALU.add))
                sh = [P, GC, NB, BLK]
                V.tensor_tensor(diag[:].rearrange("p j (b a) -> p j b a", a=BLK), bc(wd[:].unsqueeze(2), sh),
                                bc(S["block"].unsqueeze(1).unsqueeze(3), sh), ALU.mult).then_inc(s["dve_chain"], 1)
                chain["n"] += 1

            def add_pairs(g):
                dve.wait_ge(s["dve_chain"], chain["base"] + chain["n"])
                dve.wait_ge(s["m_done"], g + 1)
                V.tensor_tensor(mT[:, :, 0:3:2, :], PS[:, 3, :].rearrange("p (q k t) -> p q k t", q=GS, k=2),
                                by_seq(diag[:]), ALU.add).then_inc(s["mT_ready"], 1)

            def gate_y(g, h):
                dve.wait_ge(s["y_done"], 2 * g + h + 1)
                link(V.scalar_tensor_tensor(yT[:, h, :], xsT[:, h, :], cols[:, h, TAPS + 1:TAPS + 2],
                                            PS[:, 3 + h, :], ALU.mult, ALU.add))
                V.tensor_tensor(yT[:, h, :], yT[:, h, :], sz[:, h, :], ALU.mult).then_inc(s["y_ready"], 1)

            def residual(g):
                dve.wait_ge(s["o_done"], g + 1)
                dve.wait_ge(s["tab_in"], 16 * (g + 1))
                seq = [P, GS, 2, P]
                xg = X[:, bass.ds(g * GC, GC), :]
                link(V.tensor_tensor(by_seq(nx_b[:]), PS[:, 1, :].rearrange("p (q k d) -> p q k d", q=GS, k=2),
                                     bc(tab[:, :, 0:1, :], seq), ALU.mult))
                link(V.tensor_tensor(xg, xg, nx_b[:], ALU.add))
                moments(chunk(g), stats_b, mv_b, s["var_b"])

            def second_norm(g, first):
                seq = [P, GS, 2, P]
                dve.wait_ge(s["rstd_b"], g + 1)
                link(norm(chunk(g), mv_b, rstd_b, nx_b))
                link(V.tensor_tensor(by_seq(nx_b[:]), by_seq(nx_b[:]), bc(tab[:, :, 2:3, :], seq), ALU.mult))
                if not first:
                    dve.wait_ge(s["sorted_out"], 16 * 2 * GC * g)
                V.tensor_tensor(by_seq(h2[:, 0, :, 0:P]), by_seq(nx_b[:]), bc(tab[:, :, 1:2, :], seq),
                                ALU.add).then_inc(s["h2_ready"], 1)
                dve.wait_ge(s["h2_ready"], g + 1)
                apart(dve)
                V.engine_nop().then_inc(s["tab_free"], 1)

            def low_x(g):
                dve.wait_ge(s["xh_ready"], g + 1)
                V.tensor_tensor(xl[:], PS[:, 0, :], xh[:].bitcast(F32), ALU.subtract).then_inc(s["xl_ready"], 1)

            def take_logits(g):
                dve.wait_ge(s["logits_done"], g + 1)
                V.tensor_copy(lg[:].rearrange("p j e -> p (j e)"), PS[:, 1, 0:GC * E]).then_inc(s["lg_ready"], 1)
                dve.wait_ge(s["lg_ready"], g + 1)

            ge = [P, GC, E]

            def pick(g):
                rev = bc(S["rev"].unsqueeze(1), ge)
                for k in range(2):
                    src = lg if k == 0 else r2
                    link(V.tensor_reduce(top[:, k, :], src[:], AX.X, ALU.max))
                    if k == 0:
                        V.tensor_tensor(ex[:], lg[:], bc(top[:, 0, :].unsqueeze(2), ge), ALU.subtract).then_inc(
                            s["soft_in"], 1)
                    link(V.tensor_tensor(r1[:], src[:], bc(top[:, k, :].unsqueeze(2), ge), ALU.is_equal))
                    link(V.tensor_tensor(r1[:], r1[:], rev, ALU.mult))
                    link(V.tensor_reduce(top[:, 2, :], r1[:], AX.X, ALU.max))
                    link(V.tensor_tensor(oh[:, k], r1[:], bc(top[:, 2, :].unsqueeze(2), ge), ALU.is_equal))
                    if k == 0:
                        link(V.scalar_tensor_tensor(r2[:], oh[:, 0], -3.0e38, lg[:], ALU.mult, ALU.add))
                link(V.tensor_tensor(picked[:].rearrange("p e j -> p j e"), oh[:, 0], oh[:, 1], ALU.add))
                V.tensor_tensor_scan(ranks[:].rearrange("p e j -> p (e j)"), S["seg"],
                                     picked[:].rearrange("p e j -> p (e j)"), 0.0, ALU.mult, ALU.add).then_inc(
                    s["picked_ready"], 1)

            def weights(g):
                dve.wait_ge(s["soft_out"], g + 1)
                link(V.tensor_reduce(top[:, 3, :], ex[:], AX.X, ALU.add))
                V.reciprocal(top[:, 4, :], top[:, 3, :])
                link(V.tensor_tensor(r1[:], ex[:], oh[:, 1], ALU.mult))
                link(V.tensor_reduce(top[:, 5, :], r1[:], AX.X, ALU.add))
                link(V.tensor_tensor(top[:, 5, :], top[:, 5, :], top[:, 4, :], ALU.mult))
                link(V.scalar_tensor_tensor(top[:, 6, :], top[:, 4, :], 1e-8, top[:, 5, :], ALU.add, ALU.add))
                link(V.reciprocal(top[:, 7, :], top[:, 6, :]))

            def place(g):
                dve.wait_ge(s["counts_done"], g + 1)
                dve.wait_ge(s["picked_ready"], g + 1)
                link(V.tensor_tensor(base2[:], base[:], PS[:, 7, 0:E], ALU.add))
                V.tensor_tensor(base[:], base[:], PS[:, 7, E:2 * E], ALU.add).then_inc(s["counts_read"], 1)
                link(V.tensor_tensor(ranks[:], ranks[:], picked[:], ALU.subtract))
                link(V.tensor_tensor(ranks[:], ranks[:], bc(base2[:].unsqueeze(2), [P, E, GC]), ALU.add))
                dve.wait_ge(s["h2_both"], g + 1)
                for k in range(2):
                    V.tensor_tensor(h2[:, k, :, P], top[:, 4 + k, :], top[:, 7, :], ALU.mult)
                    V.tensor_copy(h2[:, k, :, P + 1].bitcast(I32),
                                  token2[:, bass.ds(g * GC, GC), k:k + 1].rearrange("p j o -> p (j o)"))
                    last = V.tensor_tensor(oh[:, k], oh[:, k], ranks[:].rearrange("p e j -> p j e"), ALU.mult)
                link(last)
                link(V.tensor_reduce(top[:, 8:10, :], oh[:], AX.X, ALU.add))
                V.tensor_copy(slot[:], top[:, 8:10, :]).then_inc(s["rows_ready"], 1)

            def gate_shared(g, where):
                dve.wait_ge(s["yt_done"], g + 1)
                dve.wait_ge(s["tab_g_in"], 16 * (g + 1))
                dve.wait_ge(s["gated_free"], g + 1)
                seq = [P, GS, 2, P]
                V.tensor_tensor(gated[:].rearrange("p (q k d) -> p q k d", q=GS, k=2),
                                bank("turn", where).rearrange("p (q k d) -> p q k d", q=GS, k=2),
                                bc(tab_g[:].unsqueeze(2), seq), ALU.mult).then_inc(s["y_out"], 1)
                dve.wait_ge(s["y_out"], g + 1)
                apart(dve)
                V.engine_nop().then_inc(s["tab_g_free"], 1)

            dve.wait_ge(s["x_in"], 16)
            head_moments(0)
            dve.wait_ge(s["mods_pe"], 1)
            V.tensor_copy(shift_a[:], PS[:, 2, 0:SEQS])
            V.tensor_scalar_add(scale_a[:], PS[:, 2, SEQS:2 * SEQS], 1.0)
            rows = PS[0:SEQS, 1, :].rearrange("p (m d) -> p m d", m=4)
            V.tensor_copy(mod_rows[:, 1, :], rows[:, 1, :])
            V.tensor_scalar_add(mod_rows[:, 2, :], rows[:, 2, :], 1.0)
            V.tensor_copy(mod_rows[:, 0, :], rows[:, 0, :])
            link(V.tensor_copy(mod_rows[:, 3, :], rows[:, 3, :]))
            for k, m in enumerate((0, 3)):
                V.tensor_scalar(mod_tmp[:, k, :], mod_rows[:, m, :], 0.0, 2.0, ALU.is_ge, ALU.mult)
                link(V.scalar_tensor_tensor(mod_rows[:, m, :], mod_rows[:, m, :], -1.0, mod_rows[:, m, :],
                                            ALU.mult, ALU.max))
            link(V.tensor_scalar_add(mod_tmp[:], mod_tmp[:], -1.0))
            for k, m in enumerate((0, 3)):
                last = V.scalar_tensor_tensor(mod_rows[:, m, :], mod_rows[:, m, :], 0.25, mod_tmp[:, k, :],
                                              ALU.max, ALU.mult)
            last.then_inc(s["mods_rows"], 1)
            head_norm(0)
            dve.wait_ge(s["consts_in"], 16 * NCONST)
            V.tensor_copy(base[:], S["region"])
            link(V.tensor_copy(gate_hi[:], gate_w[:]))
            link(V.tensor_tensor(gate_lo[:], gate_w[:], gate_hi[:].bitcast(F32), ALU.subtract))
            V.memset(aux_w[:], 0.0)
            link(V.memset(aux_d[:], NOWHERE))
            dve.wait_ge(s["setup_mem"], 2)
            conv(0, 0)
            conv(0, 1)
            dve.wait_ge(s["a_neg_ready"], 1)
            link(V.tensor_scalar_mul(a_neg[:], a_neg[:], -1.0))
            dve.wait_ge(s["x_in"], 32)

            def body(g, head, prev, prev2):
                if prev2:
                    product(g - 2, CUT, NARROW)
                take_dbc(g)
                if prev:
                    residual(g - 1)
                make_delta(g)
                if prev2:
                    product(g - 2, CUT + 1, NARROW)
                if prev:
                    second_norm(g - 1, not prev2)
                if prev2:
                    product(g - 2, CUT + 2, NARROW)
                exponents(g)
                factors(g)
                if prev2:
                    product(g - 2, CUT + 3, NARROW)
                pairs_by_c(g)
                if prev:
                    low_x(g - 1)
                if head:
                    head_moments(g + 1)
                if prev2:
                    gate_shared(g - 2, NARROW)
                if prev:
                    take_logits(g - 1)
                if head:
                    head_norm(g + 1)
                if prev:
                    pick(g - 1)
                    product(g - 1, 0, NARROW)
                sum_pairs(g)
                if prev:
                    low(g - 1, 0)
                add_pairs(g)
                if prev:
                    weights(g - 1)
                    place(g - 1)
                if head:
                    conv(g + 1, 0)
                gate_y(g, 0)
                if prev:
                    product(g - 1, 1, NARROW)
                gate_y(g, 1)
                if prev:
                    product(g - 1, 2, NARROW)
                    low(g - 1, 1)
                if head:
                    conv(g + 1, 1)
                if prev:
                    low(g - 1, 2)
                    product(g - 1, 3, NARROW)
                    low(g - 1, 3)

            body(0, True, False, False)
            body(1, True, True, False)
            before = chain["n"]
            with dve.Fori(2, G - 1) as g:
                chain["base"], chain["n"] = (g - 2) * PER_BODY + before, 0
                body(g, True, True, True)
                assert chain["n"] == PER_BODY, chain["n"]
            chain["base"], chain["n"] = (G - 3) * PER_BODY + before, 0
            body(G - 1, False, True, True)
            residual(G - 1)
            product(G - 2, CUT, NARROW)
            second_norm(G - 1, False)
            for c in range(CUT + 1, FC):
                product(G - 2, c, NARROW)
            low_x(G - 1)
            gate_shared(G - 2, NARROW)
            take_logits(G - 1)
            g = G - 1
            pick(g)
            product(g, 0, WIDE)
            low(g, 0)
            weights(g)
            place(g)
            dve.wait_ge(s["counts_read"], G)
            link(V.tensor_tensor(plan_f[:, 3, :], base[:], S["region"], ALU.subtract))
            link(V.tensor_tensor(cmp[:], bc(plan_f[:, 3, :].unsqueeze(2), [P, E, E]),
                                 bc(S["many"].unsqueeze(1), [P, E, E]), ALU.is_gt))
            link(V.tensor_reduce(plan_f[:, 0, :], cmp[:], AX.X, ALU.add))
            link(V.tensor_scalar(plan_f[:, 0, :], plan_f[:, 0, :], 1.0, None, ALU.max))
            link(V.tensor_tensor_scan(plan_f[:, 1, :], M["ones"][:, 0:E], plan_f[:, 0, :], 0.0, ALU.mult, ALU.add))
            link(V.tensor_tensor(plan_f[:, 1, :], plan_f[:, 1, :], plan_f[:, 0, :], ALU.subtract))
            V.tensor_copy(plan[:, 2, :], base[:])
            V.tensor_copy(plan[:, 0:2, :], plan_f[:, 0:2, :]).then_inc(s["plan_ready"], 1)
            V.engine_nop().then_inc(s["aux_read"], 1)
            for c in range(1, FC):
                product(g, c, WIDE)
                low(g, c)
            gate_shared(g, WIDE)

            def take_tile(i, moved):
                dve.wait_ge(s["rh_ready"], i + 1)
                V.tensor_tensor(xl[:], PS[:, 7, :], xh[:].bitcast(F32), ALU.subtract).then_inc(s["rl_ready"], 1)
                if moved:
                    dve.wait_ge(s["aux_moved"], i)
                V.tensor_copy(aux_w[:, 1, :], xin[:, :, P])
                V.tensor_copy(aux_d[:, 1, :], xin[:, :, P + 1].bitcast(I32)).then_inc(s["aux_read"], 1)

            dve.wait_ge(s["plan_ready"], 1)
            take_tile(0, False)

            def give_rows(i):
                dve.wait_ge(s["yt_done"], SHARED + 1 + i)
                V.tensor_tensor(y_rows[:], PS[:, 7, :].rearrange("p (r d) -> p r d", r=TR),
                                bc(aux_w[:, 0, :].unsqueeze(2), [P, TR, P]), ALU.mult).then_inc(s["y_out"], 1)

            with dve.Fori(0, E) as e:
                tiles, first = tiles_of(dve, e)
                with dve.Fori(0, tiles) as t:
                    i = first + t
                    product(SHARED + i, 0, WIDE)
                    for c in range(FC):
                        if c == 2:
                            give_rows(i)
                        if c + 1 < FC:
                            product(SHARED + i, c + 1, WIDE)
                        low(SHARED + i, c)
                        if c == FC - 3:
                            dve.wait_ge(s["results_out"], 64 * (i + 1))
                            dve.wait_ge(s["aux_read"], i + 2)
                            V.tensor_copy(aux_w[:, 0, :], aux_w[:, 1, :])
                            V.tensor_copy(aux_d[:, 0, :], aux_d[:, 1, :]).then_inc(s["aux_moved"], 1)
                    take_tile(i + 1, True)
            last_tiles, last_first = tiles_of(dve, E - 1)
            give_rows(last_first + last_tiles)
            c1 = GC - 1
            dve.wait_ge(s["gb_in"], 16)
            for step in range(G + 2):
                if step < G:
                    dve.wait_ge(s[f"final_in{step}"], 16)
                    f = fin[step][:, 0:c1]
                    V.tensor_tensor(f[:, :, 0, :], f[:, :, 0, :], f[:, :, 1, :], ALU.add).then_inc(s["final_added"], 1)
                if 0 < step <= G:
                    g = step - 1
                    dve.wait_ge(s["final_added"], g + 1)
                    for q in range(GS):
                        n = min(2, c1 - 2 * q)
                        f = fin[g][:, 2 * q:2 * q + n, 0, :]
                        last = V.tensor_tensor(f, f, bc(gb_all[:, g * GS + q:g * GS + q + 1, :], [P, n, P]), ALU.mult)
                    last.then_inc(s["final_gated"], 1)
                if step > 1:
                    g = step - 2
                    dve.wait_ge(s["final_gated"], g + 1)
                    xg = X[:, g * GC:g * GC + c1, :]
                    last = V.tensor_tensor(xg, xg, fin[g][:, 0:c1, 0, :], ALU.add)
                    if g % 2:
                        last.then_inc(s["final_ready_dve"], 1)


def kernel(L0_attn_x, L0_attn_W_in, L0_attn_conv_w, L0_attn_conv_b, L0_attn_W_x, L0_attn_A_log, L0_attn_D,
           L0_attn_W_out, L0_ffn_gate_weight, L0_ffn_shared_gate_up, L0_ffn_shared_down,
           L0_ffn_experts_gate_up, L0_ffn_experts_down, L0_c, L0_wmod):
    import concourse.bacc as bacc
    from concourse.bass_utils import run_bass_kernel_spmd

    n = np.asarray
    big, small, token = constants()
    arrays = {
        "x": n(L0_attn_x).reshape(TOKENS, P),
        "L0_attn_W_in": n(L0_attn_W_in),
        "L0_attn_W_out": n(L0_attn_W_out),
        "L0_attn_W_x": n(L0_attn_W_x),
        "a_log": n(L0_attn_A_log).reshape(1, NS),
        "cols": np.concatenate([n(L0_attn_conv_w).reshape(DI, TAPS), n(L0_attn_conv_b)[:, None],
                                n(L0_attn_D)[:, None]], 1),
        "gate_t": n(L0_ffn_gate_weight).T,
        "c_t": n(L0_c).T,
        "L0_wmod": n(L0_wmod),
        "w_gu": np.concatenate([n(L0_ffn_shared_gate_up)[None], n(L0_ffn_experts_gate_up)], 0).transpose(0, 2, 1),
        "w_dn": np.concatenate([n(L0_ffn_shared_down)[None], n(L0_ffn_experts_down)], 0).transpose(0, 2, 1),
        "big": big, "small": small, "token": token,
    }
    arrays = {k: np.ascontiguousarray(v) for k, v in arrays.items()}
    nc = bacc.Bacc("TRN2", target_bir_lowering=False, num_devices=1)
    aps = {k: nc.dram_tensor("in_" + k, v.shape, mybir.dt.from_np(v.dtype), kind="ExternalInput").ap()
           for k, v in arrays.items()}
    aps["out"] = nc.dram_tensor("out", (TOKENS, P), F32, kind="ExternalOutput").ap()
    adaln_block(nc, aps)
    r = run_bass_kernel_spmd(nc, [{"in_" + k: v for k, v in arrays.items()}], core_ids=[0])
    return r.results[0]["out"].reshape(SEQS, SEQ, P)
```
